# Optimizing a Trainium2 kernel written in Bass

```python
import numpy as np
import jax
import jax.numpy as jnp

def _softmax(x, axis=-1):
    return jax.nn.softmax(x, axis=axis)

def _gelu(x):
    return jax.nn.gelu(x, approximate=True)

def _silu(x):
    return jax.nn.silu(x)

def _sigmoid(x):
    return jax.nn.sigmoid(x)

def _layernorm(x, axis=-1, eps=1e-05):
    m = jnp.mean(x, axis=axis, keepdims=True)
    v = jnp.var(x, axis=axis, keepdims=True)
    return (x - m) / jnp.sqrt(v + eps)

def _scatter_add(tgt, idx, src, axis=0):
    return tgt.at[idx].add(src)

def _segment_sum(src, seg, n):
    return jax.ops.segment_sum(src, seg, n)
kernel_name = 'mk_decoder_preln_d1_seqx_r4_e43b97'

def setup_inputs(seed: int=0):
    np.random.seed(seed)
    _w = jnp.asarray

    def _rec_inputs():
        import jax
        import jax.numpy as jnp
        _rk = jax.random.key(seed)
        x = -0.0003929 + 0.9999 * jax.random.normal(jax.random.fold_in(_rk, 1), (16, 112, 512), jnp.float32)
        _lenS = 112 - jax.random.randint(jax.random.fold_in(_rk, 7), (16,), 0, max(1, 112 // 4) + 1, jnp.int32)
        _lenS2 = 375 - jax.random.randint(jax.random.fold_in(_rk, 8), (16,), 0, max(1, 375 // 4) + 1, jnp.int32)
        _ctx_2048P = jax.random.normal(jax.random.fold_in(_rk, 11), (16, 16, 512), jnp.float32)
        _ctx_2048c = jax.random.dirichlet(jax.random.fold_in(_rk, 511), 0.3 * jnp.ones((16,), jnp.float32), (16, 375))
        _ctx_2048t = jnp.einsum('bsk,bkd->bsd', _ctx_2048c, _ctx_2048P)
        _ctx_2048t = _ctx_2048t * jax.lax.rsqrt(jnp.mean(jnp.square(_ctx_2048t)) + 1e-12) * 0.953939
        ctx_2048 = -0.000514642 + 1.00011 * (_ctx_2048t + 0.3 * jax.random.normal(jax.random.fold_in(_rk, 611), (16, 375, 512), jnp.float32))
        _validS = jnp.arange(112)[None, :] < _lenS[:, None]
        _validS2 = jnp.arange(375)[None, :] < _lenS2[:, None]
        _causal = jnp.tril(jnp.ones((112, 112), dtype=bool))
        mask_BxS2_ik0 = jnp.where(jnp.broadcast_to(_validS2[:, :], (16, 375)), 0, 1).astype(jnp.int32)
        return (x, ctx_2048, mask_BxS2_ik0)
    x, ctx_2048, mask_BxS2_ik0 = _rec_inputs()

    def _L0_attn_setup():
        import jax, jax.numpy as jnp
        import numpy as np
        D_MODEL = 512
        N_HEADS = 16
        D_HEAD = D_MODEL // N_HEADS
        RANK = 32

        def _orthogonal(key, rows, cols, dtype=jnp.float32):
            a = jax.random.normal(key, (max(rows, cols), min(rows, cols)), dtype=jnp.float32)
            q, r = jnp.linalg.qr(a)
            q = q * jnp.sign(jnp.diagonal(r))
            if rows < cols:
                q = q.T
            return q.astype(dtype)
        key = jax.random.key(seed)
        ks = jax.random.split(key, 8)
        B, T = (2, 512)
        x = jax.random.normal(ks[0], (B, T, D_MODEL), dtype=jnp.float32)
        s = 1.0 / np.sqrt(D_MODEL)
        Wq = jax.random.uniform(ks[1], (D_MODEL, D_MODEL), minval=-s, maxval=s, dtype=jnp.float32)
        Wk = jax.random.uniform(ks[2], (D_MODEL, D_MODEL), minval=-s, maxval=s, dtype=jnp.float32)
        Wv = jax.random.uniform(ks[3], (D_MODEL, D_MODEL), minval=-s, maxval=s, dtype=jnp.float32)
        Wo = jax.random.uniform(ks[4], (D_MODEL, D_MODEL), minval=-s, maxval=s, dtype=jnp.float32)
        Wdown = _orthogonal(ks[5], D_HEAD, RANK)
        Wup = _orthogonal(ks[6], RANK, D_HEAD)
        return {'x': x, 'Wq': Wq, 'Wk': Wk, 'Wv': Wv, 'Wo': Wo, 'Wdown': Wdown, 'Wup': Wup}
    _L0_attn_all = _L0_attn_setup()
    _L0_attn_in = {k: v for k, v in _L0_attn_all.items() if k in ('Wq', 'Wk', 'Wv', 'Wo', 'Wdown', 'Wup')}
    del _L0_attn_all

    def _L0_xattn_setup():
        import jax, jax.numpy as jnp
        import numpy as np
        import math
        H = 512
        NH = 16
        HD = H // NH
        EPS_LN = 1e-05
        RES_SCALE_MAX = 0.3

        def _nan_clean(x, lim=10000.0):
            return jnp.nan_to_num(x, nan=0.0, posinf=lim, neginf=-lim)
        key = jax.random.key(seed)
        ks = jax.random.split(key, 12)
        B, S, T = (4, 512, 64)
        std = 1.0 / math.sqrt(H)
        return {'hidden_states': jax.random.normal(ks[0], (B, S, H), jnp.float32), 'audio_tokens': jax.random.normal(ks[1], (B, T, H), jnp.float32), 'attention_mask': jax.random.randint(ks[2], (B, T), 0, 2, jnp.int32), 'Wq': jax.random.normal(ks[3], (H, H), jnp.float32) * std, 'bq': jnp.zeros((H,), jnp.float32), 'Wk': jax.random.normal(ks[4], (H, H), jnp.float32) * std, 'bk': jnp.zeros((H,), jnp.float32), 'Wv': jax.random.normal(ks[5], (H, H), jnp.float32) * std, 'bv': jnp.zeros((H,), jnp.float32), 'Wo': jax.random.normal(ks[6], (H, H), jnp.float32) * std, 'bo': jnp.zeros((H,), jnp.float32), 'ln_gamma': jnp.ones((H,), jnp.float32), 'ln_beta': jnp.zeros((H,), jnp.float32), 'residual_scale': jnp.float32(0.05)}
    _L0_xattn_all = _L0_xattn_setup()
    _L0_xattn_in = {k: v for k, v in _L0_xattn_all.items() if k in ('Wq', 'bq', 'Wk', 'bk', 'Wv', 'bv', 'Wo', 'bo', 'ln_gamma', 'ln_beta', 'residual_scale')}
    del _L0_xattn_all

    def _L0_ffn_setup():
        import jax, jax.numpy as jnp
        import numpy as np
        B, S, D, H = (4, 512, 512, 2048)

        def fwht(x):
            orig_shape = x.shape
            n = orig_shape[-1]
            x = x.reshape(-1, n)
            h = 1
            while h < n:
                xb = x.reshape(-1, n // (2 * h), 2, h)
                a = xb[:, :, 0, :]
                b = xb[:, :, 1, :]
                x = jnp.stack([a + b, a - b], axis=2).reshape(-1, n)
                h *= 2
            scale = jnp.asarray(1.0 / np.sqrt(n), dtype=x.dtype)
            return (x * scale).reshape(orig_shape)
        key = jax.random.key(seed)
        kx, k1, k2, k3 = jax.random.split(key, 4)
        x = jax.random.normal(kx, (B, S, D), dtype=jnp.float32)
        W1 = jax.random.normal(k1, (H, D), dtype=jnp.float32) * (1.0 / np.sqrt(D))
        W2 = jax.random.normal(k2, (D, H), dtype=jnp.float32) * (1.0 / np.sqrt(H))
        W3 = jax.random.normal(k3, (H, D), dtype=jnp.float32) * (1.0 / np.sqrt(D))
        return {'x': x, 'W1': W1, 'W2': W2, 'W3': W3}
    _L0_ffn_all = _L0_ffn_setup()
    _L0_ffn_in = {k: v for k, v in _L0_ffn_all.items() if k in ('W1', 'W2', 'W3')}
    del _L0_ffn_all
    return {'x': x, 'ctx_2048': ctx_2048, 'mask_BxS2_ik0': mask_BxS2_ik0, 'L0_attn_Wq': _L0_attn_in['Wq'], 'L0_attn_Wk': _L0_attn_in['Wk'], 'L0_attn_Wv': _L0_attn_in['Wv'], 'L0_attn_Wo': _L0_attn_in['Wo'], 'L0_attn_Wdown': _L0_attn_in['Wdown'], 'L0_attn_Wup': _L0_attn_in['Wup'], 'L0_xattn_Wq': _L0_xattn_in['Wq'], 'L0_xattn_bq': _L0_xattn_in['bq'], 'L0_xattn_Wk': _L0_xattn_in['Wk'], 'L0_xattn_bk': _L0_xattn_in['bk'], 'L0_xattn_Wv': _L0_xattn_in['Wv'], 'L0_xattn_bv': _L0_xattn_in['bv'], 'L0_xattn_Wo': _L0_xattn_in['Wo'], 'L0_xattn_bo': _L0_xattn_in['bo'], 'L0_xattn_ln_gamma': _L0_xattn_in['ln_gamma'], 'L0_xattn_ln_beta': _L0_xattn_in['ln_beta'], 'L0_xattn_residual_scale': _L0_xattn_in['residual_scale'], 'L0_ffn_W1': _L0_ffn_in['W1'], 'L0_ffn_W2': _L0_ffn_in['W2'], 'L0_ffn_W3': _L0_ffn_in['W3']}

def reference(x, ctx_2048, mask_BxS2_ik0, L0_attn_Wq, L0_attn_Wk, L0_attn_Wv, L0_attn_Wo, L0_attn_Wdown, L0_attn_Wup, L0_xattn_Wq, L0_xattn_bq, L0_xattn_Wk, L0_xattn_bk, L0_xattn_Wv, L0_xattn_bv, L0_xattn_Wo, L0_xattn_bo, L0_xattn_ln_gamma, L0_xattn_ln_beta, L0_xattn_residual_scale, L0_ffn_W1, L0_ffn_W2, L0_ffn_W3):
    import jax
    import jax.numpy as jnp

    def _L0_attn_ref(x, Wq, Wk, Wv, Wo, Wdown, Wup):
        import jax, jax.numpy as jnp
        import numpy as np
        D_MODEL = 512
        N_HEADS = 16
        D_HEAD = D_MODEL // N_HEADS
        RANK = 32

        def _orthogonal(key, rows, cols, dtype=jnp.float32):
            a = jax.random.normal(key, (max(rows, cols), min(rows, cols)), dtype=jnp.float32)
            q, r = jnp.linalg.qr(a)
            q = q * jnp.sign(jnp.diagonal(r))
            if rows < cols:
                q = q.T
            return q.astype(dtype)
        B, T, D = x.shape
        H, dh, r = (N_HEADS, D_HEAD, RANK)
        scale = 1.0 / np.sqrt(r)

        def heads(y):
            return y.reshape(B, T, H, dh).transpose(0, 2, 1, 3)
        q = heads(x @ Wq.T)
        k = heads(x @ Wk.T)
        v = heads(x @ Wv.T)
        q_r = jnp.einsum('bhtd,dr->bhtr', q, Wdown)
        k_r = jnp.einsum('bhtd,dr->bhtr', k, Wdown)
        v_r = jnp.einsum('bhtd,dr->bhtr', v, Wdown)
        scores = jnp.einsum('bhqr,bhkr->bhqk', q_r, k_r) * scale
        attn = jax.nn.softmax(scores, axis=-1)
        y_r = jnp.einsum('bhqk,bhkr->bhqr', attn, v_r)
        y = jnp.einsum('bhtr,rd->bhtd', y_r, Wup)
        y = y.transpose(0, 2, 1, 3).reshape(B, T, D)
        out = y @ Wo.T
        return out

    def _L0_xattn_ref(hidden_states, audio_tokens, attention_mask, Wq, bq, Wk, bk, Wv, bv, Wo, bo, ln_gamma, ln_beta, residual_scale):
        import jax, jax.numpy as jnp
        import numpy as np
        import math
        H = 512
        NH = 16
        HD = H // NH
        EPS_LN = 1e-05
        RES_SCALE_MAX = 0.3

        def _nan_clean(x, lim=10000.0):
            return jnp.nan_to_num(x, nan=0.0, posinf=lim, neginf=-lim)
        B, S, _ = hidden_states.shape
        T = audio_tokens.shape[1]
        hs = _nan_clean(hidden_states).astype(jnp.float32)
        at = _nan_clean(audio_tokens).astype(jnp.float32)

        def proj(x, W, b, L):
            y = x @ W.T + b
            return y.reshape(B, L, NH, HD).transpose(0, 2, 1, 3)
        q = _nan_clean(proj(hs, Wq, bq, S))
        k = _nan_clean(proj(at, Wk, bk, T))
        v = _nan_clean(proj(at, Wv, bv, T))
        scale = max(math.sqrt(HD), 1e-08)
        scores = jnp.einsum('bhsd,bhtd->bhst', q, k) / scale
        scores = jnp.clip(scores, -50.0, 50.0)
        scores = jnp.nan_to_num(scores, nan=0.0, posinf=50.0, neginf=-50.0)
        attend = (attention_mask.astype(jnp.float32) > 0.5)[:, None, None, :]
        scores = jnp.where(attend, scores, -10000.0)
        scores = jnp.clip(scores, -50.0, 50.0)
        probs = jax.nn.softmax(scores, axis=-1)
        probs = jnp.nan_to_num(probs, nan=0.0, posinf=1.0, neginf=0.0)
        probs = probs / (probs.sum(axis=-1, keepdims=True) + 1e-08)
        ctx = jnp.einsum('bhst,bhtd->bhsd', probs, v)
        ctx = ctx.transpose(0, 2, 1, 3).reshape(B, S, H)
        delta = _nan_clean(ctx @ Wo.T + bo)
        rs = jnp.clip(residual_scale, 0.0, RES_SCALE_MAX)
        delta = rs * delta
        mu = delta.mean(axis=-1, keepdims=True)
        var = jnp.mean((delta - mu) ** 2, axis=-1, keepdims=True)
        delta = (delta - mu) / jnp.sqrt(var + EPS_LN) * ln_gamma + ln_beta
        return delta

    def _L0_ffn_ref(x, W1, W2, W3):
        import jax, jax.numpy as jnp
        import numpy as np
        B, S, D, H = (4, 512, 512, 2048)

        def fwht(x):
            orig_shape = x.shape
            n = orig_shape[-1]
            x = x.reshape(-1, n)
            h = 1
            while h < n:
                xb = x.reshape(-1, n // (2 * h), 2, h)
                a = xb[:, :, 0, :]
                b = xb[:, :, 1, :]
                x = jnp.stack([a + b, a - b], axis=2).reshape(-1, n)
                h *= 2
            scale = jnp.asarray(1.0 / np.sqrt(n), dtype=x.dtype)
            return (x * scale).reshape(orig_shape)
        up_gate = jnp.einsum('bsd,hd->bsh', x, W1)
        up_lin = jnp.einsum('bsd,hd->bsh', x, W3)
        hidden = jax.nn.silu(up_gate) * up_lin
        hidden = fwht(hidden)
        out = jnp.einsum('bsh,dh->bsd', hidden, W2)
        return out
    x = x + _L0_attn_ref(_layernorm(x, axis=-1), L0_attn_Wq, L0_attn_Wk, L0_attn_Wv, L0_attn_Wo, L0_attn_Wdown, L0_attn_Wup)
    x = x + _L0_xattn_ref(_layernorm(x, axis=-1), ctx_2048, mask_BxS2_ik0, L0_xattn_Wq, L0_xattn_bq, L0_xattn_Wk, L0_xattn_bk, L0_xattn_Wv, L0_xattn_bv, L0_xattn_Wo, L0_xattn_bo, L0_xattn_ln_gamma, L0_xattn_ln_beta, L0_xattn_residual_scale)
    x = x + _L0_ffn_ref(_layernorm(x, axis=-1), L0_ffn_W1, L0_ffn_W2, L0_ffn_W3)
    return x

_drawn_inputs = setup_inputs


def setup_inputs(seed=0):
    import zlib

    import numpy as np

    out = dict(_drawn_inputs(seed))
    spreads = {'L0_xattn_bq': (0.0, 0.1),
     'L0_xattn_bk': (0.0, 0.8),
     'L0_xattn_bv': (0.0, 0.1),
     'L0_xattn_bo': (0.0, 0.1),
     'L0_xattn_ln_gamma': (1.0, 0.2),
     'L0_xattn_ln_beta': (0.0, 0.1)}
    factors = {'L0_attn_Wq': 5.307, 'L0_attn_Wk': 4.884}
    for name, (base, spread) in spreads.items():
        noise = np.random.default_rng([zlib.crc32(name.encode()), seed]).standard_normal(out[name].shape)
        drawn = base * np.exp(spread * noise) if base else spread * noise
        out[name] = jnp.asarray(drawn.astype(out[name].dtype))
    for name, factor in factors.items():
        out[name] = (out[name] * factor).astype(out[name].dtype)
    return out
```

```python
from contextlib import ExitStack

import concourse.bass as bass
from concourse import mybir

F32 = mybir.dt.float32
F32R = mybir.dt.float32r
I32 = mybir.dt.int32
ALU = mybir.AluOpType
ACT = mybir.ActivationFunctionType
AX_X = mybir.AxisListType.X

B, T, D = 16, 112, 512
S = 375
H, DH = 16, 32
F = 2048
P = 128
KC = D // P
HQ = P // DH
PAIRS = B // 2
PT = 2 * T
QT = HQ * T
KT = 3
KP = S // KT
SE = S + 1
EPS = 1e-5
SCALE = float(DH) ** -0.5
CLIP = 50.0
MASKED = -10000.0
TOK = B * T
FT = TOK // P
HC = 256
CHUNKS = F // HC
HT = HC // P
BCOL = D // PAIRS
FGROUPS = [(0, 512), (512, 512), (1024, 512), (1536, 256)]


def three_pass(eng, out, w_hi, w_lo, m_hi, m_lo, start, stop):
    eng.matmul(out, w_hi, m_hi, start=start, stop=False)
    eng.matmul(out, w_hi, m_lo, start=False, stop=False)
    return eng.matmul(out, w_lo, m_hi, start=False, stop=stop)


def held(eng, value):
    return value if isinstance(value, int) else eng.snap(value)


def carry_waits(eng, cell):
    eng.memset(cell, 0.0)


def f32(ap):
    return ap.bitcast(F32)


class Memory:

    def __init__(self, nc, scope):
        self.nc, self.scope = nc, scope

    def sb(self, name, shape, dt=F32):
        return self.scope.enter_context(self.nc.sbuf_tensor(name, shape, dt))

    def ps(self, name, shape, dt=F32):
        return self.scope.enter_context(self.nc.psum_tensor(name, shape, dt))

    def sem(self, name):
        return self.scope.enter_context(self.nc.semaphore(name))


def build_prep(nc, dram, w, consts, sems):
    with ExitStack() as scope:
        m = Memory(nc, scope)
        wq_nat = m.sb("wq_nat", [P, KC, D])
        wv_nat = m.sb("wv_nat", [P, KC, D])
        wk_raw = m.sb("wk_raw", [P, KC * D])
        wo_raw = m.sb("wo_raw", [P, KC * D])
        down_bd = m.sb("down_bd", [P, P])
        up_bd = m.sb("up_bd", [P, P])
        fold_q = m.sb("fold_q", [P, P])
        fold_v = m.sb("fold_v", [P, P])
        ps = m.ps("ps_prep", [P, 8, 512])
        zeroed, diag_in, wq_in, wv_in, wk_in, wo_in, const_in = (
            sems.sem(n) for n in ("zeroed", "diag_in", "wq_in", "wv_in", "wk_in", "wo_in", "const_in"))
        folds_done, folds_copied, q_folded, v_folded, hi_done, prep_done = (
            sems.sem(n) for n in ("folds_done", "folds_copied", "q_folded", "v_folded", "prep_hi_done", "prep_done"))

        block = scope.enter_context(nc.Block())

        @block.sync
        def _(sp):
            sp.dma_start(wk_raw[:], dram["wk"].rearrange("p c n -> p (c n)")).then_inc(wk_in, 16)
            sp.dma_start(wq_nat[:], dram["wq"]).then_inc(wq_in, 16)
            sp.wait_ge(zeroed, 2)
            for g in range(HQ):
                r = slice(DH * g, DH * g + DH)
                sp.dma_start(down_bd[r, r], dram["wdown_t"]).then_inc(diag_in, 16)
                sp.dma_start(up_bd[r, r], dram["wup"]).then_inc(diag_in, 16)
            sp.dma_start(wv_nat[:], dram["wv"]).then_inc(wv_in, 16)
            sp.dma_start(wo_raw[:], dram["wo"].rearrange("p c n -> p (c n)")).then_inc(wo_in, 16)
            sp.dma_start(consts["ident"][:], dram["ident"]).then_inc(const_in, 16)
            sp.wait_ge(const_in, 16)

        @block.gpsimd
        def _(pool):
            pool.memset(down_bd[:], 0.0).then_inc(zeroed, 1)
            pool.memset(up_bd[:], 0.0).then_inc(zeroed, 1)
            pool.memset(consts["eps"][:], EPS).then_inc(zeroed, 1)
            pool.memset(consts["minus_half"][:], -0.5).then_inc(zeroed, 1)

        @block.tensor
        def _(pe):
            pe.wait_ge(diag_in, 16 * 2 * HQ)
            pe.matmul(ps[:, 0, 0:P], down_bd[:], down_bd[:], start=True, stop=True)
            pe.matmul(ps[:, 1, 0:P], down_bd[:], up_bd[:], start=True, stop=True).then_inc(folds_done, 1)
            pe.wait_ge(folds_copied, 2)
            for nat, fold, base, arrived, done in ((wq_nat, fold_q, 0, wq_in, q_folded),
                                                   (wv_nat, fold_v, 4, wv_in, v_folded)):
                pe.wait_ge(arrived, 16)
                for c in range(KC):
                    for o in range(KC):
                        last = pe.matmul(ps[:, base + c, o * P:(o + 1) * P], nat[:, o, c * P:(c + 1) * P],
                                         fold[:], start=True, stop=True)
                    last.then_inc(done, 1)

        @block.scalar
        def _(act):
            for n, (raw, arrived, dst) in enumerate(((wk_raw, wk_in, w["k"]), (wo_raw, wo_in, w["o"]))):
                act.wait_ge(arrived, 16)
                act.activation(dst[0][:].rearrange("p c n -> p (c n)"), raw[:], ACT.Copy).then_inc(hi_done, 1)
            for n, (base, done, dst) in enumerate(((0, q_folded, w["q"]), (4, v_folded, w["v"]))):
                for c in range(KC):
                    act.wait_ge(done, c + 1)
                    act.activation(dst[0][:, c, :], ps[:, base + c, :], ACT.Copy).then_inc(hi_done, 1)

        @block.vector
        def _(dve):
            dve.wait_ge(folds_done, 1)
            dve.tensor_copy(fold_q[:], ps[:, 0, 0:P]).then_inc(folds_copied, 1)
            dve.tensor_copy(fold_v[:], ps[:, 1, 0:P]).then_inc(folds_copied, 1)
            for n, (raw, dst) in enumerate(((wk_raw, w["k"]), (wo_raw, w["o"]))):
                dve.wait_ge(hi_done, n + 1)
                dve.tensor_tensor(dst[1][:].rearrange("p c n -> p (c n)"), raw[:],
                                  f32(dst[0][:].rearrange("p c n -> p (c n)")), ALU.subtract).then_inc(prep_done, 1)
            for n, (base, dst) in enumerate(((0, w["q"]), (4, w["v"]))):
                for c in range(KC):
                    dve.wait_ge(hi_done, 2 + n * KC + c + 1)
                    dve.tensor_tensor(dst[1][:, c, :], ps[:, base + c, :], f32(dst[0][:, c, :]),
                                      ALU.subtract).then_inc(prep_done, 1)


def build_self(nc, dram, w, consts, sems):
    UNITS = 4
    with ExitStack() as scope:
        m = Memory(nc, scope)
        x = m.sb("x", [T, B * D])
        fence = m.sb("fence_f1", [1, 1])
        st = m.sb("st", [T, 2, 6])
        mv = m.sb("mv", [T, 2, 2])
        veps = m.sb("veps", [T, 2, 1])
        rstd = m.sb("rstd", [T, 2, 1])
        xn = m.sb("xn", [T, 2, D])
        xt = [m.sb(f"xt_{n}", [P, KC, PT], F32R) for n in ("hi", "lo")]
        k = [m.sb(f"k_{n}", [P, KC, PT], F32R) for n in ("hi", "lo")]
        kbd = [m.sb(f"kbd_{n}", [P, KC, 2, HQ, T], F32R) for n in ("hi", "lo")]
        q = [m.sb(f"q_{n}", [P, KC, PT], F32R) for n in ("hi", "lo")]
        v = m.sb("v", [T, 2, D])
        mx = m.sb("mx", [T, 2, 8])
        e = m.sb("e", [T, 2, 8, T])
        total = m.sb("total", [T, 2, 8])
        rtotal = m.sb("rtotal", [T, 2, 8])
        pt = m.sb("pt", [T, 2, 8, T])
        ot = [m.sb(f"ot_{n}", [P, 2, KC, T], F32R) for n in ("hi", "lo")]
        fly = m.sb("fly", [P, 2, B, BCOL])
        gen = [m.ps(f"gen{n}", [P, 512]) for n in range(2)]
        sc = m.ps("sc", [P, 4, 512])
        av = m.ps("av", [P, 2, 512])

        names = ("x_in0 x_in1 stats_done aggr_done veps_done rstd_done xn_done xt_ready xt_hi_done xt_lo_done "
                 "k_ready k_hi_done k_lo_done kbd_hi_done kbd_lo_done q_ready q_hi_done q_lo_done v_ready v_done "
                 "sc_done mx_done sub_done exp_done total_done rtotal_done norm_done pt_ready pt_done av_done "
                 "ot_hi_done ot_lo_done y_ready x1_done x1_out0 x1_out1 fly_in fly_step fly_out kbd_zeroed").split()
        s = {n: sems.sem("s_" + n) for n in names}
        x_in, x1_out = (s["x_in0"], s["x_in1"]), (s["x1_out0"], s["x1_out1"])

        def xb(i, j):
            return x[:, bass.ds((2 * i + j) * D, D)]

        block = scope.enter_context(nc.Block())

        @block.sync
        def _(sp):
            def load(i, j):
                at = bass.ds(held(sp, (2 * i + j) * D), D)
                if not isinstance(i, int):
                    sp.wait_ge(x_in[j], 16 * i)
                sp.dma_start(x[:, at], dram["x"][:, at]).then_inc(x_in[j], 16)

            def fly_load(i):
                at = bass.ds(held(sp, i * B), B)
                if not isinstance(i, int):
                    sp.wait_ge(s["fly_out"], 16 * i)
                sp.dma_start(fly[:, 0], dram["w2"][:, at, :]).then_inc(s["fly_in"], 16)

            def fly_store(i):
                at = bass.ds(held(sp, i * B), B)
                sp.wait_ge(s["fly_step"], 8 * i + 8)
                sp.dma_start(dram["w2_fly"][:, at, :], fly[:, 0]).then_inc(s["fly_out"], 16)

            def store(i, j):
                at, done = bass.ds(held(sp, (2 * i + j) * D), D), held(sp, 2 * i + j + 1)
                sp.wait_ge(s["x1_done"], done)
                if not isinstance(i, int):
                    sp.wait_ge(x1_out[j], 16 * i)
                sp.dma_start(dram["x1"][:, at], x[:, at]).then_inc(x1_out[j], 16)

            load(0, 0)
            load(0, 1)
            fly_load(0)
            with sp.Fori(1, PAIRS) as i:
                for j in range(2):
                    load(i, j)
            store(0, 0)
            store(0, 1)
            with sp.Fori(1, PAIRS) as i:
                fly_store(i - 1)
                fly_load(i)
                for j in range(2):
                    store(i, j)
            fly_store(PAIRS - 1)
            sp.wait_ge(s["fly_out"], 16 * PAIRS)
            for j in range(2):
                sp.wait_ge(x1_out[j], 16 * PAIRS)

        @block.gpsimd
        def _(pool):
            def layernorm(i):
                for j in range(2):
                    pool.wait_ge(s["aggr_done"], 2 * i + j + 1)
                    pool.tensor_tensor(veps[:, j], mv[:, j, 1:2], consts["eps"][0:T], ALU.add).then_inc(s["veps_done"], 1)
                    pool.wait_ge(s["veps_done"], 2 * i + j + 1)
                    pool.tensor_tensor(rstd[:, j], veps[:, j], consts["minus_half"][0:T], ALU.pow).then_inc(s["rstd_done"], 1)

            def normalise(i, u):
                pool.wait_ge(s["rtotal_done"], 4 * i + u + 1)
                pool.tensor_tensor(e[:, u % 2], e[:, u % 2],
                                   rtotal[:, u % 2].unsqueeze(2).to_broadcast([T, 8, T]), ALU.mult).then_inc(s["norm_done"], 1)

            def fly_stage(i, n):
                a, b = n % 2, (n + 1) % 2
                st = 1 << n
                src = fly[:, a].rearrange("p (g two s) c -> p two g s c", two=2, s=st)
                dst = fly[:, b].rearrange("p (g two s) c -> p two g s c", two=2, s=st)
                if n == 0:
                    pool.wait_ge(s["fly_in"], 16 * i + 16)
                else:
                    pool.wait_ge(s["fly_step"], 8 * i + 2 * n)
                pool.tensor_tensor(dst[:, 0], src[:, 0], src[:, 1], ALU.add).then_inc(s["fly_step"], 1)
                pool.tensor_tensor(dst[:, 1], src[:, 0], src[:, 1], ALU.subtract).then_inc(s["fly_step"], 1)

            def step(i, last):
                for u in range(UNITS):
                    normalise(i, u)
                    if u == 0 and not last:
                        layernorm(i + 1)
                    fly_stage(i, u)

            layernorm(0)
            with pool.Fori(0, PAIRS - 1) as i:
                step(i, False)
            step(PAIRS - 1, True)

        @block.tensor
        def _(pe):
            def transpose_x(i):
                for j in range(2):
                    pe.wait_ge(s["xn_done"], 2 * i + j + 1)
                    if not (isinstance(i, int) and i == 0):
                        if j == 0:
                            pe.wait_ge(s["v_done"], 2 * i)
                        else:
                            pe.wait_ge(s["x1_done"], 2 * i - 1)
                    for c in range(KC):
                        last = pe.transpose(gen[j][:, c * T:(c + 1) * T], xn[:, j, c * P:(c + 1) * P],
                                            consts["ident"][0:T, 0:T])
                    last.then_inc(s["xt_ready"], 1)

            def project(i, name, weights):
                for half in range(2):
                    g = gen[1 - half]
                    if name == "k":
                        if half == 0:
                            pe.wait_ge(s["xt_lo_done"], 2 * i + 2)
                        elif not (isinstance(i, int) and i == 0):
                            pe.wait_ge(s["x1_done"], 2 * i)
                    else:
                        pe.wait_ge(s["k_lo_done"], 2 * i + half + 1)
                    for o in range(2):
                        mt = 2 * half + o
                        for c in range(KC):
                            last = three_pass(pe, g[:, o * PT:(o + 1) * PT],
                                              weights[0][:, c, mt * P:(mt + 1) * P], weights[1][:, c, mt * P:(mt + 1) * P],
                                              xt[0][:, c], xt[1][:, c], c == 0, c == KC - 1)
                    last.then_inc(s[name + "_ready"], 1)

            def project_v(i, j):
                pe.wait_ge(s["q_lo_done"], 2 * i + j + 1)
                for c in range(KC):
                    last = three_pass(pe, gen[1 - j][0:T, :], xt[0][:, c, j * T:(j + 1) * T], xt[1][:, c, j * T:(j + 1) * T],
                                      w["v"][0][:, c], w["v"][1][:, c], c == 0, c == KC - 1)
                last.then_inc(s["v_ready"], 1)

            def scores(i, u):
                j, b = u // 2, u % 2
                if u == 0:
                    pe.wait_ge(s["kbd_hi_done"], i + 1)
                    pe.wait_ge(s["kbd_lo_done"], i + 1)
                    pe.wait_ge(s["q_lo_done"], 2 * i + 2)
                if not (isinstance(i, int) and i == 0 and u < 2):
                    pe.wait_ge(s["pt_done"], 4 * i + u - 1)
                for n in range(2):
                    mt = 2 * b + n
                    last = three_pass(pe, sc[0:T, 2 * b + n, 0:QT],
                                      q[0][:, mt, j * T:(j + 1) * T], q[1][:, mt, j * T:(j + 1) * T],
                                      kbd[0][:, mt, j].rearrange("p h t -> p (h t)"),
                                      kbd[1][:, mt, j].rearrange("p h t -> p (h t)"), True, True)
                last.then_inc(s["sc_done"], 1)

            def transpose_p(i, u):
                b = u % 2
                pe.wait_ge(s["norm_done"], 4 * i + u + 1)
                for h in range(8):
                    last = pe.transpose(sc[0:T, 2 * b + h // 4, (h % 4) * T:(h % 4 + 1) * T], e[:, b, h],
                                        consts["ident"][0:T, 0:T])
                last.then_inc(s["pt_ready"], 1)

            def attend(i, u):
                j, b = u // 2, u % 2
                pe.wait_ge(s["pt_done"], 4 * i + u + 1)
                pe.wait_ge(s["v_done"], 2 * i + j + 1)
                if not (isinstance(i, int) and i == 0 and u < 2):
                    pe.wait_ge(s["ot_lo_done"], 4 * i + u - 1)
                for n in range(2):
                    for h in range(HQ):
                        head = (2 * b + n) * HQ + h
                        last = pe.matmul(av[DH * h:DH * (h + 1), b, n * T:(n + 1) * T],
                                         v[:, j, head * DH:(head + 1) * DH], pt[:, b, n * HQ + h],
                                         start=True, stop=True)
                last.then_inc(s["av_done"], 1)

            def output(i, j):
                pe.wait_ge(s["ot_lo_done"], 4 * i + 2 * j + 2)
                if j == 0:
                    pe.wait_ge(s["v_done"], 2 * i + 1)
                else:
                    pe.wait_ge(s["xt_lo_done"], 2 * i + 3) if not_last(i) else pe.wait_ge(s["v_done"], 2 * i + 2)
                g = gen[1 - j]
                for c in range(KC):
                    last = three_pass(pe, g[0:T, :], ot[0][:, j, c], ot[1][:, j, c], w["o"][0][:, c], w["o"][1][:, c],
                                      c == 0, c == KC - 1)
                last.then_inc(s["y_ready"], 1)

            def not_last(i):
                return not (isinstance(i, int) and i == PAIRS - 1)

            def step(i):
                project(i, "k", w["k"])
                project(i, "q", w["q"])
                scores(i, 0)
                project_v(i, 0)
                scores(i, 1)
                transpose_p(i, 0)
                project_v(i, 1)
                scores(i, 2)
                transpose_p(i, 1)
                attend(i, 0)
                scores(i, 3)
                attend(i, 1)
                transpose_p(i, 2)
                output(i, 0)
                attend(i, 2)
                transpose_p(i, 3)

            transpose_x(0)
            step(0)
            with pe.Fori(1, PAIRS) as i:
                transpose_x(i)
                attend(i - 1, 3)
                output(i - 1, 1)
                step(i)
            attend(PAIRS - 1, 3)
            output(PAIRS - 1, 1)

        @block.scalar
        def _(act):
            def pt_copy(i, u):
                b = u % 2
                act.wait_ge(s["pt_ready"], 4 * i + u + 1)
                if not (isinstance(i, int) and i == 0 and u < 2):
                    act.wait_ge(s["av_done"], 4 * i + u - 1)
                act.activation(pt[:, b].rearrange("t (n h) q -> t n (h q)", n=2), sc[0:T, 2 * b:2 * b + 2, 0:QT],
                               ACT.Copy).then_inc(s["pt_done"], 1)

            def ot_hi(i, u):
                j, b = u // 2, u % 2
                act.wait_ge(s["av_done"], 4 * i + u + 1)
                if not (isinstance(i, int) and i == 0):
                    act.wait_ge(s["y_ready"], 2 * i + j - 1)
                act.activation(ot[0][:, j, 2 * b:2 * b + 2], av[:, b, 0:2 * T].rearrange("p (n t) -> p n t", n=2),
                               ACT.Copy).then_inc(s["ot_hi_done"], 1)

            def exp(i, u):
                b = u % 2
                act.wait_ge(s["sub_done"], 4 * i + u + 1)
                act.activation(e[:, b], e[:, b], ACT.Exp, scale=SCALE).then_inc(s["exp_done"], 1)

            def v_copy(i, j):
                act.wait_ge(s["v_ready"], 2 * i + j + 1)
                if not (isinstance(i, int) and i == 0):
                    act.wait_ge(s["av_done"], 4 * i - 2 + 2 * j)
                act.activation(v[:, j], gen[1 - j][0:T, :], ACT.Copy).then_inc(s["v_done"], 1)

            def x_hi(i):
                for j in range(2):
                    act.wait_ge(s["xt_ready"], 2 * i + j + 1)
                    act.activation(xt[0][:, :, j * T:(j + 1) * T], gen[j][:, 0:QT].rearrange("p (c t) -> p c t", c=KC),
                                   ACT.Copy).then_inc(s["xt_hi_done"], 1)

            def step(i):
                for half in range(2):
                    act.wait_ge(s["k_ready"], 2 * i + half + 1)
                    act.activation(k[0][:, 2 * half:2 * half + 2], gen[1 - half][:, 0:2 * PT].rearrange("p (o t) -> p o t", o=2),
                                   ACT.Copy).then_inc(s["k_hi_done"], 1)
                act.wait_ge(s["kbd_zeroed"], 2)
                act.wait_ge(s["k_hi_done"], 2 * i + 2)
                for h in range(HQ):
                    r = slice(DH * h, DH * (h + 1))
                    last = act.activation(kbd[0][r, :, :, h], k[0][r].bitcast(F32).rearrange("p c (j t) -> p c j t", j=2), ACT.Copy)
                last.then_inc(s["kbd_hi_done"], 1)
                for half in range(2):
                    act.wait_ge(s["q_ready"], 2 * i + half + 1)
                    act.activation(q[0][:, 2 * half:2 * half + 2], gen[1 - half][:, 0:2 * PT].rearrange("p (o t) -> p o t", o=2),
                                   ACT.Copy).then_inc(s["q_hi_done"], 1)
                exp(i, 0)
                v_copy(i, 0)
                exp(i, 1)
                pt_copy(i, 0)
                v_copy(i, 1)
                exp(i, 2)
                pt_copy(i, 1)
                ot_hi(i, 0)
                exp(i, 3)
                ot_hi(i, 1)
                pt_copy(i, 2)
                ot_hi(i, 2)

            x_hi(0)
            step(0)
            with act.Fori(1, PAIRS) as i:
                pt_copy(i - 1, 3)
                x_hi(i)
                ot_hi(i - 1, 3)
                step(i)
            pt_copy(PAIRS - 1, 3)
            ot_hi(PAIRS - 1, 3)

        @block.vector
        def _(dve):
            def layernorm_stats(i):
                for j in range(2):
                    dve.wait_ge(x_in[j], 16 * i + 16)
                    dve.bn_stats(st[:, j], xb(i, j)).then_inc(s["stats_done"], 1)
                dve.wait_ge(s["stats_done"], 2 * i + 2)
                if not (isinstance(i, int) and i == 0):
                    dve.wait_ge(s["xn_done"], 2 * i)
                carry_waits(dve, fence[:])
                for j in range(2):
                    dve.bn_aggr(mv[:, j], st[:, j]).then_inc(s["aggr_done"], 1)

            def layernorm_apply(i, j):
                dve.wait_ge(s["rstd_done"], 2 * i + j + 1)
                if not (isinstance(i, int) and i == 0):
                    dve.wait_ge(s["xt_ready"], 2 * i + j - 1)
                dve.tensor_scalar(xn[:, j], xb(i, j), mv[:, j, 0:1], rstd[:, j], ALU.subtract, ALU.mult)\
                   .then_inc(s["xn_done"], 1)

            def x_lo(i):
                for j in range(2):
                    dve.wait_ge(s["xt_hi_done"], 2 * i + j + 1)
                    dve.tensor_tensor(xt[1][:, :, j * T:(j + 1) * T], gen[j][:, 0:QT].rearrange("p (c t) -> p c t", c=KC),
                                      f32(xt[0][:, :, j * T:(j + 1) * T]), ALU.subtract).then_inc(s["xt_lo_done"], 1)

            def lo(i, name, dst):
                for half in range(2):
                    dve.wait_ge(s[name + "_hi_done"], 2 * i + half + 1)
                    dve.tensor_tensor(dst[1][:, 2 * half:2 * half + 2], gen[1 - half][:, 0:2 * PT].rearrange("p (o t) -> p o t", o=2),
                                      f32(dst[0][:, 2 * half:2 * half + 2]), ALU.subtract).then_inc(s[name + "_lo_done"], 1)

            def softmax(i, u):
                b = u % 2
                src = sc[0:T, 2 * b:2 * b + 2, 0:QT].rearrange("t n (h k) -> t n h k", h=HQ)
                dve.wait_ge(s["sc_done"], 4 * i + u + 1)
                dve.reduce_max(mx[:, b].rearrange("t (n h) -> t n h", n=2), src, AX_X).then_inc(s["mx_done"], 1)
                dve.wait_ge(s["mx_done"], 4 * i + u + 1)
                if not (isinstance(i, int) and i == 0 and u < 2):
                    dve.wait_ge(s["pt_ready"], 4 * i + u - 1)
                dve.tensor_tensor(e[:, b].rearrange("t (n h) k -> t n h k", n=2), src,
                                  mx[:, b].rearrange("t (n h) -> t n h", n=2).unsqueeze(3).to_broadcast([T, 2, HQ, T]),
                                  ALU.subtract).then_inc(s["sub_done"], 1)

            def totals(i, u):
                b = u % 2
                dve.wait_ge(s["exp_done"], 4 * i + u + 1)
                dve.reduce_sum(total[:, b], e[:, b], AX_X).then_inc(s["total_done"], 1)
                dve.wait_ge(s["total_done"], 4 * i + u + 1)
                dve.reciprocal(rtotal[:, b], total[:, b]).then_inc(s["rtotal_done"], 1)

            def ot_lo(i, u):
                j, b = u // 2, u % 2
                dve.wait_ge(s["ot_hi_done"], 4 * i + u + 1)
                dve.tensor_tensor(ot[1][:, j, 2 * b:2 * b + 2], av[:, b, 0:2 * T].rearrange("p (n t) -> p n t", n=2),
                                  f32(ot[0][:, j, 2 * b:2 * b + 2]), ALU.subtract).then_inc(s["ot_lo_done"], 1)

            def add_x(i, j):
                dve.wait_ge(s["y_ready"], 2 * i + j + 1)
                dve.tensor_tensor(xb(i, j), gen[1 - j][0:T, :], xb(i, j), ALU.add).then_inc(s["x1_done"], 1)

            def step(i, last):
                lo(i, "k", k)
                dve.wait_ge(s["k_lo_done"], 2 * i + 2)
                for h in range(HQ):
                    r = slice(DH * h, DH * (h + 1))
                    end = dve.tensor_copy(kbd[1][r, :, :, h], k[1][r].rearrange("p c (j t) -> p c j t", j=2))
                end.then_inc(s["kbd_lo_done"], 1)
                lo(i, "q", q)
                softmax(i, 0)
                totals(i, 0)
                softmax(i, 1)
                totals(i, 1)
                if not last:
                    layernorm_stats(i + 1)
                softmax(i, 2)
                ot_lo(i, 0)
                totals(i, 2)
                if not last:
                    layernorm_apply(i + 1, 0)
                softmax(i, 3)
                ot_lo(i, 1)
                totals(i, 3)
                if not last:
                    layernorm_apply(i + 1, 1)
                add_x(i, 0)
                ot_lo(i, 2)

            for n in range(2):
                dve.memset(f32(kbd[n][:]), 0.0).then_inc(s["kbd_zeroed"], 1)
            layernorm_stats(0)
            for j in range(2):
                layernorm_apply(0, j)
            x_lo(0)
            dve.wait_ge(s["kbd_zeroed"], 2)
            step(0, False)
            with dve.Fori(1, PAIRS - 1) as i:
                x_lo(i)
                ot_lo(i - 1, 3)
                add_x(i - 1, 1)
                step(i, False)
            x_lo(PAIRS - 1)
            ot_lo(PAIRS - 2, 3)
            add_x(PAIRS - 2, 1)
            step(PAIRS - 1, True)
            ot_lo(PAIRS - 1, 3)
            add_x(PAIRS - 1, 1)


def build_prep_cross(nc, dram, w, c, sems):
    with ExitStack() as scope:
        m = Memory(nc, scope)
        raw = {n: m.sb(f"raw_{n}", [P, KC, D]) for n in "qkvo"}
        bv = m.sb("bv", [P, KC])
        bv_wide = m.sb("bv_wide", [P, KC, P])
        bo = m.sb("bo", [P, D])
        mask = m.sb("mask", [KP, B * KT], I32)
        maskf = m.sb("maskf", [KP, B * KT])
        ps = m.ps("ps_prep2", [P, 512])
        s = {n: sems.sem("pc_" + n) for n in
             "q_in k_in v_in o_in small_in hi_done lo_done wide_done bias_ready setup mask_step rs_step".split()}
        block = scope.enter_context(nc.Block())

        @block.sync
        def _(sp):
            for n in "kvqo":
                sp.dma_start(raw[n][:], dram["x" + n]).then_inc(s[n + "_in"], 16)
            for dst, src in ((bv[:], dram["bv"]), (c["bq"][:], dram["bq"]), (c["bk"][:], dram["bk"]),
                             (bo[:], dram["bo"].to_broadcast([P, D])), (c["gamma"][:], dram["gamma"].to_broadcast([P, D])),
                             (c["beta"][:], dram["beta"].to_broadcast([P, D])), (c["rs"][:], dram["rs"].to_broadcast([P, 1])),
                             (mask[:], dram["mask"]), (c["sel"][:], dram["sel"]), (c["spread"][:], dram["spread"])):
                sp.dma_start(dst, src).then_inc(s["small_in"], 16)

        @block.scalar
        def _(act):
            for n in "kvqo":
                act.wait_ge(s[n + "_in"], 16)
                act.activation(w[n][0][:], raw[n][:], ACT.Copy).then_inc(s["hi_done"], 1)

        @block.vector
        def _(dve):
            for i, n in enumerate("kvqo"):
                dve.wait_ge(s["hi_done"], i + 1)
                dve.tensor_tensor(w[n][1][:], raw[n][:], f32(w[n][0][:]), ALU.subtract).then_inc(s["lo_done"], 1)
            dve.wait_ge(s["bias_ready"], 1)
            dve.tensor_tensor(c["bo_full"][:], ps[:], bo[:], ALU.add).then_inc(s["setup"], 1)
            dve.tensor_copy(maskf[:], mask[:]).then_inc(s["mask_step"], 1)
            dve.wait_ge(s["mask_step"], 1)
            dve.tensor_scalar(c["bound"][:], maskf[:], 0.5, 2 * CLIP / SCALE, ALU.is_gt, ALU.mult).then_inc(s["mask_step"], 1)
            dve.wait_ge(s["mask_step"], 2)
            dve.tensor_scalar(c["bound"][:], c["bound"][:], -CLIP / SCALE, None, ALU.add).then_inc(s["mask_step"], 1)
            dve.tensor_scalar(c["rs"][:], c["rs"][:], 0.0, 0.3, ALU.max, ALU.min).then_inc(s["rs_step"], 1)
            dve.wait_ge(s["rs_step"], 1)
            dve.tensor_tensor(c["rs2"][:], c["rs"][:], c["rs"][:], ALU.mult).then_inc(s["rs_step"], 1)

        @block.gpsimd
        def _(pool):
            pool.wait_ge(s["small_in"], 160)
            pool.tensor_copy(bv_wide[:], bv[:].unsqueeze(2).to_broadcast([P, KC, P])).then_inc(s["wide_done"], 1)
            pool.memset(f32(c["ctx"][0][:, :, S:SE]), 0.0).then_inc(s["setup"], 1)
            pool.memset(f32(c["ctx"][1][:, :, S:SE]), 0.0).then_inc(s["setup"], 1)
            for n in range(2):
                pool.memset(f32(c["qbd"][n][:]), 0.0).then_inc(s["setup"], 1)

        @block.tensor
        def _(pe):
            pe.wait_ge(s["wide_done"], 1)
            pe.wait_ge(s["o_in"], 16)
            for k in range(KC):
                last = pe.matmul(ps[:], bv_wide[:, k], raw["o"][:, k], start=(k == 0), stop=(k == KC - 1))
            last.then_inc(s["bias_ready"], 1)


def build_cross(nc, dram, w, c, sems):
    with ExitStack() as scope:
        m = Memory(nc, scope)
        xa = m.sb("xa", [T, 2, D])
        xr = m.sb("xr", [T, 2, D])
        fence = m.sb("fence_f2", [1, 1])
        st = m.sb("st2", [T, 2, 6])
        mv = m.sb("mv2", [T, 2, 2])
        veps = m.sb("veps2", [T, 2, 1])
        rstd = m.sb("rstd2", [T, 2, 1])
        xn = m.sb("xn2", [T, 2, D])
        xt = [m.sb(f"xt2_{n}", [P, KC, PT], F32R) for n in ("hi", "lo")]
        q = [m.sb(f"q2_{n}", [P, KC, PT], F32R) for n in ("hi", "lo")]
        qbd, ctx = c["qbd"], c["ctx"]
        craw = m.sb("craw", [P, KC, S])
        k = [[m.sb(f"k2_{n}{j}", [P, KC, SE], F32R) for n in ("hi", "lo")] for j in range(2)]
        v = m.sb("v2", [KP, 2, KT, D])
        e = m.sb("e2", [KP, 2, KT, QT])
        esum = m.sb("esum", [KP, 2, QT])
        rz = m.sb("rz", [P, T])
        rzx = m.sb("rzx", [P, QT])
        on = m.sb("on", [P, QT])
        ot = [m.sb(f"ot2_{n}", [P, KC, T], F32R) for n in ("hi", "lo")]
        y = m.sb("y", [T, D])
        yst = m.sb("yst", [T, 6])
        ymv = m.sb("ymv", [T, 2])
        ysc = m.sb("ysc", [T, 4])
        gen = [m.ps(f"gen2_{n}", [P, 512]) for n in range(2)]
        sc = m.ps("sc2", [P, 4, 512])
        av = m.ps("av2", [P, 512])
        z = m.ps("z2", [P, 512])

        names = ("xa_in xr_in0 xr_in1 c_in x2_out0 x2_out1 stats_done aggr_done veps_done rstd_done xn_done xt_ready "
                 "xt_hi_done xt_lo_done q_ready q_hi_done q_lo_done qbd_hi_done qbd_lo_done c_hi_done c_lo_done "
                 "k_ready k_hi_done k_lo_done v_ready v_done sc_done clip_done exp_done esum_step av_done z_done "
                 "rz_done zx_ready rzx_done on_done ot_hi_done ot_lo_done y_ready y_done yst_done ymv_done ysc_step "
                 "d_done x2_step").split()
        s = {n: sems.sem("c_" + n) for n in names}
        xr_in, x2_out = (s["xr_in0"], s["xr_in1"]), (s["x2_out0"], s["x2_out1"])
        LASTB = B - 1

        def known(i, *values):
            return isinstance(i, int) and i in values

        block = scope.enter_context(nc.Block())

        @block.sync
        def _(sp):
            def context(n):
                at = bass.ds(held(sp, n * KC * S), KC * S)
                if not known(n, 0):
                    sp.wait_ge(s["c_lo_done"], 2 * n)
                sp.dma_start(craw[:].rearrange("p c s -> p (c s)"), dram["ctx"][:, at]).then_inc(s["c_in"], 16)

            def pair(i):
                at = bass.ds(held(sp, i * 2 * D), 2 * D)
                if not known(i, 0):
                    sp.wait_ge(s["xn_done"], 2 * i)
                sp.dma_start(xa[:].rearrange("t j d -> t (j d)"), dram["x1"][:, at]).then_inc(s["xa_in"], 16)

            def residual(i, j):
                at = bass.ds(held(sp, (2 * i + j) * D), D)
                if not known(i, 0):
                    sp.wait_ge(x2_out[j], 16 * i)
                sp.dma_start(xr[:, j], dram["x1"][:, at]).then_inc(xr_in[j], 16)

            def store(i, j):
                at = bass.ds(held(sp, (2 * i + j) * T), T)
                sp.wait_ge(s["x2_step"], 3 * (2 * i + j) + 3)
                sp.dma_start(dram["x2"][at, :], xr[:, j]).then_inc(x2_out[j], 16)

            def step(i, first, more, more_pairs):
                if not first:
                    store(i - 1, 1)
                    residual(i, 1)
                if more:
                    context(2 * i + 3)
                if more_pairs:
                    pair(i + 2)
                store(i, 0)
                if more:
                    residual(i + 1, 0)
                if more_pairs:
                    context(2 * i + 4)

            pair(0)
            context(0)
            context(1)
            pair(1)
            residual(0, 0)
            residual(0, 1)
            context(2)
            step(0, True, True, True)
            with sp.Fori(1, PAIRS - 2) as i:
                step(i, False, True, True)
            step(PAIRS - 2, False, True, False)
            step(PAIRS - 1, False, False, False)
            store(PAIRS - 1, 1)
            for j in range(2):
                sp.wait_ge(x2_out[j], 16 * PAIRS)

        @block.gpsimd
        def _(pool):
            def layernorm(i):
                for j in range(2):
                    pool.wait_ge(s["aggr_done"], 2 * i + j + 1)
                    pool.tensor_tensor(veps[:, j], mv[:, j, 1:2], c["eps"][0:T], ALU.add).then_inc(s["veps_done"], 1)
                    pool.wait_ge(s["veps_done"], 2 * i + j + 1)
                    pool.tensor_tensor(rstd[:, j], veps[:, j], c["minus_half"][0:T], ALU.pow).then_inc(s["rstd_done"], 1)

            def sum_tiles(n, u):
                pool.wait_ge(s["exp_done"], 4 * n + u + 1)
                if not (known(n, 0) and u < 2):
                    pool.wait_ge(s["z_done"], 4 * n + u - 1)
                pool.tensor_tensor(esum[:, u % 2], e[:, u % 2, 0], e[:, u % 2, 1], ALU.add).then_inc(s["esum_step"], 1)
                pool.wait_ge(s["esum_step"], 8 * n + 2 * u + 1)
                pool.tensor_tensor(esum[:, u % 2], esum[:, u % 2], e[:, u % 2, 2], ALU.add).then_inc(s["esum_step"], 1)

            def tail_scale(n):
                pool.wait_ge(s["ymv_done"], n + 1)
                for step, (a, b, op) in enumerate(((ymv[:, 1:2], c["rs2"][0:T], ALU.mult), (ysc[:, 0:1], c["eps"][0:T], ALU.add),
                                                   (ysc[:, 1:2], c["minus_half"][0:T], ALU.pow), (ysc[:, 2:3], c["rs"][0:T], ALU.mult))):
                    if step:
                        pool.wait_ge(s["ysc_step"], 4 * n + step)
                    pool.tensor_tensor(ysc[:, step:step + 1], a, b, op).then_inc(s["ysc_step"], 1)

            def tail(i, j):
                n = 2 * i + j
                pool.wait_ge(s["d_done"], n + 1)
                pool.tensor_tensor(y[:], y[:], c["gamma"][0:T], ALU.mult).then_inc(s["x2_step"], 1)
                pool.wait_ge(s["x2_step"], 3 * n + 1)
                pool.tensor_tensor(y[:], y[:], c["beta"][0:T], ALU.add).then_inc(s["x2_step"], 1)
                pool.wait_ge(s["x2_step"], 3 * n + 2)
                pool.wait_ge(xr_in[j], 16 * i + 16)
                pool.tensor_tensor(xr[:, j], xr[:, j], y[:], ALU.add).then_inc(s["x2_step"], 1)

            def step(i, j, last_pair):
                n = 2 * i + j
                sum_tiles(n, 0)
                sum_tiles(n, 1)
                if not known(n, 0):
                    tail_scale(n - 1)
                if j == 0 and not last_pair:
                    layernorm(i + 1)
                sum_tiles(n, 2)
                if not known(n, 0):
                    tail(i - 1, 1) if j == 0 else tail(i, 0)
                sum_tiles(n, 3)

            layernorm(0)
            step(0, 0, False)
            step(0, 1, False)
            with pool.Fori(1, PAIRS - 1) as i:
                step(i, 0, False)
                step(i, 1, False)
            step(PAIRS - 1, 0, True)
            step(PAIRS - 1, 1, True)
            tail_scale(LASTB)
            tail(PAIRS - 1, 1)

        @block.tensor
        def _(pe):
            def project_k(n, slot, mt, g):
                for kc in range(KC):
                    if mt == 0 and kc % 2 == 0:
                        pe.wait_ge(s["c_lo_done"], 2 * n + kc // 2 + 1)
                    last = three_pass(pe, gen[g][:, 0:SE], w["k"][0][:, kc, mt * P:(mt + 1) * P], w["k"][1][:, kc, mt * P:(mt + 1) * P],
                                      ctx[0][:, kc], ctx[1][:, kc], kc == 0, kc == KC - 1)
                last.then_inc(s["k_ready"], 1)

            def project_v(n, kt, g):
                for kc in range(KC):
                    last = three_pass(pe, gen[g][0:KP, :], ctx[0][:, kc, kt * KP:(kt + 1) * KP], ctx[1][:, kc, kt * KP:(kt + 1) * KP],
                                      w["v"][0][:, kc], w["v"][1][:, kc], kc == 0, kc == KC - 1)
                last.then_inc(s["v_ready"], 1)

            def transpose_x(i, j):
                pe.wait_ge(s["xn_done"], 2 * i + j + 1)
                for kc in range(KC):
                    last = pe.transpose(gen[j][:, kc * T:(kc + 1) * T], xn[:, j, kc * P:(kc + 1) * P], c["ident"][0:T, 0:T])
                last.then_inc(s["xt_ready"], 1)

            def project_q(i, half, g):
                if half == 0:
                    pe.wait_ge(s["xt_lo_done"], 2 * i + 2)
                for o in range(2):
                    mt = 2 * half + o
                    for kc in range(KC):
                        last = three_pass(pe, gen[g][:, o * PT:(o + 1) * PT], w["q"][0][:, kc, mt * P:(mt + 1) * P],
                                          w["q"][1][:, kc, mt * P:(mt + 1) * P], xt[0][:, kc], xt[1][:, kc], kc == 0, kc == KC - 1)
                last.then_inc(s["q_ready"], 1)

            def scores(n, j, u):
                if u == 0:
                    pe.wait_ge(s["qbd_hi_done"], n + 1)
                    pe.wait_ge(s["qbd_lo_done"], n + 1)
                for kt in range(KT):
                    r = KT * u + kt
                    if not (known(n, 0) and r < 4):
                        pe.wait_ge(s["clip_done"], 12 * n + r - 3)
                    last = three_pass(pe, sc[0:KP, r % 4, 0:QT], k[j][0][:, u, kt * KP:(kt + 1) * KP], k[j][1][:, u, kt * KP:(kt + 1) * KP],
                                      qbd[0][:, u].rearrange("p h t -> p (h t)"), qbd[1][:, u].rearrange("p h t -> p (h t)"), True, True)
                    last.then_inc(s["sc_done"], 1)

            def attend(n, j, u):
                pe.wait_ge(s["exp_done"], 4 * n + u + 1)
                if u == 0:
                    pe.wait_ge(s["v_done"], 3 * n + 3)
                    if not known(n, 0):
                        pe.wait_ge(s["on_done"], n)
                for kt in range(KT):
                    for h in range(HQ):
                        head = u * HQ + h
                        last = pe.matmul(av[DH * h:DH * (h + 1), u * T:(u + 1) * T], v[:, j, kt, head * DH:(head + 1) * DH],
                                         e[:, u % 2, kt, h * T:(h + 1) * T], start=(kt == 0), stop=(kt == KT - 1))
                last.then_inc(s["av_done"], 1)

            def sums(n, u):
                pe.wait_ge(s["esum_step"], 8 * n + 2 * u + 2)
                if u == 0 and not known(n, 0):
                    pe.wait_ge(s["rzx_done"], n)
                for h in range(HQ):
                    last = pe.matmul(z[DH * h:DH * (h + 1), 0:T], c["sel"][0:KP, u], esum[:, u % 2, h * T:(h + 1) * T],
                                     start=(u == 0), stop=(u == HQ - 1))
                last.then_inc(s["z_done"], 1)

            def spread(n):
                pe.wait_ge(s["rz_done"], n + 1)
                for u in range(KC):
                    last = pe.matmul(z[:, u * T:(u + 1) * T], c["spread"][:, u], rz[:], start=True, stop=True)
                last.then_inc(s["zx_ready"], 1)

            def output(n, g):
                pe.wait_ge(s["ot_lo_done"], n + 1)
                for kc in range(KC):
                    last = three_pass(pe, gen[g][0:T, :], ot[0][:, kc], ot[1][:, kc], w["o"][0][:, kc], w["o"][1][:, kc],
                                      kc == 0, kc == KC - 1)
                last.then_inc(s["y_ready"], 1)

            def step(i, j, more, more_pairs):
                n = 2 * i + j
                extra = j == 1 and more_pairs
                scores(n, j, 0)
                if not known(n, 0):
                    spread(n - 1)
                scores(n, j, 1)
                if more:
                    pe.wait_ge(s["v_done"], 3 * n + 2)
                    project_k(n + 1, 1 - j, 0, 1)
                    pe.wait_ge(s["v_done"], 3 * n + 3)
                    project_k(n + 1, 1 - j, 1, 0)
                attend(n, j, 0)
                if extra:
                    pe.wait_ge(s["k_lo_done"], 4 * n + 6)
                    transpose_x(i + 1, 0)
                if not known(n, 0):
                    pe.wait_ge(s["k_lo_done"], 4 * n + 5) if more else pe.wait_ge(s["v_done"], 3 * n + 2)
                    output(n - 1, 1)
                scores(n, j, 2)
                if extra:
                    pe.wait_ge(s["y_done"], n)
                    transpose_x(i + 1, 1)
                if more:
                    pe.wait_ge(s["xt_lo_done"], 2 * i + 3) if extra else pe.wait_ge(s["k_lo_done"], 4 * n + 6)
                    project_k(n + 1, 1 - j, 2, 0)
                if extra:
                    project_q(i + 1, 0, 1)
                sums(n, 0)
                attend(n, j, 1)
                if more:
                    if extra:
                        pe.wait_ge(s["k_lo_done"], 4 * n + 7)
                        project_k(n + 1, 1 - j, 3, 0)
                        pe.wait_ge(s["q_lo_done"], 2 * i + 3)
                        project_q(i + 1, 1, 1)
                    else:
                        pe.wait_ge(s["k_lo_done"], 5) if known(n, 0) else pe.wait_ge(s["y_done"], n)
                        project_k(n + 1, 1 - j, 3, 1)
                sums(n, 1)
                scores(n, j, 3)
                if more:
                    pe.wait_ge(s["k_lo_done"], 4 * n + (8 if extra else 7))
                    project_v(n + 1, 0, 0)
                attend(n, j, 2)
                if more:
                    pe.wait_ge(s["q_lo_done"], 2 * i + 4) if extra else pe.wait_ge(s["k_lo_done"], 4 * n + 8)
                    project_v(n + 1, 1, 1)
                sums(n, 2)
                attend(n, j, 3)
                if more:
                    pe.wait_ge(s["v_done"], 3 * n + 4)
                    project_v(n + 1, 2, 0)
                sums(n, 3)

            transpose_x(0, 0)
            transpose_x(0, 1)
            for mt in range(KC):
                pe.wait_ge(s["xt_lo_done"], mt + 1) if mt < 2 else pe.wait_ge(s["k_lo_done"], mt - 1)
                project_k(0, 0, mt, mt % 2)
            for half in range(2):
                pe.wait_ge(s["k_lo_done"], 3 + half)
                project_q(0, half, half)
            for kt in range(KT):
                pe.wait_ge(s["q_lo_done"], kt + 1) if kt < 2 else pe.wait_ge(s["v_done"], 1)
                project_v(0, kt, kt % 2)
            step(0, 0, True, True)
            step(0, 1, True, True)
            with pe.Fori(1, PAIRS - 1) as i:
                step(i, 0, True, True)
                step(i, 1, True, True)
            step(PAIRS - 1, 0, True, False)
            step(PAIRS - 1, 1, False, False)
            spread(LASTB)
            pe.wait_ge(s["y_done"], LASTB)
            output(LASTB, 1)

        @block.scalar
        def _(act):
            def context_hi(n):
                act.wait_ge(s["c_in"], 16 * n + 16)
                if not known(n, 0):
                    act.wait_ge(s["v_ready"], 3 * n)
                for r in (slice(0, 2), slice(2, KC)):
                    act.activation(ctx[0][:, r, 0:S], craw[:, r], ACT.Copy).then_inc(s["c_hi_done"], 1)

            def k_hi(n, slot, mt, g):
                act.wait_ge(s["k_ready"], 4 * n + mt + 1)
                act.activation(k[slot][0][:, mt], gen[g][:, 0:SE], ACT.Identity, bias=c["bk"][:, mt:mt + 1]).then_inc(s["k_hi_done"], 1)

            def v_copy(n, slot, kt, g):
                act.wait_ge(s["v_ready"], 3 * n + kt + 1)
                act.activation(v[:, slot, kt], gen[g][0:KP, :], ACT.Copy).then_inc(s["v_done"], 1)

            def x_hi(i):
                for j in range(2):
                    act.wait_ge(s["xt_ready"], 2 * i + j + 1)
                    act.activation(xt[0][:, :, j * T:(j + 1) * T], gen[j][:, 0:QT].rearrange("p (c t) -> p c t", c=KC),
                                   ACT.Copy).then_inc(s["xt_hi_done"], 1)

            def q_hi(i, half, g):
                act.wait_ge(s["q_ready"], 2 * i + half + 1)
                for o in range(2):
                    mt = 2 * half + o
                    last = act.activation(q[0][:, mt], gen[g][:, o * PT:(o + 1) * PT], ACT.Identity, bias=c["bq"][:, mt:mt + 1])
                last.then_inc(s["q_hi_done"], 1)

            def place_q(n, j, i):
                act.wait_ge(s["q_hi_done"], 2 * i + 2)
                if not known(n, 0):
                    act.wait_ge(s["sc_done"], 12 * n)
                for h in range(HQ):
                    r = slice(DH * h, DH * (h + 1))
                    last = act.activation(qbd[0][r, :, h], f32(q[0][r, :, j * T:(j + 1) * T]), ACT.Copy)
                last.then_inc(s["qbd_hi_done"], 1)

            def exp(n, u):
                act.wait_ge(s["clip_done"], 12 * n + 3 * u + 3)
                act.activation(e[:, u % 2], e[:, u % 2], ACT.Exp, scale=SCALE).then_inc(s["exp_done"], 1)

            def spread_copy(n):
                act.wait_ge(s["zx_ready"], n + 1)
                act.activation(rzx[:], z[:, 0:QT], ACT.Copy).then_inc(s["rzx_done"], 1)

            def out_hi(n):
                act.wait_ge(s["on_done"], n + 1)
                if not known(n, 0):
                    act.wait_ge(s["y_ready"], n)
                act.activation(ot[0][:].rearrange("p c t -> p (c t)"), on[:], ACT.Copy).then_inc(s["ot_hi_done"], 1)

            def step(i, j, more, more_pairs, more_context):
                n = 2 * i + j
                extra = j == 1 and more_pairs
                if not known(n, 0):
                    spread_copy(n - 1)
                exp(n, 0)
                if not known(n, 0):
                    out_hi(n - 1)
                exp(n, 1)
                if more:
                    k_hi(n + 1, 1 - j, 0, 1)
                if more:
                    k_hi(n + 1, 1 - j, 1, 0)
                if extra:
                    x_hi(i + 1)
                exp(n, 2)
                if more:
                    k_hi(n + 1, 1 - j, 2, 0)
                if extra:
                    q_hi(i + 1, 0, 1)
                if more:
                    k_hi(n + 1, 1 - j, 3, 0 if extra else 1)
                if extra:
                    q_hi(i + 1, 1, 1)
                exp(n, 3)
                if more:
                    place_q(n + 1, 1 - j, i + j)
                    for kt in range(KT):
                        v_copy(n + 1, 1 - j, kt, kt % 2)
                if more_context:
                    context_hi(n + 2)

            context_hi(0)
            x_hi(0)
            for mt in range(KC):
                k_hi(0, 0, mt, mt % 2)
            for half in range(2):
                q_hi(0, half, half)
            place_q(0, 0, 0)
            for kt in range(KT):
                v_copy(0, 0, kt, kt % 2)
            context_hi(1)
            step(0, 0, True, True, True)
            step(0, 1, True, True, True)
            with act.Fori(1, PAIRS - 1) as i:
                step(i, 0, True, True, True)
                step(i, 1, True, True, True)
            step(PAIRS - 1, 0, True, False, False)
            step(PAIRS - 1, 1, False, False, False)
            spread_copy(LASTB)
            out_hi(LASTB)

        @block.vector
        def _(dve):
            def context_lo(n):
                for part, r in enumerate((slice(0, 2), slice(2, KC))):
                    dve.wait_ge(s["c_hi_done"], 2 * n + part + 1)
                    dve.tensor_tensor(ctx[1][:, r, 0:S], craw[:, r], f32(ctx[0][:, r, 0:S]), ALU.subtract).then_inc(s["c_lo_done"], 1)

            def layernorm_stats(i):
                dve.wait_ge(s["xa_in"], 16 * i + 16)
                for j in range(2):
                    dve.bn_stats(st[:, j], xa[:, j]).then_inc(s["stats_done"], 1)
                if not known(i, 0):
                    dve.wait_ge(s["xn_done"], 2 * i)
                dve.wait_ge(s["stats_done"], 2 * i + 2)
                carry_waits(dve, fence[:])
                for j in range(2):
                    dve.bn_aggr(mv[:, j], st[:, j]).then_inc(s["aggr_done"], 1)

            def layernorm_apply(i):
                for j in range(2):
                    dve.wait_ge(s["rstd_done"], 2 * i + j + 1)
                    if not known(i, 0):
                        dve.wait_ge(s["xt_ready"], 2 * i + j - 1)
                    dve.tensor_scalar(xn[:, j], xa[:, j], mv[:, j, 0:1], rstd[:, j], ALU.subtract, ALU.mult)\
                       .then_inc(s["xn_done"], 1)

            def x_lo(i):
                for j in range(2):
                    dve.wait_ge(s["xt_hi_done"], 2 * i + j + 1)
                    dve.tensor_tensor(xt[1][:, :, j * T:(j + 1) * T], gen[j][:, 0:QT].rearrange("p (c t) -> p c t", c=KC),
                                      f32(xt[0][:, :, j * T:(j + 1) * T]), ALU.subtract).then_inc(s["xt_lo_done"], 1)

            def k_lo(n, slot, mt, g):
                dve.wait_ge(s["k_hi_done"], 4 * n + mt + 1)
                dve.scalar_tensor_tensor(out=k[slot][1][:, mt], in0=gen[g][:, 0:SE], scalar=c["bk"][:, mt:mt + 1],
                                         in1=f32(k[slot][0][:, mt]), op0=ALU.add, op1=ALU.subtract).then_inc(s["k_lo_done"], 1)

            def q_lo(i, half, g):
                dve.wait_ge(s["q_hi_done"], 2 * i + half + 1)
                for o in range(2):
                    mt = 2 * half + o
                    last = dve.scalar_tensor_tensor(out=q[1][:, mt], in0=gen[g][:, o * PT:(o + 1) * PT], scalar=c["bq"][:, mt:mt + 1],
                                                    in1=f32(q[0][:, mt]), op0=ALU.add, op1=ALU.subtract)
                last.then_inc(s["q_lo_done"], 1)

            def place_q(n, j, i):
                dve.wait_ge(s["q_lo_done"], 2 * i + 2)
                if not known(n, 0):
                    dve.wait_ge(s["sc_done"], 12 * n)
                for h in range(HQ):
                    r = slice(DH * h, DH * (h + 1))
                    last = dve.tensor_copy(qbd[1][r, :, h], q[1][r, :, j * T:(j + 1) * T])
                last.then_inc(s["qbd_lo_done"], 1)

            def clip(n, u):
                if not (known(n, 0) and u < 2):
                    dve.wait_ge(s["av_done"], 4 * n + u - 1)
                    dve.wait_ge(s["esum_step"], 8 * n + 2 * u - 2)
                for kt in range(KT):
                    r = KT * u + kt
                    dve.wait_ge(s["sc_done"], 12 * n + r + 1)
                    dve.tensor_scalar(e[:, u % 2, kt], sc[0:KP, r % 4, 0:QT], c["bound"][:, bass.ds(n * KT + kt, 1)],
                                      -CLIP / SCALE, ALU.min, ALU.max).then_inc(s["clip_done"], 1)

            def tail_stats(n):
                dve.wait_ge(s["y_ready"], n + 1)
                if not known(n, 0):
                    dve.wait_ge(s["x2_step"], 3 * n)
                dve.tensor_tensor(y[:], gen[1][0:T, :], c["bo_full"][0:T], ALU.add).then_inc(s["y_done"], 1)
                dve.wait_ge(s["y_done"], n + 1)
                dve.bn_stats(yst[:], y[:]).then_inc(s["yst_done"], 1)
                dve.wait_ge(s["yst_done"], n + 1)
                carry_waits(dve, fence[:])
                dve.bn_aggr(ymv[:], yst[:]).then_inc(s["ymv_done"], 1)

            def tail_apply(n):
                dve.wait_ge(s["ysc_step"], 4 * n + 4)
                dve.tensor_scalar(y[:], y[:], ymv[:, 0:1], ysc[:, 3:4], ALU.subtract, ALU.mult).then_inc(s["d_done"], 1)

            def invert_sums(n):
                dve.wait_ge(s["z_done"], 4 * n + 4)
                dve.reciprocal(rz[:], z[:, 0:T]).then_inc(s["rz_done"], 1)

            def normalise(n):
                dve.wait_ge(s["rzx_done"], n + 1)
                dve.wait_ge(s["av_done"], 4 * n + 4)
                if not known(n, 0):
                    dve.wait_ge(s["ot_lo_done"], n)
                dve.tensor_tensor(on[:], av[:, 0:QT], rzx[:], ALU.mult).then_inc(s["on_done"], 1)

            def out_lo(n):
                dve.wait_ge(s["ot_hi_done"], n + 1)
                dve.tensor_tensor(ot[1][:].rearrange("p c t -> p (c t)"), on[:], f32(ot[0][:].rearrange("p c t -> p (c t)")),
                                  ALU.subtract).then_inc(s["ot_lo_done"], 1)

            def step(i, j, more, more_pairs, more_context):
                n = 2 * i + j
                extra = j == 1 and more_pairs
                if not known(n, 0):
                    invert_sums(n - 1)
                clip(n, 0)
                if more and not known(n, 0):
                    context_lo(n + 1)
                if not known(n, 0):
                    normalise(n - 1)
                clip(n, 1)
                if not known(n, 0):
                    out_lo(n - 1)
                if more:
                    k_lo(n + 1, 1 - j, 0, 1)
                    k_lo(n + 1, 1 - j, 1, 0)
                if not known(n, 0):
                    tail_stats(n - 1)
                if extra:
                    x_lo(i + 1)
                if j == 0 and more_pairs:
                    layernorm_stats(i + 1)
                clip(n, 2)
                if more:
                    k_lo(n + 1, 1 - j, 2, 0)
                if extra:
                    q_lo(i + 1, 0, 1)
                if not known(n, 0):
                    tail_apply(n - 1)
                if more:
                    k_lo(n + 1, 1 - j, 3, 0 if extra else 1)
                if extra:
                    q_lo(i + 1, 1, 1)
                if j == 0 and more_pairs:
                    layernorm_apply(i + 1)
                clip(n, 3)
                if more:
                    place_q(n + 1, 1 - j, i + j)

            layernorm_stats(0)
            context_lo(0)
            layernorm_apply(0)
            x_lo(0)
            for mt in range(KC):
                k_lo(0, 0, mt, mt % 2)
            for half in range(2):
                q_lo(0, half, half)
            place_q(0, 0, 0)
            context_lo(1)
            step(0, 0, True, True, True)
            step(0, 1, True, True, True)
            with dve.Fori(1, PAIRS - 1) as i:
                step(i, 0, True, True, True)
                step(i, 1, True, True, True)
            step(PAIRS - 1, 0, True, False, False)
            step(PAIRS - 1, 1, False, False, False)
            invert_sums(LASTB)
            normalise(LASTB)
            out_lo(LASTB)
            tail_stats(LASTB)
            tail_apply(LASTB)


def build_ffn(nc, dram, consts, sems):
    with ExitStack() as scope:
        m = Memory(nc, scope)
        x = m.sb("x3", [P, FT * D])
        xt = [m.sb(f"xt3_{n}", [P, KC, TOK], F32R) for n in ("hi", "lo")]
        fence = m.sb("fence_f3", [1, 1])
        st = m.sb("st3", [P, 2, 6])
        mv = m.sb("mv3", [P, 2, 2])
        veps = m.sb("veps3", [P, 2, 1])
        rstd = m.sb("rstd3", [P, 2, 1])
        xn = m.sb("xn3", [P, 2, D])
        raw = [m.sb(f"raw_w{n}", [P, KC, HC]) for n in (1, 3)]
        raw2 = m.sb("raw_w2", [P, HT, D])
        wg = [[[m.sb(f"w{n}_{part}{slot}", [P, KC, HC], F32R) for part in ("hi", "lo")] for n in (1, 3)] for slot in range(2)]
        fly = [m.sb(f"fly_{n}", [P, HT, D], F32R) for n in ("hi", "lo")]
        w2 = [[m.sb(f"w2_{part}{slot}", [P, HT, D], F32R) for part in ("hi", "lo")] for slot in range(2)]
        had = m.sb("had", [P, P], F32R)
        had_raw = m.sb("had_raw", [P, P])
        gate = m.sb("gate", [P, 2, 512])
        hf = m.sb("hf", [P, 2, 512])
        hid = [m.sb(f"hid_{n}", [P, 2, HT, 512], F32R) for n in ("hi", "lo")]
        psg = m.ps("psg", [P, 2, 512])
        psu = m.ps("psu", [P, 2, 512])
        psy = m.ps("psy", [P, 2, 512])
        psh = m.ps("psh", [P, 2, 512])
        names = ("x_in0 x_in1 stats_done aggr_done veps_done rstd_done xn_done xt_ready xt_hi_done xt_lo_done had_in had_done "
                 "w_in0 w_in1 w_in2 w_hi_done w_lo_done fly_ready w2_hi_done w2_lo_done gate_ready up_ready silu_done h_done "
                 "hid_hi_done hid_lo_done y_ready y_done out_done").split()
        s = {n: sems.sem("f_" + n) for n in names}
        x_in, w_in = (s["x_in0"], s["x_in1"]), (s["w_in0"], s["w_in1"], s["w_in2"])
        TP = FT // 2
        UNITS = HT * len(FGROUPS)
        HSCALE = float(F) ** -0.5
        fly_dram = dram["w2_fly"].rearrange("p (c t) n -> p t c n", t=B)

        def known(i, *values):
            return isinstance(i, int) and i in values

        block = scope.enter_context(nc.Block())

        def xtile(t):
            return x[:, bass.ds(t * D, D)]

        @block.sync
        def _(sp):
            def tile(i, j):
                at, row = bass.ds(held(sp, (2 * i + j) * D), D), bass.ds(held(sp, (2 * i + j) * P), P)
                if not known(i, 0):
                    sp.wait_ge(x_in[j], 16 * i)
                sp.dma_start(x[:, at], dram["x2"][row, :]).then_inc(x_in[j], 16)

            def weights(c):
                at = bass.ds(held(sp, c * KC * HC), KC * HC)
                rows = [bass.ds(held(sp, c * HT + t), 1) for t in range(HT)]
                if not known(c, 0):
                    sp.wait_ge(s["w_lo_done"], 3 * c)
                for n, name in enumerate(("w1", "w3")):
                    sp.dma_start(raw[n][:].rearrange("p k n -> p (k n)"), dram[name][:, at]).then_inc(w_in[n], 16)
                for t in range(HT):
                    sp.dma_start(raw2[:, t].rearrange("p (c n) -> p c n", n=BCOL),
                                 fly_dram[:, rows[t]].rearrange("p t c n -> p (t c) n")).then_inc(w_in[2], 16)

            tile(0, 0)
            tile(0, 1)
            sp.dma_start(had_raw[:], dram["had"]).then_inc(s["had_in"], 16)
            weights(0)
            with sp.Fori(1, TP) as i:
                for j in range(2):
                    tile(i, j)
            with sp.Fori(1, CHUNKS) as c:
                weights(c)
            for t in range(FT):
                sp.wait_ge(s["y_done"], (CHUNKS - 1) * FT + t + 1)
                sp.dma_start(dram["out"][t * P:(t + 1) * P, :], x[:, t * D:(t + 1) * D]).then_inc(s["out_done"], 16)
            sp.wait_ge(s["out_done"], 16 * FT)

        @block.gpsimd
        def _(pool):
            with pool.Fori(0, TP) as i:
                for j in range(2):
                    pool.wait_ge(s["aggr_done"], 2 * i + j + 1)
                    pool.tensor_tensor(veps[:, j], mv[:, j, 1:2], consts["eps"][:], ALU.add).then_inc(s["veps_done"], 1)
                    pool.wait_ge(s["veps_done"], 2 * i + j + 1)
                    pool.tensor_tensor(rstd[:, j], veps[:, j], consts["minus_half"][:], ALU.pow).then_inc(s["rstd_done"], 1)
            with pool.Fori(0, CHUNKS) as c:
                for n in range(UNITS):
                    width = FGROUPS[n // HT][1]
                    pool.wait_ge(s["hid_hi_done"], UNITS * c + n + 1)
                    pool.tensor_tensor(hid[1][:, (n // HT) % 2, n % HT, 0:width], hf[:, n % 2, 0:width],
                                       f32(hid[0][:, (n // HT) % 2, n % HT, 0:width]), ALU.subtract).then_inc(s["hid_lo_done"], 1)

        @block.tensor
        def _(pe):
            def transpose_x(i):
                for j in range(2):
                    pe.wait_ge(s["xn_done"], 2 * i + j + 1)
                    if not known(i, 0):
                        pe.wait_ge(s["xt_lo_done"], 2 * i + j - 1)
                    for kc in range(KC):
                        last = pe.transpose(psy[:, j, kc * P:(kc + 1) * P], xn[:, j, kc * P:(kc + 1) * P], consts["ident"][:])
                    last.then_inc(s["xt_ready"], 1)

            def hadamard(c):
                pe.wait_ge(s["w_lo_done"], 3 * c + 3)
                if not known(c, 0):
                    pe.wait_ge(s["w2_lo_done"], HT * c)
                for t in range(HT):
                    pe.matmul(psh[:, t], had[:], fly[0][:, t], start=True, stop=False)
                    pe.matmul(psh[:, t], had[:], fly[1][:, t], start=False, stop=True).then_inc(s["fly_ready"], 1)

            def up(c, slot, g):
                at, width = FGROUPS[g]
                for t in range(HT):
                    n = HT * g + t
                    if n == 0:
                        pe.wait_ge(s["w_lo_done"], 3 * c + 2)
                    for which, (ps, done) in enumerate(((psg, "gate_ready"), (psu, "up_ready"))):
                        if not (known(c, 0) and n < 2):
                            pe.wait_ge(s["silu_done" if which == 0 else "h_done"], UNITS * c + n - 1)
                        for kc in range(KC):
                            wh, wl = wg[slot][which]
                            last = three_pass(pe, ps[:, t, 0:width], wh[:, kc, t * P:(t + 1) * P], wl[:, kc, t * P:(t + 1) * P],
                                              xt[0][:, kc, at:at + width], xt[1][:, kc, at:at + width], kc == 0, kc == KC - 1)
                        last.then_inc(s[done], 1)

            def down(c, slot, g):
                at, width = FGROUPS[g]
                pe.wait_ge(s["hid_lo_done"], UNITS * c + HT * g + HT)
                if g == 0:
                    pe.wait_ge(s["w2_lo_done"], HT * c + HT)
                for k in range(width // P):
                    tile = at // P + k
                    if not (known(c, 0) and tile < 2):
                        pe.wait_ge(s["y_done"], FT * c + tile - 1)
                    for t in range(HT):
                        last = three_pass(pe, psy[:, tile % 2], hid[0][:, g % 2, t, k * P:(k + 1) * P], hid[1][:, g % 2, t, k * P:(k + 1) * P],
                                          w2[slot][0][:, t], w2[slot][1][:, t], t == 0, t == HT - 1)
                    last.then_inc(s["y_ready"], 1)

            def chunk(c, slot, more):
                up(c, slot, 0)
                if not known(c, 0):
                    down(c - 1, 1 - slot, 3)
                up(c, slot, 1)
                down(c, slot, 0)
                up(c, slot, 2)
                down(c, slot, 1)
                up(c, slot, 3)
                if more:
                    hadamard(c + 1)
                down(c, slot, 2)

            transpose_x(0)
            with pe.Fori(1, TP) as i:
                transpose_x(i)
            hadamard(0)
            pe.wait_ge(s["xt_lo_done"], FT)
            chunk(0, 0, True)
            chunk(1, 1, True)
            with pe.Fori(1, CHUNKS // 2 - 1) as i:
                chunk(2 * i, 0, True)
                chunk(2 * i + 1, 1, True)
            chunk(CHUNKS - 2, 0, True)
            chunk(CHUNKS - 1, 1, False)
            down(CHUNKS - 1, 1, 3)

        @block.scalar
        def _(act):
            def x_hi(i):
                for j in range(2):
                    act.wait_ge(s["xt_ready"], 2 * i + j + 1)
                    act.activation(xt[0][:, :, bass.ds((2 * i + j) * P, P)], psy[:, j].rearrange("p (c t) -> p c t", c=KC),
                                   ACT.Copy).then_inc(s["xt_hi_done"], 1)

            def split_hi(c, slot, parts):
                for n in parts:
                    dst, src = ((wg[slot][0][0], raw[0]), (wg[slot][1][0], raw[1]), (fly[0], raw2))[n]
                    act.wait_ge(w_in[n], 16 * c + 16 if n < 2 else 32 * c + 32)
                    if n == 2 and not known(c, 0):
                        act.wait_ge(s["fly_ready"], HT * c)
                    act.activation(dst[:], src[:], ACT.Copy).then_inc(s["w_hi_done"], 1)

            def w2_hi(c, slot):
                for t in range(HT):
                    act.wait_ge(s["fly_ready"], HT * c + t + 1)
                    act.activation(w2[slot][0][:, t], psh[:, t], ACT.Copy, scale=HSCALE).then_inc(s["w2_hi_done"], 1)

            def unit(c, n):
                g, t, width = n // HT, n % HT, FGROUPS[n // HT][1]
                act.wait_ge(s["gate_ready"], UNITS * c + n + 1)
                if not (known(c, 0) and n < 2):
                    act.wait_ge(s["h_done"], UNITS * c + n - 1)
                act.activation(gate[:, t, 0:width], psg[:, t, 0:width], ACT.Silu).then_inc(s["silu_done"], 1)
                act.wait_ge(s["h_done"], UNITS * c + n + 1)
                act.activation(hid[0][:, g % 2, t, 0:width], hf[:, t, 0:width], ACT.Copy).then_inc(s["hid_hi_done"], 1)

            def chunk(c, slot, more):
                for n in range(UNITS):
                    if n % HT == 0 and not (known(c, 0) and n < 2 * HT):
                        act.wait_ge(s["y_ready"], FT * c + (-2, 0, 4, 8)[n // HT])
                    unit(c, n)
                    if n < 3 and more:
                        split_hi(c + 1, 1 - slot, (n,))
                if more:
                    w2_hi(c + 1, 1 - slot)

            split_hi(0, 0, range(3))
            with act.Fori(0, TP) as i:
                x_hi(i)
            w2_hi(0, 0)
            chunk(0, 0, True)
            chunk(1, 1, True)
            with act.Fori(1, CHUNKS // 2 - 1) as i:
                chunk(2 * i, 0, True)
                chunk(2 * i + 1, 1, True)
            chunk(CHUNKS - 2, 0, True)
            chunk(CHUNKS - 1, 1, False)

        @block.vector
        def _(dve):
            def stats(i):
                for j in range(2):
                    dve.wait_ge(x_in[j], 16 * i + 16)
                    dve.bn_stats(st[:, j], xtile(2 * i + j)).then_inc(s["stats_done"], 1)
                if not known(i, 0):
                    dve.wait_ge(s["xn_done"], 2 * i)
                dve.wait_ge(s["stats_done"], 2 * i + 2)
                carry_waits(dve, fence[:])
                for j in range(2):
                    dve.bn_aggr(mv[:, j], st[:, j]).then_inc(s["aggr_done"], 1)

            def apply(i):
                for j in range(2):
                    dve.wait_ge(s["rstd_done"], 2 * i + j + 1)
                    if not known(i, 0):
                        dve.wait_ge(s["xt_ready"], 2 * i + j - 1)
                    dve.tensor_scalar(xn[:, j], xtile(2 * i + j), mv[:, j, 0:1], rstd[:, j], ALU.subtract, ALU.mult)\
                       .then_inc(s["xn_done"], 1)

            def x_lo(i):
                for j in range(2):
                    dve.wait_ge(s["xt_hi_done"], 2 * i + j + 1)
                    at = bass.ds((2 * i + j) * P, P)
                    dve.tensor_tensor(xt[1][:, :, at], psy[:, j].rearrange("p (c t) -> p c t", c=KC), f32(xt[0][:, :, at]),
                                      ALU.subtract).then_inc(s["xt_lo_done"], 1)

            def split_lo(c, slot, parts):
                for n in parts:
                    dst, src = ((wg[slot][0], raw[0]), (wg[slot][1], raw[1]), (fly, raw2))[n]
                    dve.wait_ge(s["w_hi_done"], 3 * c + n + 1)
                    dve.tensor_tensor(dst[1][:], src[:], f32(dst[0][:]), ALU.subtract).then_inc(s["w_lo_done"], 1)

            def w2_lo(c, slot):
                for t in range(HT):
                    dve.wait_ge(s["w2_hi_done"], HT * c + t + 1)
                    dve.scalar_tensor_tensor(out=w2[slot][1][:, t], in0=psh[:, t], scalar=HSCALE, in1=f32(w2[slot][0][:, t]),
                                             op0=ALU.mult, op1=ALU.subtract).then_inc(s["w2_lo_done"], 1)

            def unit(c, n):
                t, width = n % HT, FGROUPS[n // HT][1]
                dve.wait_ge(s["silu_done"], UNITS * c + n + 1)
                dve.wait_ge(s["up_ready"], UNITS * c + n + 1)
                if not (known(c, 0) and n < 2):
                    dve.wait_ge(s["hid_lo_done"], UNITS * c + n - 1)
                dve.tensor_tensor(hf[:, t, 0:width], gate[:, t, 0:width], psu[:, t, 0:width], ALU.mult).then_inc(s["h_done"], 1)

            def add(c, tiles):
                for tile in tiles:
                    dve.wait_ge(s["y_ready"], FT * c + tile + 1)
                    part = x[:, tile * D:(tile + 1) * D]
                    dve.tensor_tensor(part, psy[:, tile % 2], part, ALU.add).then_inc(s["y_done"], 1)

            def chunk(c, slot, more):
                for n in range(4):
                    unit(c, n)
                    if n == 1 and not known(c, 0):
                        add(c - 1, (12, 13))
                    if n < 3 and more:
                        split_lo(c + 1, 1 - slot, (n,))
                add(c, range(0, 4))
                unit(c, 4)
                unit(c, 5)
                add(c, range(4, 8))
                unit(c, 6)
                unit(c, 7)
                add(c, range(8, 12))
                if more:
                    w2_lo(c + 1, 1 - slot)

            dve.wait_ge(s["had_in"], 16)
            dve.tensor_copy(had[:], had_raw[:]).then_inc(s["had_done"], 1)
            stats(0)
            apply(0)
            split_lo(0, 0, range(3))
            with dve.Fori(1, TP) as i:
                stats(i)
                x_lo(i - 1)
                apply(i)
            x_lo(TP - 1)
            w2_lo(0, 0)
            chunk(0, 0, True)
            chunk(1, 1, True)
            with dve.Fori(1, CHUNKS // 2 - 1) as i:
                chunk(2 * i, 0, True)
                chunk(2 * i + 1, 1, True)
            chunk(CHUNKS - 2, 0, True)
            chunk(CHUNKS - 1, 1, False)
            add(CHUNKS - 1, (12, 13))


def build(nc, dram):
    with ExitStack() as root:
        sems = Memory(nc, root)
        consts = {"ident": sems.sb("ident", [P, P]), "eps": sems.sb("eps", [P, 1]), "minus_half": sems.sb("minus_half", [P, 1])}
        with ExitStack() as scope:
            m = Memory(nc, scope)
            w = {n: [m.sb(f"w{n}_{part}", [P, KC, D], F32R) for part in ("hi", "lo")] for n in "qkvo"}
            build_prep(nc, dram, w, consts, sems)
            build_self(nc, dram, w, consts, sems)
        with ExitStack() as scope:
            m = Memory(nc, scope)
            w = {n: [m.sb(f"xw{n}_{part}", [P, KC, D], F32R) for part in ("hi", "lo")] for n in "qkvo"}
            c = dict(consts)
            for name, shape in (("bq", [P, KC]), ("bk", [P, KC]), ("bo_full", [P, D]), ("gamma", [P, D]), ("beta", [P, D]),
                                ("rs", [P, 1]), ("rs2", [P, 1]), ("bound", [KP, B * KT]), ("sel", [P, KC, DH]), ("spread", [P, KC, P])):
                c[name] = m.sb(name, shape)
            c["qbd"] = [m.sb(f"qbd_{n}", [P, KC, HQ, T], F32R) for n in ("hi", "lo")]
            c["ctx"] = [m.sb(f"ctx_{n}", [P, KC, SE], F32R) for n in ("hi", "lo")]
            build_prep_cross(nc, dram, w, c, sems)
            build_cross(nc, dram, w, c, sems)
        build_ffn(nc, dram, consts, sems)


def layouts(i):
    import numpy as np

    def stationary(w):
        return w.T.reshape(KC, P, D).transpose(1, 0, 2)

    def natural(w):
        return w.reshape(KC, P, D).transpose(1, 0, 2)

    def column(v):
        return v.reshape(KC, P).T

    def hidden(w):
        return w.T.reshape(KC, P, CHUNKS, HC).transpose(1, 2, 0, 3).reshape(P, CHUNKS * KC * HC)

    h = np.ones((1, 1), np.float32)
    while h.shape[0] < P:
        h = np.block([[h, h], [h, -h]])
    r = np.arange(P)
    sel = np.zeros((P, KC, DH), np.float32)
    spread = np.zeros((P, KC, P), np.float32)
    for u in range(KC):
        sel[:, u, u::KC] = 1.0
        for g in range(HQ):
            spread[DH * g + u, u, DH * g:DH * (g + 1)] = 1.0
    return {
        "x": i["x"].transpose(1, 0, 2).reshape(T, B * D),
        "ctx": i["ctx_2048"].transpose(2, 0, 1).reshape(KC, P, B, S).transpose(1, 2, 0, 3).reshape(P, B * KC * S),
        "mask": i["mask_BxS2_ik0"].reshape(B, KT, KP).transpose(2, 0, 1).reshape(KP, B * KT),
        "wq": natural(i["L0_attn_Wq"]), "wk": stationary(i["L0_attn_Wk"]), "wv": natural(i["L0_attn_Wv"]),
        "wo": stationary(i["L0_attn_Wo"]), "wdown_t": i["L0_attn_Wdown"].T, "wup": i["L0_attn_Wup"],
        "xq": stationary(i["L0_xattn_Wq"]), "xk": stationary(i["L0_xattn_Wk"]), "xv": stationary(i["L0_xattn_Wv"]),
        "xo": stationary(i["L0_xattn_Wo"]), "bq": column(i["L0_xattn_bq"]), "bk": column(i["L0_xattn_bk"]),
        "bv": column(i["L0_xattn_bv"]), "bo": i["L0_xattn_bo"].reshape(1, D), "gamma": i["L0_xattn_ln_gamma"].reshape(1, D),
        "beta": i["L0_xattn_ln_beta"].reshape(1, D), "rs": i["L0_xattn_residual_scale"].reshape(1, 1),
        "w1": hidden(i["L0_ffn_W1"]), "w3": hidden(i["L0_ffn_W3"]),
        "w2": i["L0_ffn_W2"].T.reshape(B, P, PAIRS, BCOL).transpose(1, 2, 0, 3).reshape(P, PAIRS * B, BCOL),
        "ident": np.eye(P, dtype=np.float32), "had": h, "sel": sel, "spread": spread,
    }


def kernel(**inputs):
    import numpy as np
    import concourse.bacc as bacc
    from concourse.bass_utils import run_bass_kernel_spmd

    nc = bacc.Bacc("TRN2", target_bir_lowering=False, num_devices=1)
    arrays = {"in_" + n: np.ascontiguousarray(a) for n, a in layouts({n: np.asarray(a) for n, a in inputs.items()}).items()}
    dram = {n[3:]: nc.dram_tensor(n, a.shape, mybir.dt.from_np(a.dtype), kind="ExternalInput").ap() for n, a in arrays.items()}
    dram["out"] = nc.dram_tensor("out", (TOK, D), F32, kind="ExternalOutput").ap()
    dram["x1"] = nc.dram_tensor("x1", (T, B * D), F32, kind="Internal").ap()
    dram["x2"] = nc.dram_tensor("x2", (TOK, D), F32, kind="Internal").ap()
    dram["w2_fly"] = nc.dram_tensor("w2_fly", (P, PAIRS * B, BCOL), F32, kind="Internal").ap()
    build(nc, dram)
    r = run_bass_kernel_spmd(nc, [arrays], core_ids=[0])
    return r.results[0]["out"].reshape(B, T, D)
```

```python
from contextlib import ExitStack

import concourse.bass as bass
from concourse import mybir

F32 = mybir.dt.float32
F32R = mybir.dt.float32r
I32 = mybir.dt.int32
ALU = mybir.AluOpType
ACT = mybir.ActivationFunctionType
AX_X = mybir.AxisListType.X

B, T, D = 16, 112, 512
S = 375
H, DH = 16, 32
F = 2048
P = 128
KC = D // P
HQ = P // DH
PAIRS = B // 2
PT = 2 * T
QT = HQ * T
KT = 3
KP = S // KT
SE = S + 1
EPS = 1e-5
SCALE = float(DH) ** -0.5
CLIP = 50.0
MASKED = -10000.0
TOK = B * T
FT = TOK // P
HC = 256
CHUNKS = F // HC
HT = HC // P
BCOL = D // PAIRS
FGROUPS = [(0, 512), (512, 512), (1024, 512), (1536, 256)]


def three_pass(eng, out, w_hi, w_lo, m_hi, m_lo, start, stop):
    eng.matmul(out, w_hi, m_hi, start=start, stop=False)
    eng.matmul(out, w_hi, m_lo, start=False, stop=False)
    return eng.matmul(out, w_lo, m_hi, start=False, stop=stop)


def held(eng, value):
    return value if isinstance(value, int) else eng.snap(value)


def carry_waits(eng, cell):
    eng.memset(cell, 0.0)


def f32(ap):
    return ap.bitcast(F32)


class Memory:

    def __init__(self, nc, scope):
        self.nc, self.scope = nc, scope

    def sb(self, name, shape, dt=F32):
        return self.scope.enter_context(self.nc.sbuf_tensor(name, shape, dt))

    def ps(self, name, shape, dt=F32):
        return self.scope.enter_context(self.nc.psum_tensor(name, shape, dt))

    def sem(self, name):
        return self.scope.enter_context(self.nc.semaphore(name))


def build_self(nc, dram, w, raw, consts, c, sems):
    UNITS = 4
    FLY_STAGES = ((), (0,), (1,), (2, 3))
    with ExitStack() as scope:
        m = Memory(nc, scope)
        x = m.sb("x", [T, B * D])
        fence = m.sb("fence_f1", [1, 1])
        st = m.sb("st", [T, 2, 6])
        mv = m.sb("mv", [T, 2, 2])
        veps = m.sb("veps", [T, 2, 1])
        rstd = m.sb("rstd", [T, 2, 1])
        xn = m.sb("xn", [T, 2, D])
        xt = [m.sb(f"xt_{n}", [P, KC, PT], F32R) for n in ("hi", "lo")]
        k = [m.sb(f"k_{n}", [P, KC, PT], F32R) for n in ("hi", "lo")]
        kbd = [m.sb(f"kbd_{n}", [P, KC, 2, HQ, T], F32R) for n in ("hi", "lo")]
        q = [m.sb(f"q_{n}", [P, KC, PT], F32R) for n in ("hi", "lo")]
        v = m.sb("v", [T, 2, D])
        mx = m.sb("mx", [T, 2, 8])
        bias = m.sb("bias", [T, 2, 8])
        e = m.sb("e", [T, 2, 8, T])
        total = m.sb("total", [T, 2, 8])
        rtotal = m.sb("rtotal", [T, 2, 8])
        pt = m.sb("pt", [T, 2, 8, T])
        ot = [m.sb(f"ot_{n}", [P, 2, KC, T], F32R) for n in ("hi", "lo")]
        fly = m.sb("fly", [P, 2, B, BCOL])
        down_bd = m.sb("down_bd", [P, P])
        up_bd = m.sb("up_bd", [P, P])
        fold_q = m.sb("fold_q", [P, P])
        fold_v = m.sb("fold_v", [P, P])
        gen = [m.ps(f"gen{n}", [P, 512]) for n in range(2)]
        sc = m.ps("sc", [P, 4, 512])
        av = m.ps("av", [P, 2, 512])

        names = ("x_in0 x_in1 stats_done aggr_done veps_done rstd_done xn_done xt_ready xt_hi_done xt_lo_done "
                 "k_ready k_hi_done k_lo_done kbd_done q_ready q_hi_done q_lo_done v_ready v_done "
                 "sc_done mx_done bias_done exp_done rtotal_done norm_done pt_ready pt_done av_done "
                 "ot_hi_done ot_lo_done y_ready x1_done x1_out0 x1_out1 fly_in fly_step fly_out kbd_zeroed "
                 "zeroed diag_in const_in raw_in0 raw_in1 folds_done folds_copied q_folded v_folded w_hi_done w_lo_done").split()
        s = {n: sems.sem("s_" + n) for n in names}
        x_in, x1_out, raw_in = ((s[n + "0"], s[n + "1"]) for n in ("x_in", "x1_out", "raw_in"))
        K_SPLIT, Q_SPLIT, V_SPLIT, O_SPLIT, XK_SPLIT, XQ_SPLIT, XV_SPLIT = 1, 1 + KC, 1 + 2 * KC, 2 + 2 * KC, 3 + 2 * KC, 4 + 2 * KC, 5 + 2 * KC

        def known(i, *values):
            return isinstance(i, int) and i in values

        def xb(i, j):
            return x[:, bass.ds((2 * i + j) * D, D)]

        block = scope.enter_context(nc.Block())

        @block.sync
        def _(sp):
            def load(i, j):
                at = bass.ds(held(sp, (2 * i + j) * D), D)
                if not isinstance(i, int):
                    sp.wait_ge(x_in[j], 16 * i)
                sp.dma_start(x[:, at], dram["x"][:, at]).then_inc(x_in[j], 16)

            def fly_load(i):
                at = bass.ds(held(sp, i * B), B)
                if not isinstance(i, int):
                    sp.wait_ge(s["fly_out"], 16 * i)
                sp.dma_start(fly[:, 0], dram["w2"][:, at, :]).then_inc(s["fly_in"], 16)

            def fly_store(i):
                at = bass.ds(held(sp, i * B), B)
                sp.wait_ge(s["fly_step"], 8 * i + 8)
                sp.dma_start(dram["w2_fly"][:, at, :], fly[:, 0]).then_inc(s["fly_out"], 16)

            def store(i, j):
                at, done = bass.ds(held(sp, (2 * i + j) * D), D), held(sp, 2 * i + j + 1)
                sp.wait_ge(s["x1_done"], done)
                if not isinstance(i, int):
                    sp.wait_ge(x1_out[j], 16 * i)
                sp.dma_start(dram["x1"][:, at], x[:, at]).then_inc(x1_out[j], 16)

            sp.dma_start(consts["ident"][:], dram["ident"]).then_inc(s["const_in"], 16)
            load(0, 0)
            load(0, 1)
            sp.dma_start(raw[0][:], dram["wk"]).then_inc(raw_in[0], 16)
            sp.wait_ge(s["zeroed"], 2)
            for g in range(HQ):
                r = slice(DH * g, DH * g + DH)
                sp.dma_start(down_bd[r, r], dram["wdown_t"]).then_inc(s["diag_in"], 16)
                sp.dma_start(up_bd[r, r], dram["wup"]).then_inc(s["diag_in"], 16)
            sp.dma_start(raw[1][:], dram["wq"]).then_inc(raw_in[1], 16)
            sp.wait_ge(s["w_lo_done"], K_SPLIT)
            sp.dma_start(raw[0][:], dram["wv"]).then_inc(raw_in[0], 16)
            load(1, 0)
            load(1, 1)
            sp.wait_ge(s["q_folded"], KC)
            sp.dma_start(raw[1][:], dram["wo"]).then_inc(raw_in[1], 16)
            fly_load(0)
            with sp.Fori(2, PAIRS) as i:
                for j in range(2):
                    load(i, j)
            sp.wait_ge(s["v_folded"], KC)
            sp.dma_start(raw[0][:], dram["xk"]).then_inc(raw_in[0], 16)
            sp.wait_ge(s["w_lo_done"], O_SPLIT)
            sp.dma_start(raw[1][:], dram["xq"]).then_inc(raw_in[1], 16)
            fly_store(0)
            fly_load(1)
            store(0, 0)
            store(0, 1)
            with sp.Fori(2, PAIRS) as i:
                fly_store(i - 1)
                fly_load(i)
                for j in range(2):
                    store(i - 1, j)
            sp.wait_ge(s["w_lo_done"], XK_SPLIT)
            sp.dma_start(raw[0][:], dram["xv"]).then_inc(raw_in[0], 16)
            sp.wait_ge(s["w_lo_done"], XQ_SPLIT)
            sp.dma_start(raw[1][:], dram["xo"]).then_inc(c["xo_in"], 16)
            fly_store(PAIRS - 1)
            sp.wait_ge(s["w_lo_done"], XV_SPLIT)
            sp.dma_start(raw[0][:, :, 0:S], dram["ctx"][:, 0:KC * S].rearrange("p (c s) -> p c s", c=KC)).then_inc(c["c_in"], 16)
            for j in range(2):
                store(PAIRS - 1, j)
            sp.wait_ge(s["fly_out"], 16 * PAIRS)
            for j in range(2):
                sp.wait_ge(x1_out[j], 16 * PAIRS)

        @block.gpsimd
        def _(pool):
            def layernorm(i):
                for j in range(2):
                    pool.wait_ge(s["aggr_done"], 2 * i + j + 1)
                    pool.tensor_tensor(veps[:, j], mv[:, j, 1:2], consts["eps"][0:T], ALU.add).then_inc(s["veps_done"], 1)
                    pool.wait_ge(s["veps_done"], 2 * i + j + 1)
                    pool.tensor_tensor(rstd[:, j], veps[:, j], consts["minus_half"][0:T], ALU.pow).then_inc(s["rstd_done"], 1)

            def normalise(i, u):
                pool.wait_ge(s["rtotal_done"], 4 * i + u + 1)
                pool.tensor_tensor(e[:, u % 2], e[:, u % 2],
                                   rtotal[:, u % 2].unsqueeze(2).to_broadcast([T, 8, T]), ALU.mult).then_inc(s["norm_done"], 1)

            def fly_stage(i, n):
                a, b = n % 2, (n + 1) % 2
                st = 1 << n
                src = fly[:, a].rearrange("p (g two s) c -> p two g s c", two=2, s=st)
                dst = fly[:, b].rearrange("p (g two s) c -> p two g s c", two=2, s=st)
                if n == 0:
                    pool.wait_ge(s["fly_in"], 16 * i + 16)
                else:
                    pool.wait_ge(s["fly_step"], 8 * i + 2 * n)
                pool.tensor_tensor(dst[:, 0], src[:, 0], src[:, 1], ALU.add).then_inc(s["fly_step"], 1)
                pool.tensor_tensor(dst[:, 1], src[:, 0], src[:, 1], ALU.subtract).then_inc(s["fly_step"], 1)

            def step(i, last):
                for u in range(UNITS):
                    normalise(i, u)
                    if u == 2 and not last:
                        layernorm(i + 2)
                    for n in FLY_STAGES[u]:
                        fly_stage(i, n)

            pool.memset(down_bd[:], 0.0).then_inc(s["zeroed"], 1)
            pool.memset(up_bd[:], 0.0).then_inc(s["zeroed"], 1)
            pool.memset(consts["eps"][:], EPS).then_inc(s["zeroed"], 1)
            pool.memset(consts["minus_half"][:], -0.5).then_inc(s["zeroed"], 1)
            pool.wait_ge(s["zeroed"], 4)
            layernorm(0)
            for n in range(2):
                pool.memset(f32(kbd[n][:]), 0.0).then_inc(s["kbd_zeroed"], 1)
            layernorm(1)
            with pool.Fori(0, PAIRS - 2) as i:
                step(i, False)
            step(PAIRS - 2, True)
            step(PAIRS - 1, True)

        @block.tensor
        def _(pe):
            def transpose_x(i, j):
                pe.wait_ge(s["xn_done"], 2 * i + j + 1)
                if not known(i, 0):
                    if j == 1:
                        pe.wait_ge(s["v_done"], 2 * i)
                    elif not known(i, 1):
                        pe.wait_ge(s["x1_done"], 2 * i - 2)
                    else:
                        pe.wait_ge(s["q_lo_done"], 2 * i - 1)
                for c in range(KC):
                    last = pe.transpose(gen[1 - j][:, c * T:(c + 1) * T], xn[:, j, c * P:(c + 1) * P],
                                        consts["ident"][0:T, 0:T])
                last.then_inc(s["xt_ready"], 1)

            def project(i, name, weights, half):
                if name == "q":
                    pe.wait_ge(s["k_lo_done"], 2 * i + half + 1)
                elif half == 0:
                    pe.wait_ge(s["xt_lo_done"], 2 * i + 2)
                for o in range(2):
                    mt = 2 * half + o
                    for c in range(KC):
                        last = three_pass(pe, gen[1 - half][:, o * PT:(o + 1) * PT],
                                          weights[0][:, c, mt * P:(mt + 1) * P], weights[1][:, c, mt * P:(mt + 1) * P],
                                          xt[0][:, c], xt[1][:, c], c == 0, c == KC - 1)
                last.then_inc(s[name + "_ready"], 1)

            def project_v(i, j):
                pe.wait_ge(s["q_lo_done"], 2 * i + 2) if j == 0 else pe.wait_ge(s["v_done"], 2 * i + 1)
                for c in range(KC):
                    last = three_pass(pe, gen[0][0:T, :], xt[0][:, c, j * T:(j + 1) * T], xt[1][:, c, j * T:(j + 1) * T],
                                      w["v"][0][:, c], w["v"][1][:, c], c == 0, c == KC - 1)
                last.then_inc(s["v_ready"], 1)

            def scores(i, u):
                j, b = u // 2, u % 2
                if b == 0:
                    pe.wait_ge(s["kbd_done"], 4 * i + 2 * j + 2)
                if j == 0:
                    pe.wait_ge(s["q_lo_done"], 2 * i + u + 1)
                if not (isinstance(i, int) and i == 0 and u < 2):
                    pe.wait_ge(s["pt_done"], 4 * i + u - 1)
                for n in range(2):
                    mt = 2 * b + n
                    last = three_pass(pe, sc[0:T, 2 * b + n, 0:QT],
                                      q[0][:, mt, j * T:(j + 1) * T], q[1][:, mt, j * T:(j + 1) * T],
                                      kbd[0][:, mt, j].rearrange("p h t -> p (h t)"),
                                      kbd[1][:, mt, j].rearrange("p h t -> p (h t)"), True, True)
                last.then_inc(s["sc_done"], 1)

            def transpose_p(i, u):
                b = u % 2
                pe.wait_ge(s["norm_done"], 4 * i + u + 1)
                for h in range(8):
                    last = pe.transpose(sc[0:T, 2 * b + h // 4, (h % 4) * T:(h % 4 + 1) * T], e[:, b, h],
                                        consts["ident"][0:T, 0:T])
                last.then_inc(s["pt_ready"], 1)

            def attend(i, u):
                j, b = u // 2, u % 2
                pe.wait_ge(s["pt_done"], 4 * i + u + 1)
                pe.wait_ge(s["v_done"], 2 * i + j + 1)
                if not (isinstance(i, int) and i == 0 and u < 2):
                    pe.wait_ge(s["ot_lo_done"], 4 * i + u - 1)
                for n in range(2):
                    for h in range(HQ):
                        head = (2 * b + n) * HQ + h
                        last = pe.matmul(av[DH * h:DH * (h + 1), b, n * T:(n + 1) * T],
                                         v[:, j, head * DH:(head + 1) * DH], pt[:, b, n * HQ + h],
                                         start=True, stop=True)
                last.then_inc(s["av_done"], 1)

            def output(i, j):
                pe.wait_ge(s["ot_lo_done"], 4 * i + 2 * j + 2)
                if j == 1 or known(i, PAIRS - 1):
                    pe.wait_ge(s["x1_done"], 2 * i + j)
                else:
                    pe.wait_ge(s["q_lo_done"], 2 * i + 3)
                for c in range(KC):
                    last = three_pass(pe, gen[1][0:T, :], ot[0][:, j, c], ot[1][:, j, c], w["o"][0][:, c], w["o"][1][:, c],
                                      c == 0, c == KC - 1)
                last.then_inc(s["y_ready"], 1)

            def step(i, more):
                first = known(i, 0)
                scores(i, 0)
                if known(i, 1):
                    pe.wait_ge(s["w_lo_done"], O_SPLIT)
                if not first:
                    output(i - 1, 0)
                    transpose_p(i - 1, 3)
                project_v(i, 0)
                if not first:
                    attend(i - 1, 3)
                scores(i, 1)
                if not first:
                    output(i - 1, 1)
                transpose_p(i, 0)
                project_v(i, 1)
                if more:
                    transpose_x(i + 1, 0)
                attend(i, 0)
                if more:
                    transpose_x(i + 1, 1)
                scores(i, 2)
                transpose_p(i, 1)
                if more:
                    project(i + 1, "k", w["k"], 0)
                attend(i, 1)
                if more:
                    project(i + 1, "k", w["k"], 1)
                scores(i, 3)
                if more:
                    project(i + 1, "q", w["q"], 0)
                transpose_p(i, 2)
                if more:
                    project(i + 1, "q", w["q"], 1)
                attend(i, 2)

            def fold(nat, mat, arrived, done):
                pe.wait_ge(*arrived)
                for c in range(KC):
                    for o in range(KC):
                        last = pe.matmul(sc[:, c, o * P:(o + 1) * P], nat[:, o, c * P:(c + 1) * P], mat[:], start=True, stop=True)
                    last.then_inc(done, 1)

            pe.wait_ge(s["const_in"], 16)
            for j in range(2):
                transpose_x(0, j)
            pe.wait_ge(s["diag_in"], 16 * 2 * HQ)
            pe.matmul(av[:, 0, 0:P], down_bd[:], down_bd[:], start=True, stop=True)
            pe.matmul(av[:, 1, 0:P], down_bd[:], up_bd[:], start=True, stop=True).then_inc(s["folds_done"], 1)
            pe.wait_ge(s["folds_copied"], 2)
            fold(raw[1], fold_q, (raw_in[1], 16), s["q_folded"])
            pe.wait_ge(s["w_lo_done"], K_SPLIT)
            for half in range(2):
                project(0, "k", w["k"], half)
            pe.wait_ge(s["w_lo_done"], Q_SPLIT)
            fold(raw[0], fold_v, (raw_in[0], 32), s["v_folded"])
            for half in range(2):
                project(0, "q", w["q"], half)
            pe.wait_ge(s["w_lo_done"], V_SPLIT)
            step(0, True)
            step(1, True)
            with pe.Fori(2, PAIRS - 1) as i:
                step(i, True)
            step(PAIRS - 1, False)
            output(PAIRS - 1, 0)
            transpose_p(PAIRS - 1, 3)
            attend(PAIRS - 1, 3)
            output(PAIRS - 1, 1)

        @block.scalar
        def _(act):
            def pt_copy(i, u):
                b = u % 2
                act.wait_ge(s["pt_ready"], 4 * i + u + 1)
                if not (isinstance(i, int) and i == 0 and u < 2):
                    act.wait_ge(s["av_done"], 4 * i + u - 1)
                act.activation(pt[:, b].rearrange("t (n h) q -> t n (h q)", n=2), sc[0:T, 2 * b:2 * b + 2, 0:QT],
                               ACT.Copy).then_inc(s["pt_done"], 1)

            def ot_hi(i, u):
                j, b = u // 2, u % 2
                act.wait_ge(s["av_done"], 4 * i + u + 1)
                if not (isinstance(i, int) and i == 0):
                    act.wait_ge(s["y_ready"], 2 * i + j - 1)
                act.activation(ot[0][:, j, 2 * b:2 * b + 2], av[:, b, 0:2 * T].rearrange("p (n t) -> p n t", n=2),
                               ACT.Copy).then_inc(s["ot_hi_done"], 1)

            def exp(i, u, n):
                b = u % 2
                if n == 0:
                    act.wait_ge(s["bias_done"], 4 * i + u + 1)
                    if not (known(i, 0) and u < 2):
                        act.wait_ge(s["pt_ready"], 4 * i + u - 1)
                for h in range(HQ):
                    head = n * HQ + h
                    last = act.activation(e[:, b, head], sc[0:T, 2 * b + n, h * T:(h + 1) * T], ACT.Exp, bias=bias[:, b, head:head + 1],
                                          scale=SCALE, accum_out=total[:, b, head:head + 1])
                last.then_inc(s["exp_done"], 1)

            def x_hi(i, j):
                act.wait_ge(s["xt_ready"], 2 * i + j + 1)
                if not known(i, 0):
                    act.wait_ge(s["v_ready"], 2 * i + j - 1)
                act.activation(xt[0][:, :, j * T:(j + 1) * T], gen[1 - j][:, 0:QT].rearrange("p (c t) -> p c t", c=KC),
                               ACT.Copy).then_inc(s["xt_hi_done"], 1)

            def hi(i, name, dst, half):
                act.wait_ge(s[name + "_ready"], 2 * i + half + 1)
                if not known(i, 0):
                    act.wait_ge(s["kbd_done"], 4 * i) if name == "k" else act.wait_ge(s["sc_done"], 4 * i)
                act.activation(dst[0][:, 2 * half:2 * half + 2], gen[1 - half][:, 0:2 * PT].rearrange("p (o t) -> p o t", o=2),
                               ACT.Copy).then_inc(s[name + "_hi_done"], 1)

            def split_hi(name, b, loads):
                act.wait_ge(raw_in[b], 16 * loads)
                act.activation(w[name][0][:], raw[b][:], ACT.Copy).then_inc(s["w_hi_done"], 1)

            def folded_hi(name, done):
                for c in range(KC):
                    act.wait_ge(done, c + 1)
                    act.activation(w[name][0][:, c], sc[:, c], ACT.Copy).then_inc(s["w_hi_done"], 1)

            def step(i, more):
                first = known(i, 0)
                if not first:
                    ot_hi(i - 1, 2)
                exp(i, 0, 0)
                exp(i, 0, 1)
                if not more:
                    split_hi("k", 0, 3)
                    split_hi("q", 1, 3)
                if not first:
                    pt_copy(i - 1, 3)
                    ot_hi(i - 1, 3)
                exp(i, 1, 0)
                exp(i, 1, 1)
                pt_copy(i, 0)
                if first:
                    split_hi("o", 1, 2)
                if not more:
                    act.wait_ge(s["v_ready"], 2 * PAIRS)
                    split_hi("v", 0, 4)
                if more:
                    x_hi(i + 1, 0)
                    x_hi(i + 1, 1)
                ot_hi(i, 0)
                pt_copy(i, 1)
                exp(i, 2, 0)
                exp(i, 2, 1)
                if more:
                    hi(i + 1, "k", k, 0)
                ot_hi(i, 1)
                if more:
                    hi(i + 1, "k", k, 1)
                exp(i, 3, 0)
                if more:
                    hi(i + 1, "q", q, 0)
                exp(i, 3, 1)
                pt_copy(i, 2)
                if more:
                    hi(i + 1, "q", q, 1)

            for j in range(2):
                x_hi(0, j)
            split_hi("k", 0, 1)
            folded_hi("q", s["q_folded"])
            for half in range(2):
                hi(0, "k", k, half)
            folded_hi("v", s["v_folded"])
            for half in range(2):
                hi(0, "q", q, half)
            step(0, True)
            with act.Fori(1, PAIRS - 1) as i:
                step(i, True)
            step(PAIRS - 1, False)
            ot_hi(PAIRS - 1, 2)
            pt_copy(PAIRS - 1, 3)
            ot_hi(PAIRS - 1, 3)

        @block.vector
        def _(dve):
            def layernorm_stats(i):
                for j in range(2):
                    dve.wait_ge(x_in[j], 16 * i + 16)
                    dve.bn_stats(st[:, j], xb(i, j)).then_inc(s["stats_done"], 1)
                dve.wait_ge(s["stats_done"], 2 * i + 2)
                if not (isinstance(i, int) and i == 0):
                    dve.wait_ge(s["xn_done"], 2 * i)
                carry_waits(dve, fence[:])
                for j in range(2):
                    dve.bn_aggr(mv[:, j], st[:, j]).then_inc(s["aggr_done"], 1)

            def layernorm_apply(i, j):
                dve.wait_ge(s["rstd_done"], 2 * i + j + 1)
                if not (isinstance(i, int) and i == 0):
                    dve.wait_ge(s["xt_ready"], 2 * i + j - 1)
                dve.tensor_scalar(xn[:, j], xb(i, j), mv[:, j, 0:1], rstd[:, j], ALU.subtract, ALU.mult)\
                   .then_inc(s["xn_done"], 1)

            def x_lo(i, j):
                dve.wait_ge(s["xt_hi_done"], 2 * i + j + 1)
                dve.tensor_tensor(xt[1][:, :, j * T:(j + 1) * T], gen[1 - j][:, 0:QT].rearrange("p (c t) -> p c t", c=KC),
                                  f32(xt[0][:, :, j * T:(j + 1) * T]), ALU.subtract).then_inc(s["xt_lo_done"], 1)

            def lo(i, name, dst, half):
                dve.wait_ge(s[name + "_hi_done"], 2 * i + half + 1)
                dve.tensor_tensor(dst[1][:, 2 * half:2 * half + 2], gen[1 - half][:, 0:2 * PT].rearrange("p (o t) -> p o t", o=2),
                                  f32(dst[0][:, 2 * half:2 * half + 2]), ALU.subtract).then_inc(s[name + "_lo_done"], 1)

            def place_k(i, j, part):
                if part == 0:
                    dve.wait_ge(s["k_lo_done"], 2 * i + 2)
                    if not known(i, 0):
                        dve.wait_ge(s["sc_done"], 4 * i - 2 + 2 * j)
                for h in range(HQ):
                    r = slice(DH * h, DH * (h + 1))
                    end = dve.tensor_copy(kbd[part][r, :, j, h], k[part][r, :, j * T:(j + 1) * T])
                end.then_inc(s["kbd_done"], 1)

            def maximum(i, u):
                b = u % 2
                src = sc[0:T, 2 * b:2 * b + 2, 0:QT].rearrange("t n (h k) -> t n h k", h=HQ)
                dve.wait_ge(s["sc_done"], 4 * i + u + 1)
                dve.reduce_max(mx[:, b].rearrange("t (n h) -> t n h", n=2), src, AX_X).then_inc(s["mx_done"], 1)
                dve.wait_ge(s["mx_done"], 4 * i + u + 1)
                if not (known(i, 0) and u < 2):
                    dve.wait_ge(s["exp_done"], 8 * i + 2 * u - 2)
                dve.tensor_scalar(bias[:, b], mx[:, b], -SCALE, None, ALU.mult).then_inc(s["bias_done"], 1)

            def invert_total(i, u):
                dve.wait_ge(s["exp_done"], 8 * i + 2 * u + 2)
                if not (known(i, 0) and u < 2):
                    dve.wait_ge(s["norm_done"], 4 * i + u - 1)
                dve.reciprocal(rtotal[:, u % 2], total[:, u % 2]).then_inc(s["rtotal_done"], 1)

            def v_copy(i, j):
                dve.wait_ge(s["v_ready"], 2 * i + j + 1)
                if not known(i, 0):
                    dve.wait_ge(s["av_done"], 4 * i - 2 + 2 * j)
                dve.tensor_copy(v[:, j], gen[0][0:T, :]).then_inc(s["v_done"], 1)

            def ot_lo(i, u):
                j, b = u // 2, u % 2
                dve.wait_ge(s["ot_hi_done"], 4 * i + u + 1)
                dve.tensor_tensor(ot[1][:, j, 2 * b:2 * b + 2], av[:, b, 0:2 * T].rearrange("p (n t) -> p n t", n=2),
                                  f32(ot[0][:, j, 2 * b:2 * b + 2]), ALU.subtract).then_inc(s["ot_lo_done"], 1)

            def add_x(i, j):
                dve.wait_ge(s["y_ready"], 2 * i + j + 1)
                dve.tensor_tensor(xb(i, j), gen[1][0:T, :], xb(i, j), ALU.add).then_inc(s["x1_done"], 1)

            def split_lo(name, b, count):
                dve.wait_ge(s["w_hi_done"], count)
                dve.tensor_tensor(w[name][1][:], raw[b][:], f32(w[name][0][:]), ALU.subtract).then_inc(s["w_lo_done"], 1)

            def folded_lo(name, count):
                for c in range(KC):
                    dve.wait_ge(s["w_hi_done"], count - KC + c + 1)
                    dve.tensor_tensor(w[name][1][:, c], sc[:, c], f32(w[name][0][:, c]), ALU.subtract).then_inc(s["w_lo_done"], 1)

            def step(i, more, more_stats):
                first = known(i, 0)
                maximum(i, 0)
                if not first:
                    ot_lo(i - 1, 2)
                place_k(i, 1, 0)
                if not first:
                    add_x(i - 1, 0)
                place_k(i, 1, 1)
                invert_total(i, 0)
                if more:
                    layernorm_apply(i + 1, 0)
                v_copy(i, 0)
                if not first:
                    ot_lo(i - 1, 3)
                maximum(i, 1)
                if not more:
                    split_lo("k", 0, XK_SPLIT)
                    split_lo("q", 1, XQ_SPLIT)
                if more:
                    layernorm_apply(i + 1, 1)
                if not first:
                    add_x(i - 1, 1)
                invert_total(i, 1)
                v_copy(i, 1)
                if more:
                    x_lo(i + 1, 0)
                    x_lo(i + 1, 1)
                ot_lo(i, 0)
                maximum(i, 2)
                if first:
                    split_lo("o", 1, O_SPLIT)
                if not more:
                    split_lo("v", 0, XV_SPLIT)
                if more_stats:
                    layernorm_stats(i + 2)
                invert_total(i, 2)
                if more:
                    lo(i + 1, "k", k, 0)
                ot_lo(i, 1)
                if more:
                    lo(i + 1, "k", k, 1)
                maximum(i, 3)
                if more:
                    place_k(i + 1, 0, 0)
                    place_k(i + 1, 0, 1)
                    lo(i + 1, "q", q, 0)
                invert_total(i, 3)
                if more:
                    lo(i + 1, "q", q, 1)

            layernorm_stats(0)
            for j in range(2):
                layernorm_apply(0, j)
            for j in range(2):
                x_lo(0, j)
            dve.wait_ge(s["folds_done"], 1)
            dve.tensor_copy(fold_q[:], av[:, 0, 0:P]).then_inc(s["folds_copied"], 1)
            dve.tensor_copy(fold_v[:], av[:, 1, 0:P]).then_inc(s["folds_copied"], 1)
            split_lo("k", 0, K_SPLIT)
            folded_lo("q", Q_SPLIT)
            for half in range(2):
                lo(0, "k", k, half)
            dve.wait_ge(s["kbd_zeroed"], 2)
            place_k(0, 0, 0)
            place_k(0, 0, 1)
            folded_lo("v", V_SPLIT)
            for half in range(2):
                lo(0, "q", q, half)
            layernorm_stats(1)
            step(0, True, True)
            with dve.Fori(1, PAIRS - 2) as i:
                step(i, True, True)
            step(PAIRS - 2, True, False)
            step(PAIRS - 1, False, False)
            ot_lo(PAIRS - 1, 2)
            add_x(PAIRS - 1, 0)
            ot_lo(PAIRS - 1, 3)
            add_x(PAIRS - 1, 1)


def build_cross(nc, dram, w, raw, c, sems):
    with ExitStack() as scope:
        m = Memory(nc, scope)
        xa = m.sb("xa", [T, 2, D])
        xr = m.sb("xr", [T, 2, D])
        fence = m.sb("fence_f2", [1, 1])
        st = m.sb("st2", [T, 2, 6])
        mv = m.sb("mv2", [T, 2, 2])
        veps = m.sb("veps2", [T, 2, 1])
        rstd = m.sb("rstd2", [T, 2, 1])
        xn = m.sb("xn2", [T, 2, D])
        xt = [m.sb(f"xt2_{n}", [P, KC, PT], F32R) for n in ("hi", "lo")]
        q = [m.sb(f"q2_{n}", [P, KC, PT], F32R) for n in ("hi", "lo")]
        qbd = [m.sb(f"qbd_{n}", [P, KC, HQ, T], F32R) for n in ("hi", "lo")]
        ctx = [m.sb(f"ctx_{n}", [P, KC, SE], F32R) for n in ("hi", "lo")]
        craw = raw[0][:, :, 0:S]
        k = [[m.sb(f"k2_{n}{j}", [P, KC, SE], F32R) for n in ("hi", "lo")] for j in range(2)]
        v = m.sb("v2", [KP, 2, KT, D])
        e = m.sb("e2", [KP, 2, KT, QT])
        esum = m.sb("esum", [KP, 2, QT])
        rz = m.sb("rz", [P, T])
        rzx = m.sb("rzx", [P, QT])
        on = m.sb("on", [P, QT])
        ot = [m.sb(f"ot2_{n}", [P, KC, T], F32R) for n in ("hi", "lo")]
        y = m.sb("y", [T, D])
        yst = m.sb("yst", [T, 6])
        ymv = m.sb("ymv", [T, 2])
        ysc = m.sb("ysc", [T, 4])
        bv = m.sb("bv", [P, KC])
        bv_wide = m.sb("bv_wide", [P, KC, P])
        bo = m.sb("bo", [P, D])
        mask = m.sb("mask", [KP, B * KT], I32)
        maskf = m.sb("maskf", [KP, B * KT])
        for name, shape in (("bq", [P, KC]), ("bk", [P, KC]), ("bo_full", [P, D]), ("gamma", [P, D]), ("beta", [P, D]),
                            ("rs", [P, 1]), ("rs2", [P, 1]), ("bound", [KP, B * KT]), ("sel", [P, KC, DH]), ("spread", [P, KC, P])):
            c[name] = m.sb(name, shape)
        gen = [m.ps(f"gen2_{n}", [P, 512]) for n in range(2)]
        sc = m.ps("sc2", [P, 4, 512])
        av = m.ps("av2", [P, 512])
        z = m.ps("z2", [P, 512])

        names = ("xa_in xr_in0 xr_in1 x2_out0 x2_out1 stats_done aggr_done veps_done rstd_done xn_done xt_ready "
                 "xt_hi_done xt_lo_done q_ready q_hi_done q_lo_done qbd_hi_done qbd_lo_done c_hi_done c_lo_done "
                 "k_ready k_hi_done k_lo_done v_ready v_done sc_done clip_done exp_done esum_step av_done z_done "
                 "rz_done zx_ready rzx_done on_done ot_hi_done ot_lo_done y_ready y_done yst_done ymv_done ysc_step "
                 "d_done x2_step small_in wide_done bias_ready bias_added setup mask_step rs_step xo_hi_done xo_lo_done").split()
        s = {n: sems.sem("c_" + n) for n in names}
        s["c_in"], s["xo_in"] = c["c_in"], c["xo_in"]
        xr_in, x2_out = (s["xr_in0"], s["xr_in1"]), (s["x2_out0"], s["x2_out1"])
        LASTB = B - 1

        def known(i, *values):
            return isinstance(i, int) and i in values

        block = scope.enter_context(nc.Block())

        @block.sync
        def _(sp):
            def context(n):
                at = bass.ds(held(sp, n * KC * S), KC * S)
                if not known(n, 0):
                    sp.wait_ge(s["c_lo_done"], 2 * n)
                sp.dma_start(craw, dram["ctx"][:, at].rearrange("p (c s) -> p c s", c=KC)).then_inc(s["c_in"], 16)

            def pair(i):
                at = bass.ds(held(sp, i * 2 * D), 2 * D)
                if not known(i, 0):
                    sp.wait_ge(s["xn_done"], 2 * i)
                sp.dma_start(xa[:].rearrange("t j d -> t (j d)"), dram["x1"][:, at]).then_inc(s["xa_in"], 16)

            def residual(i, j):
                at = bass.ds(held(sp, (2 * i + j) * D), D)
                if not known(i, 0):
                    sp.wait_ge(x2_out[j], 16 * i)
                sp.dma_start(xr[:, j], dram["x1"][:, at]).then_inc(xr_in[j], 16)

            def store(i, j):
                at = bass.ds(held(sp, (2 * i + j) * T), T)
                sp.wait_ge(s["x2_step"], 3 * (2 * i + j) + 3)
                sp.dma_start(dram["x2"][at, :], xr[:, j]).then_inc(x2_out[j], 16)

            def step(i, first, more, more_pairs):
                if not first:
                    store(i - 1, 1)
                    residual(i, 1)
                if more:
                    context(2 * i + 3)
                if more_pairs:
                    pair(i + 2)
                store(i, 0)
                if more:
                    residual(i + 1, 0)
                if more_pairs:
                    context(2 * i + 4)

            pair(0)
            for dst, src in ((bv[:], dram["bv"]), (c["bk"][:], dram["bk"]), (c["bq"][:], dram["bq"]),
                             (bo[:], dram["bo"].to_broadcast([P, D])), (mask[:], dram["mask"]),
                             (c["sel"][:], dram["sel"]), (c["spread"][:], dram["spread"]),
                             (c["rs"][:], dram["rs"].to_broadcast([P, 1])), (c["gamma"][:], dram["gamma"].to_broadcast([P, D])),
                             (c["beta"][:], dram["beta"].to_broadcast([P, D]))):
                sp.dma_start(dst, src).then_inc(s["small_in"], 16)
            context(1)
            pair(1)
            residual(0, 0)
            residual(0, 1)
            context(2)
            step(0, True, True, True)
            with sp.Fori(1, PAIRS - 2) as i:
                step(i, False, True, True)
            step(PAIRS - 2, False, True, False)
            step(PAIRS - 1, False, False, False)
            store(PAIRS - 1, 1)
            for j in range(2):
                sp.wait_ge(x2_out[j], 16 * PAIRS)

        @block.gpsimd
        def _(pool):
            def layernorm(i):
                for j in range(2):
                    pool.wait_ge(s["aggr_done"], 2 * i + j + 1)
                    pool.tensor_tensor(veps[:, j], mv[:, j, 1:2], c["eps"][0:T], ALU.add).then_inc(s["veps_done"], 1)
                    pool.wait_ge(s["veps_done"], 2 * i + j + 1)
                    pool.tensor_tensor(rstd[:, j], veps[:, j], c["minus_half"][0:T], ALU.pow).then_inc(s["rstd_done"], 1)

            def sum_tiles(n, u):
                pool.wait_ge(s["exp_done"], 4 * n + u + 1)
                if not (known(n, 0) and u < 2):
                    pool.wait_ge(s["z_done"], 4 * n + u - 1)
                pool.tensor_tensor(esum[:, u % 2], e[:, u % 2, 0], e[:, u % 2, 1], ALU.add).then_inc(s["esum_step"], 1)
                pool.wait_ge(s["esum_step"], 8 * n + 2 * u + 1)
                pool.tensor_tensor(esum[:, u % 2], esum[:, u % 2], e[:, u % 2, 2], ALU.add).then_inc(s["esum_step"], 1)

            def tail_scale(n):
                pool.wait_ge(s["ymv_done"], n + 1)
                for step, (a, b, op) in enumerate(((ymv[:, 1:2], c["rs2"][0:T], ALU.mult), (ysc[:, 0:1], c["eps"][0:T], ALU.add),
                                                   (ysc[:, 1:2], c["minus_half"][0:T], ALU.pow), (ysc[:, 2:3], c["rs"][0:T], ALU.mult))):
                    if step:
                        pool.wait_ge(s["ysc_step"], 4 * n + step)
                    pool.tensor_tensor(ysc[:, step:step + 1], a, b, op).then_inc(s["ysc_step"], 1)

            def tail(i, j):
                n = 2 * i + j
                pool.wait_ge(s["d_done"], n + 1)
                pool.tensor_tensor(y[:], y[:], c["gamma"][0:T], ALU.mult).then_inc(s["x2_step"], 1)
                pool.wait_ge(s["x2_step"], 3 * n + 1)
                pool.tensor_tensor(y[:], y[:], c["beta"][0:T], ALU.add).then_inc(s["x2_step"], 1)
                pool.wait_ge(s["x2_step"], 3 * n + 2)
                pool.wait_ge(xr_in[j], 16 * i + 16)
                pool.tensor_tensor(xr[:, j], xr[:, j], y[:], ALU.add).then_inc(s["x2_step"], 1)

            def step(i, j, last_pair):
                n = 2 * i + j
                sum_tiles(n, 0)
                sum_tiles(n, 1)
                if not known(n, 0):
                    tail_scale(n - 1)
                if j == 0 and not last_pair:
                    layernorm(i + 1)
                sum_tiles(n, 2)
                if not known(n, 0):
                    tail(i - 1, 1) if j == 0 else tail(i, 0)
                sum_tiles(n, 3)

            for n in range(2):
                pool.memset(f32(ctx[n][:, :, S:SE]), 0.0).then_inc(s["setup"], 1)
            pool.wait_ge(s["small_in"], 160)
            pool.tensor_copy(bv_wide[:], bv[:].unsqueeze(2).to_broadcast([P, KC, P])).then_inc(s["wide_done"], 1)
            layernorm(0)
            for n in range(2):
                pool.memset(f32(qbd[n][:]), 0.0).then_inc(s["setup"], 1)
            step(0, 0, False)
            step(0, 1, False)
            with pool.Fori(1, PAIRS - 1) as i:
                step(i, 0, False)
                step(i, 1, False)
            step(PAIRS - 1, 0, True)
            step(PAIRS - 1, 1, True)
            tail_scale(LASTB)
            tail(PAIRS - 1, 1)

        @block.tensor
        def _(pe):
            def project_k(n, slot, mt, g):
                for kc in range(KC):
                    if mt == 0 and kc % 2 == 0:
                        pe.wait_ge(s["c_lo_done"], 2 * n + kc // 2 + 1)
                    last = three_pass(pe, gen[g][:, 0:SE], w["k"][0][:, kc, mt * P:(mt + 1) * P], w["k"][1][:, kc, mt * P:(mt + 1) * P],
                                      ctx[0][:, kc], ctx[1][:, kc], kc == 0, kc == KC - 1)
                last.then_inc(s["k_ready"], 1)

            def project_v(n, kt, g):
                for kc in range(KC):
                    last = three_pass(pe, gen[g][0:KP, :], ctx[0][:, kc, kt * KP:(kt + 1) * KP], ctx[1][:, kc, kt * KP:(kt + 1) * KP],
                                      w["v"][0][:, kc], w["v"][1][:, kc], kc == 0, kc == KC - 1)
                last.then_inc(s["v_ready"], 1)

            def transpose_x(i, j):
                pe.wait_ge(s["xn_done"], 2 * i + j + 1)
                for kc in range(KC):
                    last = pe.transpose(gen[j][:, kc * T:(kc + 1) * T], xn[:, j, kc * P:(kc + 1) * P], c["ident"][0:T, 0:T])
                last.then_inc(s["xt_ready"], 1)

            def project_q(i, half, g):
                if half == 0:
                    pe.wait_ge(s["xt_lo_done"], 2 * i + 2)
                for o in range(2):
                    mt = 2 * half + o
                    for kc in range(KC):
                        last = three_pass(pe, gen[g][:, o * PT:(o + 1) * PT], w["q"][0][:, kc, mt * P:(mt + 1) * P],
                                          w["q"][1][:, kc, mt * P:(mt + 1) * P], xt[0][:, kc], xt[1][:, kc], kc == 0, kc == KC - 1)
                last.then_inc(s["q_ready"], 1)

            def scores(n, j, u):
                if u == 0:
                    pe.wait_ge(s["qbd_hi_done"], n + 1)
                    pe.wait_ge(s["qbd_lo_done"], n + 1)
                for kt in range(KT):
                    r = KT * u + kt
                    if not (known(n, 0) and r < 4):
                        pe.wait_ge(s["clip_done"], 12 * n + r - 3)
                    last = three_pass(pe, sc[0:KP, r % 4, 0:QT], k[j][0][:, u, kt * KP:(kt + 1) * KP], k[j][1][:, u, kt * KP:(kt + 1) * KP],
                                      qbd[0][:, u].rearrange("p h t -> p (h t)"), qbd[1][:, u].rearrange("p h t -> p (h t)"), True, True)
                    last.then_inc(s["sc_done"], 1)

            def attend(n, j, u):
                pe.wait_ge(s["exp_done"], 4 * n + u + 1)
                if u == 0:
                    pe.wait_ge(s["v_done"], 3 * n + 3)
                    if not known(n, 0):
                        pe.wait_ge(s["on_done"], n)
                for kt in range(KT):
                    for h in range(HQ):
                        head = u * HQ + h
                        last = pe.matmul(av[DH * h:DH * (h + 1), u * T:(u + 1) * T], v[:, j, kt, head * DH:(head + 1) * DH],
                                         e[:, u % 2, kt, h * T:(h + 1) * T], start=(kt == 0), stop=(kt == KT - 1))
                last.then_inc(s["av_done"], 1)

            def sums(n, u):
                pe.wait_ge(s["esum_step"], 8 * n + 2 * u + 2)
                if u == 0 and not known(n, 0):
                    pe.wait_ge(s["rzx_done"], n)
                for h in range(HQ):
                    last = pe.matmul(z[DH * h:DH * (h + 1), 0:T], c["sel"][0:KP, u], esum[:, u % 2, h * T:(h + 1) * T],
                                     start=(u == 0), stop=(u == HQ - 1))
                last.then_inc(s["z_done"], 1)

            def spread(n):
                pe.wait_ge(s["rz_done"], n + 1)
                for u in range(KC):
                    last = pe.matmul(z[:, u * T:(u + 1) * T], c["spread"][:, u], rz[:], start=True, stop=True)
                last.then_inc(s["zx_ready"], 1)

            def output(n, g):
                pe.wait_ge(s["ot_lo_done"], n + 1)
                for kc in range(KC):
                    last = three_pass(pe, gen[g][0:T, :], ot[0][:, kc], ot[1][:, kc], w["o"][0][:, kc], w["o"][1][:, kc],
                                      kc == 0, kc == KC - 1)
                last.then_inc(s["y_ready"], 1)

            def step(i, j, more, more_pairs):
                n = 2 * i + j
                extra = j == 1 and more_pairs
                scores(n, j, 0)
                if not known(n, 0):
                    spread(n - 1)
                scores(n, j, 1)
                if more:
                    pe.wait_ge(s["v_done"], 3 * n + 2)
                    project_k(n + 1, 1 - j, 0, 1)
                    pe.wait_ge(s["v_done"], 3 * n + 3)
                    project_k(n + 1, 1 - j, 1, 0)
                attend(n, j, 0)
                if extra:
                    pe.wait_ge(s["k_lo_done"], 4 * n + 6)
                    transpose_x(i + 1, 0)
                if not known(n, 0):
                    pe.wait_ge(s["k_lo_done"], 4 * n + 5) if more else pe.wait_ge(s["v_done"], 3 * n + 2)
                    output(n - 1, 1)
                scores(n, j, 2)
                if extra:
                    pe.wait_ge(s["y_done"], n)
                    transpose_x(i + 1, 1)
                if more:
                    pe.wait_ge(s["xt_lo_done"], 2 * i + 3) if extra else pe.wait_ge(s["k_lo_done"], 4 * n + 6)
                    project_k(n + 1, 1 - j, 2, 0)
                if extra:
                    project_q(i + 1, 0, 1)
                sums(n, 0)
                attend(n, j, 1)
                if more:
                    if extra:
                        pe.wait_ge(s["k_lo_done"], 4 * n + 7)
                        project_k(n + 1, 1 - j, 3, 0)
                        pe.wait_ge(s["q_lo_done"], 2 * i + 3)
                        project_q(i + 1, 1, 1)
                    else:
                        pe.wait_ge(s["k_lo_done"], 5) if known(n, 0) else pe.wait_ge(s["y_done"], n)
                        project_k(n + 1, 1 - j, 3, 1)
                sums(n, 1)
                scores(n, j, 3)
                if more:
                    pe.wait_ge(s["k_lo_done"], 4 * n + (8 if extra else 7))
                    project_v(n + 1, 0, 0)
                attend(n, j, 2)
                if more:
                    pe.wait_ge(s["q_lo_done"], 2 * i + 4) if extra else pe.wait_ge(s["k_lo_done"], 4 * n + 8)
                    project_v(n + 1, 1, 1)
                sums(n, 2)
                attend(n, j, 3)
                if more:
                    pe.wait_ge(s["v_done"], 3 * n + 4)
                    project_v(n + 1, 2, 0)
                sums(n, 3)

            def bias():
                pe.wait_ge(s["wide_done"], 1)
                pe.wait_ge(s["xo_in"], 16)
                for kc in range(KC):
                    last = pe.matmul(av[:], bv_wide[:, kc], raw[1][:, kc], start=(kc == 0), stop=(kc == KC - 1))
                last.then_inc(s["bias_ready"], 1)

            pe.wait_ge(s["setup"], 2)
            for mt in range(KC):
                if mt >= 2:
                    pe.wait_ge(s["k_lo_done"], mt - 1)
                project_k(0, 0, mt, mt % 2)
            for j in range(2):
                pe.wait_ge(s["k_lo_done"], 3 + j)
                transpose_x(0, j)
            bias()
            for half in range(2):
                project_q(0, half, half)
            for kt in range(KT):
                pe.wait_ge(s["q_lo_done"], kt + 1) if kt < 2 else pe.wait_ge(s["v_done"], 1)
                project_v(0, kt, kt % 2)
            pe.wait_ge(s["small_in"], 160)
            pe.wait_ge(s["bias_added"], 1)
            pe.wait_ge(s["xo_lo_done"], 1)
            step(0, 0, True, True)
            step(0, 1, True, True)
            with pe.Fori(1, PAIRS - 1) as i:
                step(i, 0, True, True)
                step(i, 1, True, True)
            step(PAIRS - 1, 0, True, False)
            step(PAIRS - 1, 1, False, False)
            spread(LASTB)
            pe.wait_ge(s["y_done"], LASTB)
            output(LASTB, 1)

        @block.scalar
        def _(act):
            def context_hi(n):
                act.wait_ge(s["c_in"], 16 * n + 16)
                if not known(n, 0):
                    act.wait_ge(s["v_ready"], 3 * n)
                for r in (slice(0, 2), slice(2, KC)):
                    act.activation(ctx[0][:, r, 0:S], craw[:, r], ACT.Copy).then_inc(s["c_hi_done"], 1)

            def k_hi(n, slot, mt, g):
                act.wait_ge(s["k_ready"], 4 * n + mt + 1)
                act.activation(k[slot][0][:, mt], gen[g][:, 0:SE], ACT.Identity, bias=c["bk"][:, mt:mt + 1]).then_inc(s["k_hi_done"], 1)

            def v_copy(n, slot, kt, g):
                act.wait_ge(s["v_ready"], 3 * n + kt + 1)
                act.activation(v[:, slot, kt], gen[g][0:KP, :], ACT.Copy).then_inc(s["v_done"], 1)

            def x_hi(i):
                for j in range(2):
                    act.wait_ge(s["xt_ready"], 2 * i + j + 1)
                    act.activation(xt[0][:, :, j * T:(j + 1) * T], gen[j][:, 0:QT].rearrange("p (c t) -> p c t", c=KC),
                                   ACT.Copy).then_inc(s["xt_hi_done"], 1)

            def q_hi(i, half, g):
                act.wait_ge(s["q_ready"], 2 * i + half + 1)
                for o in range(2):
                    mt = 2 * half + o
                    last = act.activation(q[0][:, mt], gen[g][:, o * PT:(o + 1) * PT], ACT.Identity, bias=c["bq"][:, mt:mt + 1])
                last.then_inc(s["q_hi_done"], 1)

            def place_q(n, j, i):
                act.wait_ge(s["q_hi_done"], 2 * i + 2)
                if not known(n, 0):
                    act.wait_ge(s["sc_done"], 12 * n)
                for h in range(HQ):
                    r = slice(DH * h, DH * (h + 1))
                    last = act.activation(qbd[0][r, :, h], f32(q[0][r, :, j * T:(j + 1) * T]), ACT.Copy)
                last.then_inc(s["qbd_hi_done"], 1)

            def exp(n, u):
                act.wait_ge(s["clip_done"], 12 * n + 3 * u + 3)
                act.activation(e[:, u % 2], e[:, u % 2], ACT.Exp, scale=SCALE).then_inc(s["exp_done"], 1)

            def spread_copy(n):
                act.wait_ge(s["zx_ready"], n + 1)
                act.activation(rzx[:], z[:, 0:QT], ACT.Copy).then_inc(s["rzx_done"], 1)

            def out_hi(n):
                act.wait_ge(s["on_done"], n + 1)
                if not known(n, 0):
                    act.wait_ge(s["y_ready"], n)
                act.activation(ot[0][:].rearrange("p c t -> p (c t)"), on[:], ACT.Copy).then_inc(s["ot_hi_done"], 1)

            def step(i, j, more, more_pairs, more_context):
                n = 2 * i + j
                extra = j == 1 and more_pairs
                if not known(n, 0):
                    spread_copy(n - 1)
                exp(n, 0)
                if not known(n, 0):
                    out_hi(n - 1)
                exp(n, 1)
                if more:
                    k_hi(n + 1, 1 - j, 0, 1)
                if more:
                    k_hi(n + 1, 1 - j, 1, 0)
                if extra:
                    x_hi(i + 1)
                exp(n, 2)
                if more:
                    k_hi(n + 1, 1 - j, 2, 0)
                if extra:
                    q_hi(i + 1, 0, 1)
                if more:
                    k_hi(n + 1, 1 - j, 3, 0 if extra else 1)
                if extra:
                    q_hi(i + 1, 1, 1)
                exp(n, 3)
                if more:
                    place_q(n + 1, 1 - j, i + j)
                    for kt in range(KT):
                        v_copy(n + 1, 1 - j, kt, kt % 2)
                if more_context:
                    context_hi(n + 2)

            context_hi(0)
            act.wait_ge(s["small_in"], 160)
            for mt in range(KC):
                k_hi(0, 0, mt, mt % 2)
            x_hi(0)
            act.wait_ge(s["xo_in"], 16)
            act.activation(w["o"][0][:], raw[1][:], ACT.Copy).then_inc(s["xo_hi_done"], 1)
            for half in range(2):
                q_hi(0, half, half)
            act.wait_ge(s["setup"], 4)
            place_q(0, 0, 0)
            for kt in range(KT):
                v_copy(0, 0, kt, kt % 2)
            context_hi(1)
            step(0, 0, True, True, True)
            step(0, 1, True, True, True)
            with act.Fori(1, PAIRS - 1) as i:
                step(i, 0, True, True, True)
                step(i, 1, True, True, True)
            step(PAIRS - 1, 0, True, False, False)
            step(PAIRS - 1, 1, False, False, False)
            spread_copy(LASTB)
            out_hi(LASTB)

        @block.vector
        def _(dve):
            def context_lo(n):
                for part, r in enumerate((slice(0, 2), slice(2, KC))):
                    dve.wait_ge(s["c_hi_done"], 2 * n + part + 1)
                    dve.tensor_tensor(ctx[1][:, r, 0:S], craw[:, r], f32(ctx[0][:, r, 0:S]), ALU.subtract).then_inc(s["c_lo_done"], 1)

            def layernorm_stats(i):
                dve.wait_ge(s["xa_in"], 16 * i + 16)
                for j in range(2):
                    dve.bn_stats(st[:, j], xa[:, j]).then_inc(s["stats_done"], 1)
                if not known(i, 0):
                    dve.wait_ge(s["xn_done"], 2 * i)
                dve.wait_ge(s["stats_done"], 2 * i + 2)
                carry_waits(dve, fence[:])
                for j in range(2):
                    dve.bn_aggr(mv[:, j], st[:, j]).then_inc(s["aggr_done"], 1)

            def layernorm_apply(i):
                for j in range(2):
                    dve.wait_ge(s["rstd_done"], 2 * i + j + 1)
                    if not known(i, 0):
                        dve.wait_ge(s["xt_ready"], 2 * i + j - 1)
                    dve.tensor_scalar(xn[:, j], xa[:, j], mv[:, j, 0:1], rstd[:, j], ALU.subtract, ALU.mult)\
                       .then_inc(s["xn_done"], 1)

            def x_lo(i):
                for j in range(2):
                    dve.wait_ge(s["xt_hi_done"], 2 * i + j + 1)
                    dve.tensor_tensor(xt[1][:, :, j * T:(j + 1) * T], gen[j][:, 0:QT].rearrange("p (c t) -> p c t", c=KC),
                                      f32(xt[0][:, :, j * T:(j + 1) * T]), ALU.subtract).then_inc(s["xt_lo_done"], 1)

            def k_lo(n, slot, mt, g):
                dve.wait_ge(s["k_hi_done"], 4 * n + mt + 1)
                dve.scalar_tensor_tensor(out=k[slot][1][:, mt], in0=gen[g][:, 0:SE], scalar=c["bk"][:, mt:mt + 1],
                                         in1=f32(k[slot][0][:, mt]), op0=ALU.add, op1=ALU.subtract).then_inc(s["k_lo_done"], 1)

            def q_lo(i, half, g):
                dve.wait_ge(s["q_hi_done"], 2 * i + half + 1)
                for o in range(2):
                    mt = 2 * half + o
                    last = dve.scalar_tensor_tensor(out=q[1][:, mt], in0=gen[g][:, o * PT:(o + 1) * PT], scalar=c["bq"][:, mt:mt + 1],
                                                    in1=f32(q[0][:, mt]), op0=ALU.add, op1=ALU.subtract)
                last.then_inc(s["q_lo_done"], 1)

            def place_q(n, j, i):
                dve.wait_ge(s["q_lo_done"], 2 * i + 2)
                if not known(n, 0):
                    dve.wait_ge(s["sc_done"], 12 * n)
                for h in range(HQ):
                    r = slice(DH * h, DH * (h + 1))
                    last = dve.tensor_copy(qbd[1][r, :, h], q[1][r, :, j * T:(j + 1) * T])
                last.then_inc(s["qbd_lo_done"], 1)

            def clip(n, u):
                if not (known(n, 0) and u < 2):
                    dve.wait_ge(s["av_done"], 4 * n + u - 1)
                    dve.wait_ge(s["esum_step"], 8 * n + 2 * u - 2)
                for kt in range(KT):
                    r = KT * u + kt
                    dve.wait_ge(s["sc_done"], 12 * n + r + 1)
                    dve.tensor_scalar(e[:, u % 2, kt], sc[0:KP, r % 4, 0:QT], c["bound"][:, bass.ds(n * KT + kt, 1)],
                                      -CLIP / SCALE, ALU.min, ALU.max).then_inc(s["clip_done"], 1)

            def tail_stats(n):
                dve.wait_ge(s["y_ready"], n + 1)
                if not known(n, 0):
                    dve.wait_ge(s["x2_step"], 3 * n)
                dve.tensor_tensor(y[:], gen[1][0:T, :], c["bo_full"][0:T], ALU.add).then_inc(s["y_done"], 1)
                dve.wait_ge(s["y_done"], n + 1)
                dve.bn_stats(yst[:], y[:]).then_inc(s["yst_done"], 1)
                dve.wait_ge(s["yst_done"], n + 1)
                carry_waits(dve, fence[:])
                dve.bn_aggr(ymv[:], yst[:]).then_inc(s["ymv_done"], 1)

            def tail_apply(n):
                dve.wait_ge(s["ysc_step"], 4 * n + 4)
                dve.tensor_scalar(y[:], y[:], ymv[:, 0:1], ysc[:, 3:4], ALU.subtract, ALU.mult).then_inc(s["d_done"], 1)

            def invert_sums(n):
                dve.wait_ge(s["z_done"], 4 * n + 4)
                dve.reciprocal(rz[:], z[:, 0:T]).then_inc(s["rz_done"], 1)

            def normalise(n):
                dve.wait_ge(s["rzx_done"], n + 1)
                dve.wait_ge(s["av_done"], 4 * n + 4)
                if not known(n, 0):
                    dve.wait_ge(s["ot_lo_done"], n)
                dve.tensor_tensor(on[:], av[:, 0:QT], rzx[:], ALU.mult).then_inc(s["on_done"], 1)

            def out_lo(n):
                dve.wait_ge(s["ot_hi_done"], n + 1)
                dve.tensor_tensor(ot[1][:].rearrange("p c t -> p (c t)"), on[:], f32(ot[0][:].rearrange("p c t -> p (c t)")),
                                  ALU.subtract).then_inc(s["ot_lo_done"], 1)

            def step(i, j, more, more_pairs, more_context):
                n = 2 * i + j
                extra = j == 1 and more_pairs
                if not known(n, 0):
                    invert_sums(n - 1)
                clip(n, 0)
                if more and not known(n, 0):
                    context_lo(n + 1)
                if not known(n, 0):
                    normalise(n - 1)
                clip(n, 1)
                if not known(n, 0):
                    out_lo(n - 1)
                if more:
                    k_lo(n + 1, 1 - j, 0, 1)
                    k_lo(n + 1, 1 - j, 1, 0)
                if not known(n, 0):
                    tail_stats(n - 1)
                if extra:
                    x_lo(i + 1)
                if j == 0 and more_pairs:
                    layernorm_stats(i + 1)
                clip(n, 2)
                if more:
                    k_lo(n + 1, 1 - j, 2, 0)
                if extra:
                    q_lo(i + 1, 0, 1)
                if not known(n, 0):
                    tail_apply(n - 1)
                if more:
                    k_lo(n + 1, 1 - j, 3, 0 if extra else 1)
                if extra:
                    q_lo(i + 1, 1, 1)
                if j == 0 and more_pairs:
                    layernorm_apply(i + 1)
                clip(n, 3)
                if more:
                    place_q(n + 1, 1 - j, i + j)

            context_lo(0)
            layernorm_stats(0)
            dve.wait_ge(s["small_in"], 160)
            layernorm_apply(0)
            dve.tensor_copy(maskf[:], mask[:]).then_inc(s["mask_step"], 1)
            dve.wait_ge(s["mask_step"], 1)
            dve.tensor_scalar(c["bound"][:], maskf[:], 0.5, 2 * CLIP / SCALE, ALU.is_gt, ALU.mult).then_inc(s["mask_step"], 1)
            dve.wait_ge(s["mask_step"], 2)
            dve.tensor_scalar(c["bound"][:], c["bound"][:], -CLIP / SCALE, None, ALU.add).then_inc(s["mask_step"], 1)
            dve.tensor_scalar(c["rs"][:], c["rs"][:], 0.0, 0.3, ALU.max, ALU.min).then_inc(s["rs_step"], 1)
            dve.wait_ge(s["rs_step"], 1)
            dve.tensor_tensor(c["rs2"][:], c["rs"][:], c["rs"][:], ALU.mult).then_inc(s["rs_step"], 1)
            for mt in range(KC):
                k_lo(0, 0, mt, mt % 2)
            x_lo(0)
            dve.wait_ge(s["bias_ready"], 1)
            dve.tensor_tensor(c["bo_full"][:], av[:], bo[:], ALU.add).then_inc(s["bias_added"], 1)
            dve.wait_ge(s["xo_hi_done"], 1)
            dve.tensor_tensor(w["o"][1][:], raw[1][:], f32(w["o"][0][:]), ALU.subtract).then_inc(s["xo_lo_done"], 1)
            for half in range(2):
                q_lo(0, half, half)
            dve.wait_ge(s["setup"], 4)
            dve.wait_ge(s["mask_step"], 3)
            place_q(0, 0, 0)
            context_lo(1)
            step(0, 0, True, True, True)
            step(0, 1, True, True, True)
            with dve.Fori(1, PAIRS - 1) as i:
                step(i, 0, True, True, True)
                step(i, 1, True, True, True)
            step(PAIRS - 1, 0, True, False, False)
            step(PAIRS - 1, 1, False, False, False)
            invert_sums(LASTB)
            normalise(LASTB)
            out_lo(LASTB)
            tail_stats(LASTB)
            tail_apply(LASTB)


def build_ffn(nc, dram, consts, sems):
    with ExitStack() as scope:
        m = Memory(nc, scope)
        x = m.sb("x3", [P, FT * D])
        xt = [m.sb(f"xt3_{n}", [P, KC, TOK], F32R) for n in ("hi", "lo")]
        fence = m.sb("fence_f3", [1, 1])
        st = m.sb("st3", [P, 2, 6])
        mv = m.sb("mv3", [P, 2, 2])
        veps = m.sb("veps3", [P, 2, 1])
        rstd = m.sb("rstd3", [P, 2, 1])
        xn = m.sb("xn3", [P, 2, D])
        raw = [m.sb(f"raw_w{n}", [P, KC, HC]) for n in (1, 3)]
        raw2 = m.sb("raw_w2", [P, HT, D])
        wg = [[[m.sb(f"w{n}_{part}{slot}", [P, KC, HC], F32R) for part in ("hi", "lo")] for n in (1, 3)] for slot in range(2)]
        fly = [m.sb(f"fly_{n}", [P, HT, D], F32R) for n in ("hi", "lo")]
        w2 = [[m.sb(f"w2_{part}{slot}", [P, HT, D], F32R) for part in ("hi", "lo")] for slot in range(2)]
        had = m.sb("had", [P, P], F32R)
        had_raw = m.sb("had_raw", [P, P])
        gate = m.sb("gate", [P, 2, 512])
        hf = m.sb("hf", [P, 2, 512])
        hid = [m.sb(f"hid_{n}", [P, 2, HT, 512], F32R) for n in ("hi", "lo")]
        psg = m.ps("psg", [P, 2, 512])
        psu = m.ps("psu", [P, 2, 512])
        psy = m.ps("psy", [P, 2, 512])
        psh = m.ps("psh", [P, 2, 512])
        names = ("x_in0 x_in1 stats_done aggr_done veps_done rstd_done xn_done xt_ready xt_hi_done xt_lo_done had_in had_done "
                 "w_in0 w_in1 w_in2 w_hi_done w_lo_done fly_ready w2_hi_done w2_lo_done gate_ready up_ready silu_done h_done "
                 "hid_hi_done hid_lo_done y_ready y_done out_done").split()
        s = {n: sems.sem("f_" + n) for n in names}
        x_in, w_in = (s["x_in0"], s["x_in1"]), (s["w_in0"], s["w_in1"], s["w_in2"])
        TP = FT // 2
        LEAD = 3
        UNITS = HT * len(FGROUPS)
        HSCALE = float(F) ** -0.5
        fly_dram = dram["w2_fly"].rearrange("p (c t) n -> p t c n", t=B)

        def known(i, *values):
            return isinstance(i, int) and i in values

        block = scope.enter_context(nc.Block())

        def xtile(t):
            return x[:, bass.ds(t * D, D)]

        @block.sync
        def _(sp):
            def tile(i, j):
                at, row = bass.ds(held(sp, (2 * i + j) * D), D), bass.ds(held(sp, (2 * i + j) * P), P)
                if not known(i, 0):
                    sp.wait_ge(x_in[j], 16 * i)
                sp.dma_start(x[:, at], dram["x2"][row, :]).then_inc(x_in[j], 16)

            def weights(c):
                at = bass.ds(held(sp, c * KC * HC), KC * HC)
                rows = [bass.ds(held(sp, c * HT + t), 1) for t in range(HT)]
                if not known(c, 0):
                    sp.wait_ge(s["w_lo_done"], 3 * c)
                for n, name in enumerate(("w1", "w3")):
                    sp.dma_start(raw[n][:].rearrange("p k n -> p (k n)"), dram[name][:, at]).then_inc(w_in[n], 16)
                for t in range(HT):
                    sp.dma_start(raw2[:, t].rearrange("p (c n) -> p c n", n=BCOL),
                                 fly_dram[:, rows[t]].rearrange("p t c n -> p (t c) n")).then_inc(w_in[2], 16)

            tile(0, 0)
            tile(0, 1)
            sp.dma_start(had_raw[:], dram["had"]).then_inc(s["had_in"], 16)
            weights(0)
            with sp.Fori(1, TP) as i:
                for j in range(2):
                    tile(i, j)
            with sp.Fori(1, CHUNKS) as c:
                weights(c)
            for t in range(FT):
                sp.wait_ge(s["y_done"], (CHUNKS - 1) * FT + t + 1)
                sp.dma_start(dram["out"][t * P:(t + 1) * P, :], x[:, t * D:(t + 1) * D]).then_inc(s["out_done"], 16)
            sp.wait_ge(s["out_done"], 16 * FT)

        @block.gpsimd
        def _(pool):
            def layernorm(i):
                for j in range(2):
                    pool.wait_ge(s["aggr_done"], 2 * i + j + 1)
                    pool.tensor_tensor(veps[:, j], mv[:, j, 1:2], consts["eps"][:], ALU.add).then_inc(s["veps_done"], 1)
                    pool.wait_ge(s["veps_done"], 2 * i + j + 1)
                    pool.tensor_tensor(rstd[:, j], veps[:, j], consts["minus_half"][:], ALU.pow).then_inc(s["rstd_done"], 1)

            def hidden_lo(c, n):
                width = FGROUPS[n // HT][1]
                pool.wait_ge(s["hid_hi_done"], UNITS * c + n + 1)
                pool.tensor_tensor(hid[1][:, (n // HT) % 2, n % HT, 0:width], hf[:, n % 2, 0:width],
                                   f32(hid[0][:, (n // HT) % 2, n % HT, 0:width]), ALU.subtract).then_inc(s["hid_lo_done"], 1)

            for i in range(LEAD):
                layernorm(i)
            for n in range(UNITS):
                if n + LEAD < TP:
                    layernorm(n + LEAD)
                hidden_lo(0, n)
            with pool.Fori(1, CHUNKS) as c:
                for n in range(UNITS):
                    hidden_lo(c, n)

        @block.tensor
        def _(pe):
            def transpose_x(i):
                for j in range(2):
                    pe.wait_ge(s["xn_done"], 2 * i + j + 1)
                    if i:
                        pe.wait_ge(s["xt_lo_done"], 2 * i + j - 1)
                    if i == TP - 1:
                        pe.wait_ge(s["y_done"], 3 + j)
                    for kc in range(KC):
                        last = pe.transpose(psy[:, j, kc * P:(kc + 1) * P], xn[:, j, kc * P:(kc + 1) * P], consts["ident"][:])
                    last.then_inc(s["xt_ready"], 1)

            def hadamard(c):
                pe.wait_ge(s["w_lo_done"], 3 * c + 3)
                if not known(c, 0):
                    pe.wait_ge(s["w2_lo_done"], HT * c)
                for t in range(HT):
                    pe.matmul(psh[:, t], had[:], fly[0][:, t], start=True, stop=False)
                    pe.matmul(psh[:, t], had[:], fly[1][:, t], start=False, stop=True).then_inc(s["fly_ready"], 1)

            def up(c, slot, g):
                at, width = FGROUPS[g]
                for t in range(HT):
                    n = HT * g + t
                    if n == 0:
                        pe.wait_ge(s["w_lo_done"], 3 * c + 2)
                    if t == 0 and known(c, 0):
                        pe.wait_ge(s["xt_lo_done"], (at + width) // P)
                    for which, (ps, done) in enumerate(((psg, "gate_ready"), (psu, "up_ready"))):
                        if not (known(c, 0) and n < 2):
                            pe.wait_ge(s["silu_done" if which == 0 else "h_done"], UNITS * c + n - 1)
                        for kc in range(KC):
                            wh, wl = wg[slot][which]
                            last = three_pass(pe, ps[:, t, 0:width], wh[:, kc, t * P:(t + 1) * P], wl[:, kc, t * P:(t + 1) * P],
                                              xt[0][:, kc, at:at + width], xt[1][:, kc, at:at + width], kc == 0, kc == KC - 1)
                        last.then_inc(s[done], 1)
                        if which == 0 and known(c, 0) and n + LEAD - 1 < TP:
                            transpose_x(n + LEAD - 1)

            def down(c, slot, g):
                at, width = FGROUPS[g]
                pe.wait_ge(s["hid_lo_done"], UNITS * c + HT * g + HT)
                if g == 0:
                    pe.wait_ge(s["w2_lo_done"], HT * c + HT)
                for k in range(width // P):
                    tile = at // P + k
                    if not (known(c, 0) and tile < 2):
                        pe.wait_ge(s["y_done"], FT * c + tile - 1)
                    if known(c, 0) and tile < 6:
                        pe.wait_ge(s["xt_lo_done"], 2 * (TP - 2 + tile // 4) + tile % 2 + 1)
                    for t in range(HT):
                        last = three_pass(pe, psy[:, tile % 2], hid[0][:, g % 2, t, k * P:(k + 1) * P], hid[1][:, g % 2, t, k * P:(k + 1) * P],
                                          w2[slot][0][:, t], w2[slot][1][:, t], t == 0, t == HT - 1)
                    last.then_inc(s["y_ready"], 1)

            def chunk(c, slot, more):
                up(c, slot, 0)
                if known(c, 0):
                    hadamard(0)
                else:
                    down(c - 1, 1 - slot, 3)
                up(c, slot, 1)
                down(c, slot, 0)
                up(c, slot, 2)
                down(c, slot, 1)
                up(c, slot, 3)
                if more:
                    hadamard(c + 1)
                down(c, slot, 2)

            for i in range(LEAD - 1):
                transpose_x(i)
            chunk(0, 0, True)
            chunk(1, 1, True)
            with pe.Fori(1, CHUNKS // 2 - 1) as i:
                chunk(2 * i, 0, True)
                chunk(2 * i + 1, 1, True)
            chunk(CHUNKS - 2, 0, True)
            chunk(CHUNKS - 1, 1, False)
            down(CHUNKS - 1, 1, 3)

        @block.scalar
        def _(act):
            def x_hi(i):
                for j in range(2):
                    act.wait_ge(s["xt_ready"], 2 * i + j + 1)
                    act.activation(xt[0][:, :, bass.ds((2 * i + j) * P, P)], psy[:, j].rearrange("p (c t) -> p c t", c=KC),
                                   ACT.Copy).then_inc(s["xt_hi_done"], 1)

            def split_hi(c, slot, parts):
                for n in parts:
                    dst, src = ((wg[slot][0][0], raw[0]), (wg[slot][1][0], raw[1]), (fly[0], raw2))[n]
                    act.wait_ge(w_in[n], 16 * c + 16 if n < 2 else 32 * c + 32)
                    if n == 2 and not known(c, 0):
                        act.wait_ge(s["fly_ready"], HT * c)
                    act.activation(dst[:], src[:], ACT.Copy).then_inc(s["w_hi_done"], 1)

            def w2_hi(c, slot):
                for t in range(HT):
                    act.wait_ge(s["fly_ready"], HT * c + t + 1)
                    act.activation(w2[slot][0][:, t], psh[:, t], ACT.Copy, scale=HSCALE).then_inc(s["w2_hi_done"], 1)

            def unit(c, n):
                g, t, width = n // HT, n % HT, FGROUPS[n // HT][1]
                act.wait_ge(s["gate_ready"], UNITS * c + n + 1)
                if not (known(c, 0) and n < 2):
                    act.wait_ge(s["h_done"], UNITS * c + n - 1)
                act.activation(gate[:, t, 0:width], psg[:, t, 0:width], ACT.Silu).then_inc(s["silu_done"], 1)
                act.wait_ge(s["h_done"], UNITS * c + n + 1)
                act.activation(hid[0][:, g % 2, t, 0:width], hf[:, t, 0:width], ACT.Copy).then_inc(s["hid_hi_done"], 1)

            def chunk(c, slot, more):
                for n in range(UNITS):
                    if n % HT == 0 and not (known(c, 0) and n < 2 * HT):
                        act.wait_ge(s["y_ready"], FT * c + (-2, 0, 4, 8)[n // HT])
                    if known(c, 0) and n + LEAD - 1 < TP:
                        x_hi(n + LEAD - 1)
                    unit(c, n)
                    if n == 1 and known(c, 0):
                        w2_hi(0, 0)
                    if n < 3 and more:
                        split_hi(c + 1, 1 - slot, (n,))
                if more:
                    w2_hi(c + 1, 1 - slot)

            split_hi(0, 0, (0, 1))
            for i in range(LEAD - 1):
                x_hi(i)
            split_hi(0, 0, (2,))
            chunk(0, 0, True)
            chunk(1, 1, True)
            with act.Fori(1, CHUNKS // 2 - 1) as i:
                chunk(2 * i, 0, True)
                chunk(2 * i + 1, 1, True)
            chunk(CHUNKS - 2, 0, True)
            chunk(CHUNKS - 1, 1, False)

        @block.vector
        def _(dve):
            def stats(i):
                for j in range(2):
                    dve.wait_ge(x_in[j], 16 * i + 16)
                    dve.bn_stats(st[:, j], xtile(2 * i + j)).then_inc(s["stats_done"], 1)
                if not known(i, 0):
                    dve.wait_ge(s["xn_done"], 2 * i)
                dve.wait_ge(s["stats_done"], 2 * i + 2)
                carry_waits(dve, fence[:])
                for j in range(2):
                    dve.bn_aggr(mv[:, j], st[:, j]).then_inc(s["aggr_done"], 1)

            def apply(i):
                for j in range(2):
                    dve.wait_ge(s["rstd_done"], 2 * i + j + 1)
                    if not known(i, 0):
                        dve.wait_ge(s["xt_ready"], 2 * i + j - 1)
                    dve.tensor_scalar(xn[:, j], xtile(2 * i + j), mv[:, j, 0:1], rstd[:, j], ALU.subtract, ALU.mult)\
                       .then_inc(s["xn_done"], 1)

            def x_lo(i):
                for j in range(2):
                    dve.wait_ge(s["xt_hi_done"], 2 * i + j + 1)
                    at = bass.ds((2 * i + j) * P, P)
                    dve.tensor_tensor(xt[1][:, :, at], psy[:, j].rearrange("p (c t) -> p c t", c=KC), f32(xt[0][:, :, at]),
                                      ALU.subtract).then_inc(s["xt_lo_done"], 1)

            def split_lo(c, slot, parts):
                for n in parts:
                    dst, src = ((wg[slot][0], raw[0]), (wg[slot][1], raw[1]), (fly, raw2))[n]
                    dve.wait_ge(s["w_hi_done"], 3 * c + n + 1)
                    dve.tensor_tensor(dst[1][:], src[:], f32(dst[0][:]), ALU.subtract).then_inc(s["w_lo_done"], 1)

            def w2_lo(c, slot):
                for t in range(HT):
                    dve.wait_ge(s["w2_hi_done"], HT * c + t + 1)
                    dve.scalar_tensor_tensor(out=w2[slot][1][:, t], in0=psh[:, t], scalar=HSCALE, in1=f32(w2[slot][0][:, t]),
                                             op0=ALU.mult, op1=ALU.subtract).then_inc(s["w2_lo_done"], 1)

            def unit(c, n):
                t, width = n % HT, FGROUPS[n // HT][1]
                dve.wait_ge(s["silu_done"], UNITS * c + n + 1)
                dve.wait_ge(s["up_ready"], UNITS * c + n + 1)
                if not (known(c, 0) and n < 2):
                    dve.wait_ge(s["hid_lo_done"], UNITS * c + n - 1)
                dve.tensor_tensor(hf[:, t, 0:width], gate[:, t, 0:width], psu[:, t, 0:width], ALU.mult).then_inc(s["h_done"], 1)

            def add(c, tiles):
                for tile in tiles:
                    dve.wait_ge(s["y_ready"], FT * c + tile + 1)
                    part = x[:, tile * D:(tile + 1) * D]
                    dve.tensor_tensor(part, psy[:, tile % 2], part, ALU.add).then_inc(s["y_done"], 1)

            def chunk(c, slot, more):
                for n in range(4):
                    if known(c, 0):
                        x_lo(n + LEAD - 1)
                    unit(c, n)
                    if known(c, 0) and n + LEAD < TP:
                        stats(n + LEAD)
                        apply(n + LEAD)
                    if n == 1:
                        w2_lo(0, 0) if known(c, 0) else add(c - 1, (12, 13))
                    if n < 3 and more:
                        split_lo(c + 1, 1 - slot, (n,))
                add(c, range(0, 4))
                if known(c, 0):
                    x_lo(TP - 1)
                unit(c, 4)
                unit(c, 5)
                add(c, range(4, 8))
                unit(c, 6)
                unit(c, 7)
                add(c, range(8, 12))
                if more:
                    w2_lo(c + 1, 1 - slot)

            stats(0)
            apply(0)
            split_lo(0, 0, (0, 1))
            for i in range(1, LEAD):
                stats(i)
                x_lo(i - 1)
                apply(i)
            dve.wait_ge(s["had_in"], 16)
            dve.tensor_copy(had[:], had_raw[:]).then_inc(s["had_done"], 1)
            split_lo(0, 0, (2,))
            chunk(0, 0, True)
            chunk(1, 1, True)
            with dve.Fori(1, CHUNKS // 2 - 1) as i:
                chunk(2 * i, 0, True)
                chunk(2 * i + 1, 1, True)
            chunk(CHUNKS - 2, 0, True)
            chunk(CHUNKS - 1, 1, False)
            add(CHUNKS - 1, (12, 13))


def build(nc, dram):
    with ExitStack() as root:
        sems = Memory(nc, root)
        consts = {"ident": sems.sb("ident", [P, P]), "eps": sems.sb("eps", [P, 1]), "minus_half": sems.sb("minus_half", [P, 1])}
        with ExitStack() as scope:
            m = Memory(nc, scope)
            w = {n: [m.sb(f"w{n}_{part}", [P, KC, D], F32R) for part in ("hi", "lo")] for n in "qkvo"}
            raw = [m.sb(f"raw{n}", [P, KC, D]) for n in range(2)]
            c = dict(consts, c_in=sems.sem("c_in"), xo_in=sems.sem("xo_in"))
            build_self(nc, dram, w, raw, consts, c, sems)
            build_cross(nc, dram, w, raw, c, sems)
        build_ffn(nc, dram, consts, sems)


def layouts(i):
    import numpy as np

    def stationary(w):
        return w.T.reshape(KC, P, D).transpose(1, 0, 2)

    def natural(w):
        return w.reshape(KC, P, D).transpose(1, 0, 2)

    def column(v):
        return v.reshape(KC, P).T

    def hidden(w):
        return w.T.reshape(KC, P, CHUNKS, HC).transpose(1, 2, 0, 3).reshape(P, CHUNKS * KC * HC)

    h = np.ones((1, 1), np.float32)
    while h.shape[0] < P:
        h = np.block([[h, h], [h, -h]])
    r = np.arange(P)
    sel = np.zeros((P, KC, DH), np.float32)
    spread = np.zeros((P, KC, P), np.float32)
    for u in range(KC):
        sel[:, u, u::KC] = 1.0
        for g in range(HQ):
            spread[DH * g + u, u, DH * g:DH * (g + 1)] = 1.0
    return {
        "x": i["x"].transpose(1, 0, 2).reshape(T, B * D),
        "ctx": i["ctx_2048"].transpose(2, 0, 1).reshape(KC, P, B, S).transpose(1, 2, 0, 3).reshape(P, B * KC * S),
        "mask": i["mask_BxS2_ik0"].reshape(B, KT, KP).transpose(2, 0, 1).reshape(KP, B * KT),
        "wq": natural(i["L0_attn_Wq"]), "wk": stationary(i["L0_attn_Wk"]), "wv": natural(i["L0_attn_Wv"]),
        "wo": stationary(i["L0_attn_Wo"]), "wdown_t": i["L0_attn_Wdown"].T, "wup": i["L0_attn_Wup"],
        "xq": stationary(i["L0_xattn_Wq"]), "xk": stationary(i["L0_xattn_Wk"]), "xv": stationary(i["L0_xattn_Wv"]),
        "xo": stationary(i["L0_xattn_Wo"]), "bq": column(i["L0_xattn_bq"]), "bk": column(i["L0_xattn_bk"]),
        "bv": column(i["L0_xattn_bv"]), "bo": i["L0_xattn_bo"].reshape(1, D), "gamma": i["L0_xattn_ln_gamma"].reshape(1, D),
        "beta": i["L0_xattn_ln_beta"].reshape(1, D), "rs": i["L0_xattn_residual_scale"].reshape(1, 1),
        "w1": hidden(i["L0_ffn_W1"]), "w3": hidden(i["L0_ffn_W3"]),
        "w2": i["L0_ffn_W2"].T.reshape(B, P, PAIRS, BCOL).transpose(1, 2, 0, 3).reshape(P, PAIRS * B, BCOL),
        "ident": np.eye(P, dtype=np.float32), "had": h, "sel": sel, "spread": spread,
    }


def kernel(**inputs):
    import numpy as np
    import concourse.bacc as bacc
    from concourse.bass_utils import run_bass_kernel_spmd

    nc = bacc.Bacc("TRN2", target_bir_lowering=False, num_devices=1)
    arrays = {"in_" + n: np.ascontiguousarray(a) for n, a in layouts({n: np.asarray(a) for n, a in inputs.items()}).items()}
    dram = {n[3:]: nc.dram_tensor(n, a.shape, mybir.dt.from_np(a.dtype), kind="ExternalInput").ap() for n, a in arrays.items()}
    dram["out"] = nc.dram_tensor("out", (TOK, D), F32, kind="ExternalOutput").ap()
    dram["x1"] = nc.dram_tensor("x1", (T, B * D), F32, kind="Internal").ap()
    dram["x2"] = nc.dram_tensor("x2", (TOK, D), F32, kind="Internal").ap()
    dram["w2_fly"] = nc.dram_tensor("w2_fly", (P, PAIRS * B, BCOL), F32, kind="Internal").ap()
    build(nc, dram)
    r = run_bass_kernel_spmd(nc, [arrays], core_ids=[0])
    return r.results[0]["out"].reshape(B, T, D)
```

```python
from contextlib import ExitStack

import concourse.bass as bass
from concourse import mybir

F32 = mybir.dt.float32
F32R = mybir.dt.float32r
I32 = mybir.dt.int32
ALU = mybir.AluOpType
ACT = mybir.ActivationFunctionType
AX_X = mybir.AxisListType.X

B, T, D = 16, 112, 512
S = 375
H, DH = 16, 32
F = 2048
P = 128
KC = D // P
HQ = P // DH
PAIRS = B // 2
PT = 2 * T
QT = HQ * T
KT = 3
KP = S // KT
SE = S + 1
EPS = 1e-5
SCALE = float(DH) ** -0.5
CLIP = 50.0
MASKED = -10000.0
TOK = B * T
FT = TOK // P
HC = 256
CHUNKS = F // HC
HT = HC // P
BCOL = D // PAIRS
FGROUPS = [(0, 512), (512, 512), (1024, 512), (1536, 256)]
TILES_G = FGROUPS[0][1] // P
TP = FT // 2
SHARED = ("x2_out0", "x2_out1", "c_in", "xa_in", "small_in", "xo_in", "padded", "c_hi_done", "c_lo_done", "k_ready", "k_hi_done", "k_lo_done")
CTX_PAIRS = 3
KEY_PAIRS = 6
READY_KEYS = 3
LEAD = 3


def three_pass(eng, out, w_hi, w_lo, m_hi, m_lo, start, stop):
    eng.matmul(out, w_hi, m_hi, start=start, stop=False)
    eng.matmul(out, w_hi, m_lo, start=False, stop=False)
    return eng.matmul(out, w_lo, m_hi, start=False, stop=stop)


def key_rows(pe, out, w, ctx, mt, chunks=range(KC)):
    for kc in chunks:
        last = three_pass(pe, out, w["k"][0][:, kc, mt * P:(mt + 1) * P], w["k"][1][:, kc, mt * P:(mt + 1) * P],
                          ctx[0][:, kc], ctx[1][:, kc], kc == 0, kc == KC - 1)
    return last


def key_hi(act, k, src, bk, mt):
    return act.activation(k[0][:, mt], src, ACT.Identity, bias=bk[:, mt:mt + 1])


def key_lo(dve, k, src, bk, mt):
    return dve.scalar_tensor_tensor(out=k[1][:, mt], in0=src, scalar=bk[:, mt:mt + 1], in1=f32(k[0][:, mt]),
                                    op0=ALU.add, op1=ALU.subtract)


def held(eng, value):
    return value if isinstance(value, int) else eng.snap(value)


def carry_waits(eng, cell):
    eng.memset(cell, 0.0)


def f32(ap):
    return ap.bitcast(F32)


class Memory:

    def __init__(self, nc, scope):
        self.nc, self.scope = nc, scope

    def sb(self, name, shape, dt=F32):
        return self.scope.enter_context(self.nc.sbuf_tensor(name, shape, dt))

    def ps(self, name, shape, dt=F32):
        return self.scope.enter_context(self.nc.psum_tensor(name, shape, dt))

    def sem(self, name):
        return self.scope.enter_context(self.nc.semaphore(name))


def build_self(nc, dram, w, raw, consts, c, sems):
    UNITS = 4
    FLY_STAGES = ((), (0,), (1,), (2, 3))
    with ExitStack() as scope:
        m = Memory(nc, scope)
        x = c["stream"]
        ctx, k_first = c["ctx"], c["k_slot0"]
        fence = m.sb("fence_f1", [1, 1])
        st = m.sb("st", [T, 2, 6])
        mv = m.sb("mv", [T, 2, 2])
        veps = m.sb("veps", [T, 2, 1])
        rstd = m.sb("rstd", [T, 2, 1])
        xn = m.sb("xn", [T, 2, D])
        xt = [m.sb(f"xt_{n}", [P, KC, PT], F32R) for n in ("hi", "lo")]
        k = [m.sb(f"k_{n}", [P, KC, PT], F32R) for n in ("hi", "lo")]
        kbd = [m.sb(f"kbd_{n}", [P, KC, 2, HQ, T], F32R) for n in ("hi", "lo")]
        q = [m.sb(f"q_{n}", [P, KC, PT], F32R) for n in ("hi", "lo")]
        v = m.sb("v", [T, 2, D])
        mx = m.sb("mx", [T, 2, 8])
        bias = m.sb("bias", [T, 2, 8])
        e = m.sb("e", [T, 2, 8, T])
        total = m.sb("total", [T, 2, 8])
        rtotal = m.sb("rtotal", [T, 2, 8])
        pt = m.sb("pt", [T, 2, 8, T])
        ot = [m.sb(f"ot_{n}", [P, 2, KC, T], F32R) for n in ("hi", "lo")]
        fly = m.sb("fly", [P, 2, B, BCOL])
        down_bd = m.sb("down_bd", [P, P])
        up_bd = m.sb("up_bd", [P, P])
        fold_q = m.sb("fold_q", [P, P])
        fold_v = m.sb("fold_v", [P, P])
        gen = [m.ps(f"gen{n}", [P, 512]) for n in range(2)]
        sc = m.ps("sc", [P, 4, 512])
        av = m.ps("av", [P, 2, 512])

        names = ("x_in0 x_in1 stats_done aggr_done veps_done rstd_done xn_done xt_ready xt_hi_done xt_lo_done "
                 "k_ready k_hi_done k_lo_done kbd_done q_ready q_hi_done q_lo_done v_ready v_done "
                 "sc_done mx_done bias_done exp_done rtotal_done norm_done pt_ready pt_done av_done "
                 "ot_hi_done ot_lo_done y_ready x1_done fly_in fly_step fly_out kbd_zeroed "
                 "zeroed diag_in const_in raw_in0 raw_in1 folds_done folds_copied q_folded v_folded w_hi_done w_lo_done").split()
        s = {n: sems.sem("s_" + n) for n in names}
        x_in, x1_out, raw_in = (s["x_in0"], s["x_in1"]), c["x1_out"], (s["raw_in0"], s["raw_in1"])
        K_SPLIT, Q_SPLIT, V_SPLIT, O_SPLIT, XK_SPLIT, XQ_SPLIT, XV_SPLIT = 1, 1 + KC, 1 + 2 * KC, *range(2 + 2 * KC, 6 + 2 * KC)

        def known(i, *values):
            return isinstance(i, int) and i in values

        def xb(i, j):
            return x[:, bass.ds((2 * i + j) * D, D)]

        block = scope.enter_context(nc.Block())

        @block.sync
        def _(sp):
            def load(i, j):
                at = bass.ds(held(sp, (2 * i + j) * D), D)
                if not isinstance(i, int):
                    sp.wait_ge(x_in[j], 16 * i)
                sp.dma_start(x[:, at], dram["x"][:, at]).then_inc(x_in[j], 16)

            def fly_load(i):
                at = bass.ds(held(sp, i * B), B)
                if not isinstance(i, int):
                    sp.wait_ge(s["fly_out"], 16 * i)
                sp.dma_start(fly[:, 0], dram["w2"][:, at, :]).then_inc(s["fly_in"], 16)

            def fly_store(i):
                at = bass.ds(held(sp, i * B), B)
                sp.wait_ge(s["fly_step"], 8 * i + 8)
                sp.dma_start(dram["w2_fly"][:, at, :], fly[:, 0]).then_inc(s["fly_out"], 16)

            def store(i, j):
                at, done = bass.ds(held(sp, (2 * i + j) * D), D), held(sp, 2 * i + j + 1)
                sp.wait_ge(s["x1_done"], done)
                if not isinstance(i, int):
                    sp.wait_ge(x1_out[j], 16 * i)
                sp.dma_start(dram["x1"][:, at], x[:, at]).then_inc(x1_out[j], 16)

            sp.dma_start(consts["ident"][:], dram["ident"]).then_inc(s["const_in"], 16)
            load(0, 0)
            load(0, 1)
            sp.dma_start(raw[0][:], dram["wk"]).then_inc(raw_in[0], 16)
            sp.wait_ge(s["zeroed"], 2)
            for g in range(HQ):
                r = slice(DH * g, DH * g + DH)
                sp.dma_start(down_bd[r, r], dram["wdown_t"]).then_inc(s["diag_in"], 16)
                sp.dma_start(up_bd[r, r], dram["wup"]).then_inc(s["diag_in"], 16)
            sp.dma_start(raw[1][:], dram["wq"]).then_inc(raw_in[1], 16)
            sp.wait_ge(s["w_lo_done"], K_SPLIT)
            sp.dma_start(raw[0][:], dram["wv"]).then_inc(raw_in[0], 16)
            load(1, 0)
            load(1, 1)
            sp.wait_ge(s["q_folded"], KC)
            sp.dma_start(raw[1][:], dram["wo"]).then_inc(raw_in[1], 16)
            fly_load(0)
            with sp.Fori(2, PAIRS) as i:
                for j in range(2):
                    load(i, j)
            sp.wait_ge(s["v_folded"], KC)
            sp.dma_start(raw[0][:], dram["xk"]).then_inc(raw_in[0], 16)
            sp.wait_ge(s["w_lo_done"], O_SPLIT)
            sp.dma_start(raw[1][:], dram["xq"]).then_inc(raw_in[1], 16)
            for name, src in (("bk", dram["bk"]), ("bq", dram["bq"]), ("bv", dram["bv"]), ("mask", dram["mask"]),
                              ("rs", dram["rs"].to_broadcast([P, 1]))):
                sp.dma_start(c[name][:], src).then_inc(c["small_in"], 16)
            fly_store(0)
            fly_load(1)
            store(0, 0)
            store(0, 1)
            with sp.Fori(2, PAIRS - 1) as i:
                fly_store(i - 1)
                fly_load(i)
                for j in range(2):
                    store(i - 1, j)
            fly_store(PAIRS - 2)
            sp.wait_ge(s["fly_out"], 16 * (PAIRS - 1))
            fly_load(PAIRS - 1)
            store(PAIRS - 2, 0)
            sp.wait_ge(s["w_lo_done"], XK_SPLIT)
            sp.dma_start(raw[0][:, :, 0:S], dram["ctx"][:, 0:KC * S].rearrange("p (c s) -> p c s", c=KC)).then_inc(c["c_in"], 16)
            store(PAIRS - 2, 1)
            sp.wait_ge(s["w_lo_done"], XQ_SPLIT)
            sp.dma_start(raw[1][:], dram["xv"]).then_inc(raw_in[1], 16)
            for j in range(2):
                sp.wait_ge(c["x1_out"][j], 16 * (PAIRS - 1))
            sp.dma_start(c["spare"][0][0:T].rearrange("t j d -> t (j d)"), dram["x1"][:, 0:2 * D]).then_inc(c["xa_in"], 16)
            sp.wait_ge(c["c_lo_done"], 2)
            sp.dma_start(raw[0][:, :, 0:S], dram["ctx"][:, KC * S:2 * KC * S].rearrange("p (c s) -> p c s", c=KC)).then_inc(c["c_in"], 16)
            sp.wait_ge(s["w_lo_done"], XV_SPLIT)
            sp.dma_start(raw[1][:], dram["xo"]).then_inc(c["xo_in"], 16)
            fly_store(PAIRS - 1)
            for j in range(2):
                store(PAIRS - 1, j)
            sp.wait_ge(s["fly_out"], 16 * PAIRS)

        @block.gpsimd
        def _(pool):
            def layernorm(i):
                for j in range(2):
                    pool.wait_ge(s["aggr_done"], 2 * i + j + 1)
                    pool.tensor_tensor(veps[:, j], mv[:, j, 1:2], consts["eps"][0:T], ALU.add).then_inc(s["veps_done"], 1)
                    pool.wait_ge(s["veps_done"], 2 * i + j + 1)
                    pool.tensor_tensor(rstd[:, j], veps[:, j], consts["minus_half"][0:T], ALU.pow).then_inc(s["rstd_done"], 1)

            def normalise(i, u):
                pool.wait_ge(s["rtotal_done"], 4 * i + u + 1)
                pool.tensor_tensor(e[:, u % 2], e[:, u % 2],
                                   rtotal[:, u % 2].unsqueeze(2).to_broadcast([T, 8, T]), ALU.mult).then_inc(s["norm_done"], 1)

            def fly_stage(i, n):
                a, b = n % 2, (n + 1) % 2
                st = 1 << n
                src = fly[:, a].rearrange("p (g two s) c -> p two g s c", two=2, s=st)
                dst = fly[:, b].rearrange("p (g two s) c -> p two g s c", two=2, s=st)
                if n == 0:
                    pool.wait_ge(s["fly_in"], 16 * i + 16)
                else:
                    pool.wait_ge(s["fly_step"], 8 * i + 2 * n)
                pool.tensor_tensor(dst[:, 0], src[:, 0], src[:, 1], ALU.add).then_inc(s["fly_step"], 1)
                pool.tensor_tensor(dst[:, 1], src[:, 0], src[:, 1], ALU.subtract).then_inc(s["fly_step"], 1)

            def step(i, last):
                for u in range(UNITS):
                    normalise(i, u)
                    if u == 2 and not last:
                        layernorm(i + 2)
                    for n in FLY_STAGES[u]:
                        fly_stage(i, n)

            pool.memset(down_bd[:], 0.0).then_inc(s["zeroed"], 1)
            pool.memset(up_bd[:], 0.0).then_inc(s["zeroed"], 1)
            pool.memset(consts["eps"][:], EPS).then_inc(s["zeroed"], 1)
            pool.memset(consts["minus_half"][:], -0.5).then_inc(s["zeroed"], 1)
            pool.wait_ge(s["zeroed"], 4)
            layernorm(0)
            for n in range(2):
                pool.memset(f32(kbd[n][:]), 0.0).then_inc(s["kbd_zeroed"], 1)
            layernorm(1)
            with pool.Fori(0, PAIRS - 2) as i:
                step(i, False)
            step(PAIRS - 2, True)
            for j in range(2):
                pool.wait_ge(c["x1_out"][j], 16 * CTX_PAIRS)
            for n in range(2):
                pool.memset(f32(ctx[n][:, :, S:SE]), 0.0).then_inc(c["padded"], 1)
            step(PAIRS - 1, True)

        @block.tensor
        def _(pe):
            def transpose_x(i, j):
                pe.wait_ge(s["xn_done"], 2 * i + j + 1)
                if not known(i, 0):
                    if j == 1:
                        pe.wait_ge(s["v_done"], 2 * i)
                    elif not known(i, 1):
                        pe.wait_ge(s["x1_done"], 2 * i - 2)
                    else:
                        pe.wait_ge(s["q_lo_done"], 2 * i - 1)
                for c in range(KC):
                    last = pe.transpose(gen[1 - j][:, c * T:(c + 1) * T], xn[:, j, c * P:(c + 1) * P],
                                        consts["ident"][0:T, 0:T])
                last.then_inc(s["xt_ready"], 1)

            def project(i, name, weights, half):
                if name == "q":
                    pe.wait_ge(s["k_lo_done"], 2 * i + half + 1)
                elif half == 0:
                    pe.wait_ge(s["xt_lo_done"], 2 * i + 2)
                for o in range(2):
                    mt = 2 * half + o
                    for c in range(KC):
                        last = three_pass(pe, gen[1 - half][:, o * PT:(o + 1) * PT],
                                          weights[0][:, c, mt * P:(mt + 1) * P], weights[1][:, c, mt * P:(mt + 1) * P],
                                          xt[0][:, c], xt[1][:, c], c == 0, c == KC - 1)
                last.then_inc(s[name + "_ready"], 1)

            def project_v(i, j):
                pe.wait_ge(s["q_lo_done"], 2 * i + 2) if j == 0 else pe.wait_ge(s["v_done"], 2 * i + 1)
                for c in range(KC):
                    last = three_pass(pe, gen[0][0:T, :], xt[0][:, c, j * T:(j + 1) * T], xt[1][:, c, j * T:(j + 1) * T],
                                      w["v"][0][:, c], w["v"][1][:, c], c == 0, c == KC - 1)
                last.then_inc(s["v_ready"], 1)

            def scores(i, u):
                j, b = u // 2, u % 2
                if b == 0:
                    pe.wait_ge(s["kbd_done"], 4 * i + 2 * j + 2)
                if j == 0:
                    pe.wait_ge(s["q_lo_done"], 2 * i + u + 1)
                if not (isinstance(i, int) and i == 0 and u < 2):
                    pe.wait_ge(s["pt_done"], 4 * i + u - 1)
                for n in range(2):
                    mt = 2 * b + n
                    last = three_pass(pe, sc[0:T, 2 * b + n, 0:QT],
                                      q[0][:, mt, j * T:(j + 1) * T], q[1][:, mt, j * T:(j + 1) * T],
                                      kbd[0][:, mt, j].rearrange("p h t -> p (h t)"),
                                      kbd[1][:, mt, j].rearrange("p h t -> p (h t)"), True, True)
                last.then_inc(s["sc_done"], 1)

            def transpose_p(i, u):
                b = u % 2
                pe.wait_ge(s["norm_done"], 4 * i + u + 1)
                for h in range(8):
                    last = pe.transpose(sc[0:T, 2 * b + h // 4, (h % 4) * T:(h % 4 + 1) * T], e[:, b, h],
                                        consts["ident"][0:T, 0:T])
                last.then_inc(s["pt_ready"], 1)

            def attend(i, u):
                j, b = u // 2, u % 2
                pe.wait_ge(s["pt_done"], 4 * i + u + 1)
                pe.wait_ge(s["v_done"], 2 * i + j + 1)
                if not (isinstance(i, int) and i == 0 and u < 2):
                    pe.wait_ge(s["ot_lo_done"], 4 * i + u - 1)
                for n in range(2):
                    for h in range(HQ):
                        head = (2 * b + n) * HQ + h
                        last = pe.matmul(av[DH * h:DH * (h + 1), b, n * T:(n + 1) * T],
                                         v[:, j, head * DH:(head + 1) * DH], pt[:, b, n * HQ + h],
                                         start=True, stop=True)
                last.then_inc(s["av_done"], 1)

            def output(i, j):
                pe.wait_ge(s["ot_lo_done"], 4 * i + 2 * j + 2)
                if known(i, PAIRS - 1) and j == 0:
                    pe.wait_ge(c["k_lo_done"], 2)
                elif j == 1:
                    pe.wait_ge(s["x1_done"], 2 * i + j)
                else:
                    pe.wait_ge(s["q_lo_done"], 2 * i + 3)
                for kc in range(KC):
                    last = three_pass(pe, gen[1][0:T, :], ot[0][:, j, kc], ot[1][:, j, kc], w["o"][0][:, kc], w["o"][1][:, kc],
                                      kc == 0, kc == KC - 1)
                last.then_inc(s["y_ready"], 1)

            def first_keys(mt):
                if mt == 0:
                    pe.wait_ge(s["v_done"], 2 * PAIRS)
                    pe.wait_ge(c["padded"], 2)
                    pe.wait_ge(s["w_lo_done"], XK_SPLIT)
                    pe.wait_ge(c["c_lo_done"], 2)
                elif mt == 1:
                    pe.wait_ge(s["x1_done"], 2 * PAIRS - 2)
                else:
                    pe.wait_ge(c["k_lo_done"], mt - 1)
                key_rows(pe, gen[mt % 2][:, 0:SE], w, ctx, mt).then_inc(c["k_ready"], 1)

            def step(i, more):
                first = known(i, 0)
                scores(i, 0)
                if known(i, 1):
                    pe.wait_ge(s["w_lo_done"], O_SPLIT)
                if not first:
                    output(i - 1, 0)
                    transpose_p(i - 1, 3)
                project_v(i, 0)
                if not first:
                    attend(i - 1, 3)
                scores(i, 1)
                if not first:
                    output(i - 1, 1)
                transpose_p(i, 0)
                project_v(i, 1)
                if more:
                    transpose_x(i + 1, 0)
                attend(i, 0)
                if more:
                    transpose_x(i + 1, 1)
                scores(i, 2)
                transpose_p(i, 1)
                if more:
                    project(i + 1, "k", w["k"], 0)
                attend(i, 1)
                if more:
                    project(i + 1, "k", w["k"], 1)
                scores(i, 3)
                project(i + 1, "q", w["q"], 0) if more else first_keys(0)
                transpose_p(i, 2)
                project(i + 1, "q", w["q"], 1) if more else first_keys(1)
                attend(i, 2)

            def fold(nat, mat, arrived, done):
                pe.wait_ge(*arrived)
                for c in range(KC):
                    for o in range(KC):
                        last = pe.matmul(sc[:, c, o * P:(o + 1) * P], nat[:, o, c * P:(c + 1) * P], mat[:], start=True, stop=True)
                    last.then_inc(done, 1)

            pe.wait_ge(s["const_in"], 16)
            for j in range(2):
                transpose_x(0, j)
            pe.wait_ge(s["diag_in"], 16 * 2 * HQ)
            pe.matmul(av[:, 0, 0:P], down_bd[:], down_bd[:], start=True, stop=True)
            pe.matmul(av[:, 1, 0:P], down_bd[:], up_bd[:], start=True, stop=True).then_inc(s["folds_done"], 1)
            pe.wait_ge(s["folds_copied"], 2)
            fold(raw[1], fold_q, (raw_in[1], 16), s["q_folded"])
            pe.wait_ge(s["w_lo_done"], K_SPLIT)
            for half in range(2):
                project(0, "k", w["k"], half)
            pe.wait_ge(s["w_lo_done"], Q_SPLIT)
            fold(raw[0], fold_v, (raw_in[0], 32), s["v_folded"])
            for half in range(2):
                project(0, "q", w["q"], half)
            pe.wait_ge(s["w_lo_done"], V_SPLIT)
            step(0, True)
            step(1, True)
            with pe.Fori(2, PAIRS - 1) as i:
                step(i, True)
            step(PAIRS - 1, False)
            first_keys(2)
            transpose_p(PAIRS - 1, 3)
            output(PAIRS - 1, 0)
            attend(PAIRS - 1, 3)
            output(PAIRS - 1, 1)

        @block.scalar
        def _(act):
            def pt_copy(i, u):
                b = u % 2
                act.wait_ge(s["pt_ready"], 4 * i + u + 1)
                if not (isinstance(i, int) and i == 0 and u < 2):
                    act.wait_ge(s["av_done"], 4 * i + u - 1)
                act.activation(pt[:, b].rearrange("t (n h) q -> t n (h q)", n=2), sc[0:T, 2 * b:2 * b + 2, 0:QT],
                               ACT.Copy).then_inc(s["pt_done"], 1)

            def ot_hi(i, u):
                j, b = u // 2, u % 2
                act.wait_ge(s["av_done"], 4 * i + u + 1)
                if not (isinstance(i, int) and i == 0):
                    act.wait_ge(s["y_ready"], 2 * i + j - 1)
                act.activation(ot[0][:, j, 2 * b:2 * b + 2], av[:, b, 0:2 * T].rearrange("p (n t) -> p n t", n=2),
                               ACT.Copy).then_inc(s["ot_hi_done"], 1)

            def exp(i, u, n):
                b = u % 2
                if n == 0:
                    act.wait_ge(s["bias_done"], 4 * i + u + 1)
                    if not (known(i, 0) and u < 2):
                        act.wait_ge(s["pt_ready"], 4 * i + u - 1)
                for h in range(HQ):
                    head = n * HQ + h
                    last = act.activation(e[:, b, head], sc[0:T, 2 * b + n, h * T:(h + 1) * T], ACT.Exp, bias=bias[:, b, head:head + 1],
                                          scale=SCALE, accum_out=total[:, b, head:head + 1])
                last.then_inc(s["exp_done"], 1)

            def x_hi(i, j):
                act.wait_ge(s["xt_ready"], 2 * i + j + 1)
                if not known(i, 0):
                    act.wait_ge(s["v_ready"], 2 * i + j - 1)
                act.activation(xt[0][:, :, j * T:(j + 1) * T], gen[1 - j][:, 0:QT].rearrange("p (c t) -> p c t", c=KC),
                               ACT.Copy).then_inc(s["xt_hi_done"], 1)

            def hi(i, name, dst, half):
                act.wait_ge(s[name + "_ready"], 2 * i + half + 1)
                if not known(i, 0):
                    act.wait_ge(s["kbd_done"], 4 * i) if name == "k" else act.wait_ge(s["sc_done"], 4 * i)
                act.activation(dst[0][:, 2 * half:2 * half + 2], gen[1 - half][:, 0:2 * PT].rearrange("p (o t) -> p o t", o=2),
                               ACT.Copy).then_inc(s[name + "_hi_done"], 1)

            def split_hi(name, b, loads):
                act.wait_ge(raw_in[b], 16 * loads)
                act.activation(w[name][0][:], raw[b][:], ACT.Copy).then_inc(s["w_hi_done"], 1)

            def folded_hi(name, done):
                for c in range(KC):
                    act.wait_ge(done, c + 1)
                    act.activation(w[name][0][:, c], sc[:, c], ACT.Copy).then_inc(s["w_hi_done"], 1)

            def first_context_hi():
                act.wait_ge(c["c_in"], 16)
                for j in range(2):
                    act.wait_ge(c["x1_out"][j], 16 * CTX_PAIRS)
                for r in (slice(0, 2), slice(2, KC)):
                    act.activation(ctx[0][:, r, 0:S], raw[0][:, r, 0:S], ACT.Copy).then_inc(c["c_hi_done"], 1)

            def first_key_hi(mt):
                act.wait_ge(c["k_ready"], mt + 1)
                if mt == 0:
                    act.wait_ge(c["small_in"], 80)
                    for j in range(2):
                        act.wait_ge(c["x1_out"][j], 16 * KEY_PAIRS)
                key_hi(act, k_first, gen[mt % 2][:, 0:SE], c["bk"], mt).then_inc(c["k_hi_done"], 1)

            def step(i, more):
                first = known(i, 0)
                if not first:
                    ot_hi(i - 1, 2)
                if not more:
                    split_hi("k", 0, 3)
                exp(i, 0, 0)
                exp(i, 0, 1)
                if not first:
                    pt_copy(i - 1, 3)
                    ot_hi(i - 1, 3)
                if not more:
                    split_hi("q", 1, 3)
                exp(i, 1, 0)
                exp(i, 1, 1)
                pt_copy(i, 0)
                if first:
                    split_hi("o", 1, 2)
                if more:
                    x_hi(i + 1, 0)
                    x_hi(i + 1, 1)
                ot_hi(i, 0)
                if not more:
                    first_context_hi()
                pt_copy(i, 1)
                exp(i, 2, 0)
                exp(i, 2, 1)
                if more:
                    hi(i + 1, "k", k, 0)
                ot_hi(i, 1)
                if more:
                    hi(i + 1, "k", k, 1)
                else:
                    act.wait_ge(s["v_ready"], 2 * PAIRS)
                    split_hi("v", 1, 4)
                exp(i, 3, 0)
                if more:
                    hi(i + 1, "q", q, 0)
                else:
                    first_key_hi(0)
                    pt_copy(i, 2)
                exp(i, 3, 1)
                if more:
                    pt_copy(i, 2)
                if more:
                    hi(i + 1, "q", q, 1)

            for j in range(2):
                x_hi(0, j)
            split_hi("k", 0, 1)
            folded_hi("q", s["q_folded"])
            for half in range(2):
                hi(0, "k", k, half)
            folded_hi("v", s["v_folded"])
            for half in range(2):
                hi(0, "q", q, half)
            step(0, True)
            with act.Fori(1, PAIRS - 1) as i:
                step(i, True)
            step(PAIRS - 1, False)
            ot_hi(PAIRS - 1, 2)
            first_key_hi(1)
            pt_copy(PAIRS - 1, 3)
            first_key_hi(2)
            ot_hi(PAIRS - 1, 3)

        @block.vector
        def _(dve):
            def layernorm_stats(i):
                for j in range(2):
                    dve.wait_ge(x_in[j], 16 * i + 16)
                    dve.bn_stats(st[:, j], xb(i, j)).then_inc(s["stats_done"], 1)
                dve.wait_ge(s["stats_done"], 2 * i + 2)
                if not (isinstance(i, int) and i == 0):
                    dve.wait_ge(s["xn_done"], 2 * i)
                carry_waits(dve, fence[:])
                for j in range(2):
                    dve.bn_aggr(mv[:, j], st[:, j]).then_inc(s["aggr_done"], 1)

            def layernorm_apply(i, j):
                dve.wait_ge(s["rstd_done"], 2 * i + j + 1)
                if not (isinstance(i, int) and i == 0):
                    dve.wait_ge(s["xt_ready"], 2 * i + j - 1)
                dve.tensor_scalar(xn[:, j], xb(i, j), mv[:, j, 0:1], rstd[:, j], ALU.subtract, ALU.mult)\
                   .then_inc(s["xn_done"], 1)

            def x_lo(i, j):
                dve.wait_ge(s["xt_hi_done"], 2 * i + j + 1)
                dve.tensor_tensor(xt[1][:, :, j * T:(j + 1) * T], gen[1 - j][:, 0:QT].rearrange("p (c t) -> p c t", c=KC),
                                  f32(xt[0][:, :, j * T:(j + 1) * T]), ALU.subtract).then_inc(s["xt_lo_done"], 1)

            def lo(i, name, dst, half):
                dve.wait_ge(s[name + "_hi_done"], 2 * i + half + 1)
                dve.tensor_tensor(dst[1][:, 2 * half:2 * half + 2], gen[1 - half][:, 0:2 * PT].rearrange("p (o t) -> p o t", o=2),
                                  f32(dst[0][:, 2 * half:2 * half + 2]), ALU.subtract).then_inc(s[name + "_lo_done"], 1)

            def place_k(i, j, part):
                if part == 0:
                    dve.wait_ge(s["k_lo_done"], 2 * i + 2)
                    if not known(i, 0):
                        dve.wait_ge(s["sc_done"], 4 * i - 2 + 2 * j)
                for h in range(HQ):
                    r = slice(DH * h, DH * (h + 1))
                    end = dve.tensor_copy(kbd[part][r, :, j, h], k[part][r, :, j * T:(j + 1) * T])
                end.then_inc(s["kbd_done"], 1)

            def maximum(i, u):
                b = u % 2
                src = sc[0:T, 2 * b:2 * b + 2, 0:QT].rearrange("t n (h k) -> t n h k", h=HQ)
                dve.wait_ge(s["sc_done"], 4 * i + u + 1)
                dve.reduce_max(mx[:, b].rearrange("t (n h) -> t n h", n=2), src, AX_X).then_inc(s["mx_done"], 1)
                dve.wait_ge(s["mx_done"], 4 * i + u + 1)
                if not (known(i, 0) and u < 2):
                    dve.wait_ge(s["exp_done"], 8 * i + 2 * u - 2)
                dve.tensor_scalar(bias[:, b], mx[:, b], -SCALE, None, ALU.mult).then_inc(s["bias_done"], 1)

            def invert_total(i, u):
                dve.wait_ge(s["exp_done"], 8 * i + 2 * u + 2)
                if not (known(i, 0) and u < 2):
                    dve.wait_ge(s["norm_done"], 4 * i + u - 1)
                dve.reciprocal(rtotal[:, u % 2], total[:, u % 2]).then_inc(s["rtotal_done"], 1)

            def v_copy(i, j):
                dve.wait_ge(s["v_ready"], 2 * i + j + 1)
                if not known(i, 0):
                    dve.wait_ge(s["av_done"], 4 * i - 2 + 2 * j)
                dve.tensor_copy(v[:, j], gen[0][0:T, :]).then_inc(s["v_done"], 1)

            def ot_lo(i, u):
                j, b = u // 2, u % 2
                dve.wait_ge(s["ot_hi_done"], 4 * i + u + 1)
                dve.tensor_tensor(ot[1][:, j, 2 * b:2 * b + 2], av[:, b, 0:2 * T].rearrange("p (n t) -> p n t", n=2),
                                  f32(ot[0][:, j, 2 * b:2 * b + 2]), ALU.subtract).then_inc(s["ot_lo_done"], 1)

            def add_x(i, j):
                dve.wait_ge(s["y_ready"], 2 * i + j + 1)
                dve.tensor_tensor(xb(i, j), gen[1][0:T, :], xb(i, j), ALU.add).then_inc(s["x1_done"], 1)

            def split_lo(name, b, count):
                dve.wait_ge(s["w_hi_done"], count)
                dve.tensor_tensor(w[name][1][:], raw[b][:], f32(w[name][0][:]), ALU.subtract).then_inc(s["w_lo_done"], 1)

            def folded_lo(name, count):
                for c in range(KC):
                    dve.wait_ge(s["w_hi_done"], count - KC + c + 1)
                    dve.tensor_tensor(w[name][1][:, c], sc[:, c], f32(w[name][0][:, c]), ALU.subtract).then_inc(s["w_lo_done"], 1)

            def first_context_lo():
                for part, r in enumerate((slice(0, 2), slice(2, KC))):
                    dve.wait_ge(c["c_hi_done"], part + 1)
                    dve.tensor_tensor(ctx[1][:, r, 0:S], raw[0][:, r, 0:S], f32(ctx[0][:, r, 0:S]), ALU.subtract).then_inc(c["c_lo_done"], 1)

            def first_key_lo(mt):
                dve.wait_ge(c["k_hi_done"], mt + 1)
                key_lo(dve, k_first, gen[mt % 2][:, 0:SE], c["bk"], mt).then_inc(c["k_lo_done"], 1)

            def step(i, more, more_stats):
                first = known(i, 0)
                maximum(i, 0)
                if not first:
                    ot_lo(i - 1, 2)
                place_k(i, 1, 0)
                if not first:
                    add_x(i - 1, 0)
                place_k(i, 1, 1)
                invert_total(i, 0)
                if more:
                    layernorm_apply(i + 1, 0)
                    v_copy(i, 0)
                else:
                    split_lo("k", 0, XK_SPLIT)
                if not first:
                    ot_lo(i - 1, 3)
                if not more:
                    v_copy(i, 0)
                maximum(i, 1)
                if not more:
                    split_lo("q", 1, XQ_SPLIT)
                if more:
                    layernorm_apply(i + 1, 1)
                if not first:
                    add_x(i - 1, 1)
                invert_total(i, 1)
                v_copy(i, 1)
                if more:
                    x_lo(i + 1, 0)
                    x_lo(i + 1, 1)
                ot_lo(i, 0)
                maximum(i, 2)
                if not more:
                    first_context_lo()
                if first:
                    split_lo("o", 1, O_SPLIT)
                if more_stats:
                    layernorm_stats(i + 2)
                invert_total(i, 2)
                if more:
                    lo(i + 1, "k", k, 0)
                ot_lo(i, 1)
                if more:
                    lo(i + 1, "k", k, 1)
                maximum(i, 3)
                if not more:
                    split_lo("v", 1, XV_SPLIT)
                    first_key_lo(0)
                if more:
                    place_k(i + 1, 0, 0)
                    place_k(i + 1, 0, 1)
                    lo(i + 1, "q", q, 0)
                invert_total(i, 3)
                if more:
                    lo(i + 1, "q", q, 1)

            layernorm_stats(0)
            for j in range(2):
                layernorm_apply(0, j)
            for j in range(2):
                x_lo(0, j)
            dve.wait_ge(s["folds_done"], 1)
            dve.tensor_copy(fold_q[:], av[:, 0, 0:P]).then_inc(s["folds_copied"], 1)
            dve.tensor_copy(fold_v[:], av[:, 1, 0:P]).then_inc(s["folds_copied"], 1)
            split_lo("k", 0, K_SPLIT)
            folded_lo("q", Q_SPLIT)
            for half in range(2):
                lo(0, "k", k, half)
            dve.wait_ge(s["kbd_zeroed"], 2)
            place_k(0, 0, 0)
            place_k(0, 0, 1)
            folded_lo("v", V_SPLIT)
            for half in range(2):
                lo(0, "q", q, half)
            layernorm_stats(1)
            step(0, True, True)
            with dve.Fori(1, PAIRS - 2) as i:
                step(i, True, True)
            step(PAIRS - 2, True, False)
            step(PAIRS - 1, False, False)
            ot_lo(PAIRS - 1, 2)
            first_key_lo(1)
            first_key_lo(2)
            add_x(PAIRS - 1, 0)
            ot_lo(PAIRS - 1, 3)
            add_x(PAIRS - 1, 1)


def build_cross(nc, dram, w, raw, c, f, sems):
    with ExitStack() as scope:
        m = Memory(nc, scope)
        xa, xn = f["spare"]
        xr = m.sb("xr", [T, 2, D])
        fence = m.sb("fence_f2", [1, 1])
        st = m.sb("st2", [T, 2, 6])
        mv = m.sb("mv2", [T, 2, 2])
        veps = m.sb("veps2", [T, 2, 1])
        rstd = m.sb("rstd2", [T, 2, 1])
        xt = [m.sb(f"xt2_{n}", [P, KC, PT], F32R) for n in ("hi", "lo")]
        q = [m.sb(f"q2_{n}", [P, KC, PT], F32R) for n in ("hi", "lo")]
        qbd = [m.sb(f"qbd_{n}", [P, KC, HQ, T], F32R) for n in ("hi", "lo")]
        ctx = c["ctx"]
        craw = raw[0][:, :, 0:S]
        k = [c["k_slot0"], [m.sb(f"k2_{n}1", [P, KC, SE], F32R) for n in ("hi", "lo")]]
        tst, tmv = m.sb("tst", [P, 2, 6]), m.sb("tmv", [P, 2, 2])
        tveps, trstd = m.sb("tveps", [P, 2, 1]), m.sb("trstd", [P, 2, 1])
        v = m.sb("v2", [KP, 2, KT, D])
        e = m.sb("e2", [KP, 2, KT, QT])
        esum = m.sb("esum", [KP, 2, QT])
        ones = m.sb("ones", [KP, DH])
        rz = m.sb("rz", [P, QT])
        on = m.sb("on", [P, QT])
        ot = [m.sb(f"ot2_{n}", [P, KC, T], F32R) for n in ("hi", "lo")]
        y = m.sb("y", [T, D])
        yst = m.sb("yst", [T, 6])
        ymv = m.sb("ymv", [T, 2])
        ysc = m.sb("ysc", [T, 4])
        bv_wide = m.sb("bv_wide", [P, KC, P])
        bo = m.sb("bo", [P, D])
        maskf = m.sb("maskf", [KP, B * KT])
        for name, shape in (("bo_full", [P, D]), ("gamma", [P, D]), ("beta", [P, D]), ("rs2", [P, 1]), ("bound", [KP, B * KT])):
            c[name] = m.sb(name, shape)
        gen = [m.ps(f"gen2_{n}", [P, 512]) for n in range(2)]
        sc = m.ps("sc2", [P, 4, 512])
        av = m.ps("av2", [P, 512])
        z = m.ps("z2", [P, 512])

        names = ("xr_in0 xr_in1 stats_done aggr_done veps_done rstd_done xn_done xt_ready "
                 "xt_hi_done xt_lo_done q_ready q_hi_done q_lo_done qbd_hi_done qbd_lo_done "
                 "v_ready v_done sc_done clip_done exp_done esum_step av_done z_done "
                 "rz_done on_done ot_hi_done ot_lo_done y_ready y_done yst_done ymv_done ysc_step "
                 "d_done x2_step last_step wide_in wide_done bias_ready bias_added setup mask_step rs_step xo_hi_done xo_lo_done").split()
        s = {n: sems.sem("c_" + n) for n in names}
        s.update({n: c[n] for n in SHARED})
        xr_in, x2_out = (s["xr_in0"], s["xr_in1"]), (s["x2_out0"], s["x2_out1"])
        LASTB = B - 1

        y_last = e[0:T, 0].rearrange("p k q -> p (k q)")[:, 0:D]

        def tile_bank(p, j):
            return sc[:, 2 * (p - 1) + j] if p else gen[j][:]

        def known(i, *values):
            return isinstance(i, int) and i in values

        block = scope.enter_context(nc.Block())

        @block.sync
        def _(sp):
            def context(n):
                at = bass.ds(held(sp, n * KC * S), KC * S)
                sp.wait_ge(s["c_lo_done"], 2 * n)
                sp.dma_start(craw, dram["ctx"][:, at].rearrange("p (c s) -> p c s", c=KC)).then_inc(s["c_in"], 16)

            def pair(i):
                at = bass.ds(held(sp, i * 2 * D), 2 * D)
                sp.wait_ge(s["xn_done"], 2 * i)
                sp.dma_start(xa[0:T].rearrange("t j d -> t (j d)"), dram["x1"][:, at]).then_inc(s["xa_in"], 16)

            def residual(i, j):
                at = bass.ds(held(sp, (2 * i + j) * D), D)
                if not known(i, 0):
                    sp.wait_ge(x2_out[j], 16 * i)
                sp.dma_start(xr[:, j], dram["x1"][:, at]).then_inc(xr_in[j], 16)

            def store(i, j):
                at = bass.ds(held(sp, (2 * i + j) * T), T)
                if known(i, PAIRS - 1) and j == 1:
                    sp.wait_ge(s["last_step"], 3)
                else:
                    sp.wait_ge(s["x2_step"], 3 * (2 * i + j) + 3)
                sp.dma_start(dram["x2"][at, :], xr[:, j]).then_inc(x2_out[j], 16)

            def ready_tiles(p):
                sp.wait_ge(f["xn_done"], 2 * p) if p else sp.wait_ge(s["xn_done"], 2 * PAIRS)
                for j in range(2):
                    row = (2 * p + j) * P
                    sp.dma_start(xa[:, j], dram["x2"][row:row + P, :]).then_inc(f["x_in" + str(j)], 16)

            def ready_weights():
                for n, name in enumerate(("w1", "w3")):
                    sp.dma_start(f["raw"][n], dram[name][:, 0:KC * HC].rearrange("p (k n) -> p k n", k=KC)).then_inc(f["w_in" + str(n)], 16)
                sp.wait_ge(s["c_lo_done"], 2 * B)
                for t in range(HT):
                    sp.dma_start(f["raw2"][:, t].rearrange("p (c n) -> p c n", n=BCOL), f["fly_dram"][:, t]).then_inc(f["w_in2"], 16)

            def step(i, first, more, more_pairs):
                if known(i, PAIRS - 1):
                    ready_tiles(0)
                    ready_weights()
                if not first:
                    store(i - 1, 1)
                    residual(i, 1)
                if more:
                    context(2 * i + 3)
                if more_pairs:
                    pair(i + 2)
                if known(i, PAIRS - 1):
                    for p in range(1, LEAD):
                        ready_tiles(p)
                store(i, 0)
                if more:
                    residual(i + 1, 0)
                if more_pairs:
                    context(2 * i + 4)

            for dst, name in ((bo, "bo"), (c["gamma"], "gamma"), (c["beta"], "beta")):
                sp.dma_start(dst[:], dram[name].to_broadcast([P, D])).then_inc(s["wide_in"], 16)
            for j in range(2):
                sp.wait_ge(c["x1_out"][j], 16 * PAIRS)
            residual(0, 0)
            residual(0, 1)
            pair(1)
            context(2)
            step(0, True, True, True)
            with sp.Fori(1, PAIRS - 2) as i:
                step(i, False, True, True)
            step(PAIRS - 2, False, True, False)
            step(PAIRS - 1, False, False, False)
            store(PAIRS - 1, 1)

        @block.gpsimd
        def _(pool):
            def layernorm(i):
                for j in range(2):
                    pool.wait_ge(s["aggr_done"], 2 * i + j + 1)
                    pool.tensor_tensor(veps[:, j], mv[:, j, 1:2], c["eps"][0:T], ALU.add).then_inc(s["veps_done"], 1)
                    pool.wait_ge(s["veps_done"], 2 * i + j + 1)
                    pool.tensor_tensor(rstd[:, j], veps[:, j], c["minus_half"][0:T], ALU.pow).then_inc(s["rstd_done"], 1)

            def tile_scale(p):
                for j in range(2):
                    pool.wait_ge(f["aggr_done"], 2 * p + j + 1)
                    pool.tensor_tensor(tveps[:, j], tmv[:, j, 1:2], c["eps"][:], ALU.add).then_inc(f["veps_done"], 1)
                    pool.wait_ge(f["veps_done"], 2 * p + j + 1)
                    pool.tensor_tensor(trstd[:, j], tveps[:, j], c["minus_half"][:], ALU.pow).then_inc(f["rstd_done"], 1)

            def sum_tiles(n, u):
                pool.wait_ge(s["exp_done"], 4 * n + u + 1)
                if not (known(n, 0) and u < 2):
                    pool.wait_ge(s["z_done"], 4 * n + u - 1)
                pool.tensor_tensor(esum[:, u % 2], e[:, u % 2, 0], e[:, u % 2, 1], ALU.add).then_inc(s["esum_step"], 1)
                pool.wait_ge(s["esum_step"], 8 * n + 2 * u + 1)
                pool.tensor_tensor(esum[:, u % 2], esum[:, u % 2], e[:, u % 2, 2], ALU.add).then_inc(s["esum_step"], 1)

            def tail_scale(n):
                pool.wait_ge(s["ymv_done"], n + 1)
                for step, (a, b, op) in enumerate(((ymv[:, 1:2], c["rs2"][0:T], ALU.mult), (ysc[:, 0:1], c["eps"][0:T], ALU.add),
                                                   (ysc[:, 1:2], c["minus_half"][0:T], ALU.pow), (ysc[:, 2:3], c["rs"][0:T], ALU.mult))):
                    if step:
                        pool.wait_ge(s["ysc_step"], 4 * n + step)
                    pool.tensor_tensor(ysc[:, step:step + 1], a, b, op).then_inc(s["ysc_step"], 1)

            def tail(i, j, part):
                n = 2 * i + j
                if part == 0:
                    pool.wait_ge(s["d_done"], n + 1)
                    if known(n, 0):
                        pool.wait_ge(s["wide_in"], 48)
                    pool.tensor_tensor(y[:], y[:], c["gamma"][0:T], ALU.mult).then_inc(s["x2_step"], 1)
                elif part == 1:
                    pool.wait_ge(s["x2_step"], 3 * n + 1)
                    pool.tensor_tensor(y[:], y[:], c["beta"][0:T], ALU.add).then_inc(s["x2_step"], 1)
                else:
                    pool.wait_ge(s["x2_step"], 3 * n + 2)
                    pool.wait_ge(xr_in[j], 16 * i + 16)
                    pool.tensor_tensor(xr[:, j], xr[:, j], y[:], ALU.add).then_inc(s["x2_step"], 1)

            def step(i, j, last_pair):
                n = 2 * i + j
                sum_tiles(n, 0)
                sum_tiles(n, 1)
                if not known(n, 0):
                    tail_scale(n - 1)
                if j == 0 and not last_pair:
                    layernorm(i + 1)
                sum_tiles(n, 2)
                if not known(n, 0):
                    for part in range(3):
                        tail(i - 1, 1, part) if j == 0 else tail(i, 0, part)
                sum_tiles(n, 3)

            pool.memset(ones[:], 1.0).then_inc(s["setup"], 1)
            pool.wait_ge(s["small_in"], 80)
            pool.tensor_copy(bv_wide[:], c["bv"][:].unsqueeze(2).to_broadcast([P, KC, P])).then_inc(s["wide_done"], 1)
            layernorm(0)
            for n in range(2):
                pool.memset(f32(qbd[n][:]), 0.0).then_inc(s["setup"], 1)
            step(0, 0, False)
            step(0, 1, False)
            with pool.Fori(1, PAIRS - 1) as i:
                step(i, 0, False)
                step(i, 1, False)
            step(PAIRS - 1, 0, True)
            tile_scale(0)
            for u in range(KC):
                sum_tiles(LASTB, u)
            tile_scale(1)
            tail_scale(LASTB - 1)
            tail(PAIRS - 1, 0, 0)
            tail_scale(LASTB)
            tile_scale(2)
            tail(PAIRS - 1, 0, 1)
            tail(PAIRS - 1, 0, 2)

        @block.tensor
        def _(pe):
            def project_k(n, slot, mt, g):
                for part in range(2):
                    if mt == 0:
                        pe.wait_ge(s["c_lo_done"], 2 * n + part + 1)
                    last = key_rows(pe, gen[g][:, 0:SE], w, ctx, mt, range(2 * part, 2 * part + 2))
                last.then_inc(s["k_ready"], 1)

            def project_v(n, kt, bank):
                for kc in range(KC):
                    last = three_pass(pe, bank[0:KP, :], ctx[0][:, kc, kt * KP:(kt + 1) * KP], ctx[1][:, kc, kt * KP:(kt + 1) * KP],
                                      w["v"][0][:, kc], w["v"][1][:, kc], kc == 0, kc == KC - 1)
                last.then_inc(s["v_ready"], 1)

            def transpose_x(i, j):
                pe.wait_ge(s["xn_done"], 2 * i + j + 1)
                for kc in range(KC):
                    last = pe.transpose(gen[j][:, kc * T:(kc + 1) * T], xn[0:T, j, kc * P:(kc + 1) * P], c["ident"][0:T, 0:T])
                last.then_inc(s["xt_ready"], 1)

            def tile_transpose(p):
                for j in range(2):
                    pe.wait_ge(f["xn_done"], 2 * p + j + 1)
                    pe.wait_ge(s["clip_done"], KT * KC * B) if p else pe.wait_ge(s["v_done"], KT * B)
                    for kc in range(KC):
                        last = pe.transpose(tile_bank(p, j)[:, kc * P:(kc + 1) * P], xn[:, j, kc * P:(kc + 1) * P], c["ident"][:])
                    last.then_inc(f["xt_ready"], 1)

            def project_q(i, half, g):
                if half == 0:
                    pe.wait_ge(s["xt_lo_done"], 2 * i + 2)
                for o in range(2):
                    mt = 2 * half + o
                    for kc in range(KC):
                        last = three_pass(pe, gen[g][:, o * PT:(o + 1) * PT], w["q"][0][:, kc, mt * P:(mt + 1) * P],
                                          w["q"][1][:, kc, mt * P:(mt + 1) * P], xt[0][:, kc], xt[1][:, kc], kc == 0, kc == KC - 1)
                last.then_inc(s["q_ready"], 1)

            def scores(n, j, u):
                if u == 0:
                    pe.wait_ge(s["qbd_hi_done"], n + 1)
                    pe.wait_ge(s["qbd_lo_done"], n + 1)
                for kt in range(KT):
                    r = KT * u + kt
                    if not (known(n, 0) and r < 4):
                        pe.wait_ge(s["clip_done"], 12 * n + r - 3)
                    last = three_pass(pe, sc[0:KP, r % 4, 0:QT], k[j][0][:, u, kt * KP:(kt + 1) * KP], k[j][1][:, u, kt * KP:(kt + 1) * KP],
                                      qbd[0][:, u].rearrange("p h t -> p (h t)"), qbd[1][:, u].rearrange("p h t -> p (h t)"), True, True)
                    last.then_inc(s["sc_done"], 1)

            def attend(n, j, u):
                if known(n, 0) and u == 0:
                    pe.wait_ge(s["bias_added"], 1)
                pe.wait_ge(s["exp_done"], 4 * n + u + 1)
                if u == 0:
                    pe.wait_ge(s["v_done"], 3 * n + 3)
                    if not known(n, 0):
                        pe.wait_ge(s["on_done"], n)
                for kt in range(KT):
                    for h in range(HQ):
                        head = u * HQ + h
                        last = pe.matmul(av[DH * h:DH * (h + 1), u * T:(u + 1) * T], v[:, j, kt, head * DH:(head + 1) * DH],
                                         e[:, u % 2, kt, h * T:(h + 1) * T], start=(kt == 0), stop=(kt == KT - 1))
                last.then_inc(s["av_done"], 1)

            def sums(n, u):
                pe.wait_ge(s["esum_step"], 8 * n + 2 * u + 2)
                if not (known(n, 0) and u == 0):
                    pe.wait_ge(s["rz_done"], 4 * n + u)
                for h in range(HQ):
                    last = pe.matmul(z[DH * h:DH * (h + 1), u * T:(u + 1) * T], ones[:], esum[:, u % 2, h * T:(h + 1) * T],
                                     start=True, stop=True)
                last.then_inc(s["z_done"], 1)

            def output(n, g):
                pe.wait_ge(s["ot_lo_done"], n + 1)
                for kc in range(KC):
                    last = three_pass(pe, gen[g][0:T, :], ot[0][:, kc], ot[1][:, kc], w["o"][0][:, kc], w["o"][1][:, kc],
                                      kc == 0, kc == KC - 1)
                last.then_inc(s["y_ready"], 1)

            def step(i, j, more, more_pairs):
                n = 2 * i + j
                extra = j == 1 and more_pairs
                scores(n, j, 0)
                scores(n, j, 1)
                if more:
                    pe.wait_ge(s["v_done"], 3 * n + 2)
                    project_k(n + 1, 1 - j, 0, 1)
                    pe.wait_ge(s["v_done"], 3 * n + 3)
                    project_k(n + 1, 1 - j, 1, 0)
                attend(n, j, 0)
                sums(n, 0)
                if not known(n, 0):
                    pe.wait_ge(s["k_lo_done"], 4 * n + 5) if more else pe.wait_ge(s["v_done"], 3 * n + 2)
                    output(n - 1, 1)
                if extra:
                    pe.wait_ge(s["k_lo_done"], 4 * n + 6)
                    transpose_x(i + 1, 0)
                scores(n, j, 2)
                if extra:
                    pe.wait_ge(s["y_done"], n)
                    transpose_x(i + 1, 1)
                if more:
                    pe.wait_ge(s["xt_lo_done"], 2 * i + 3) if extra else pe.wait_ge(s["k_lo_done"], 4 * n + 6)
                    project_k(n + 1, 1 - j, 2, 0)
                if extra:
                    project_q(i + 1, 0, 1)
                attend(n, j, 1)
                if more:
                    if extra:
                        pe.wait_ge(s["k_lo_done"], 4 * n + 7)
                        project_k(n + 1, 1 - j, 3, 0)
                        pe.wait_ge(s["q_lo_done"], 2 * i + 3)
                        project_q(i + 1, 1, 1)
                    else:
                        pe.wait_ge(s["k_lo_done"], 5) if known(n, 0) else pe.wait_ge(s["y_done"], n)
                        project_k(n + 1, 1 - j, 3, 1)
                scores(n, j, 3)
                sums(n, 1)
                if more:
                    pe.wait_ge(s["k_lo_done"], 4 * n + (8 if extra else 7))
                    project_v(n + 1, 0, gen[0])
                attend(n, j, 2)
                if more:
                    pe.wait_ge(s["q_lo_done"], 2 * i + 4) if extra else pe.wait_ge(s["k_lo_done"], 4 * n + 8)
                    project_v(n + 1, 1, gen[1])
                sums(n, 2)
                attend(n, j, 3)
                if more:
                    pe.wait_ge(s["v_done"], 3 * n + 4)
                    project_v(n + 1, 2, gen[0])
                sums(n, 3)

            def bias():
                pe.wait_ge(s["wide_done"], 1)
                pe.wait_ge(s["xo_in"], 16)
                for kc in range(KC):
                    last = pe.matmul(av[:], bv_wide[:, kc], raw[1][:, kc], start=(kc == 0), stop=(kc == KC - 1))
                last.then_inc(s["bias_ready"], 1)

            for mt in range(READY_KEYS, KC):
                project_k(0, 0, mt, mt % 2)
            project_v(0, 0, sc[:, 0])
            pe.wait_ge(s["k_lo_done"], KC)
            for j in range(2):
                transpose_x(0, j)
            project_v(0, 1, sc[:, 1])
            for half in range(2):
                project_q(0, half, half)
            pe.wait_ge(s["q_lo_done"], 1)
            project_v(0, 2, gen[0])
            bias()
            pe.wait_ge(s["setup"], 3)
            pe.wait_ge(s["xo_lo_done"], 1)
            pe.wait_ge(s["v_done"], 2)
            step(0, 0, True, True)
            step(0, 1, True, True)
            with pe.Fori(1, PAIRS - 1) as i:
                step(i, 0, True, True)
                step(i, 1, True, True)
            step(PAIRS - 1, 0, True, False)
            scores(LASTB, 1, 0)
            scores(LASTB, 1, 1)
            attend(LASTB, 1, 0)
            tile_transpose(0)
            scores(LASTB, 1, 2)
            sums(LASTB, 0)
            attend(LASTB, 1, 1)
            scores(LASTB, 1, 3)
            sums(LASTB, 1)
            attend(LASTB, 1, 2)
            sums(LASTB, 2)
            attend(LASTB, 1, 3)
            sums(LASTB, 3)
            pe.wait_ge(f["xt_lo_done"], 2)
            output(LASTB - 1, 1)
            output(LASTB, 0)
            tile_transpose(1)
            tile_transpose(2)

        @block.scalar
        def _(act):
            def context_hi(n):
                act.wait_ge(s["c_in"], 16 * n + 16)
                if not known(n, 0):
                    act.wait_ge(s["v_ready"], 3 * n)
                for r in (slice(0, 2), slice(2, KC)):
                    act.activation(ctx[0][:, r, 0:S], craw[:, r], ACT.Copy).then_inc(s["c_hi_done"], 1)

            def k_hi(n, slot, mt, g):
                act.wait_ge(s["k_ready"], 4 * n + mt + 1)
                key_hi(act, k[slot], gen[g][:, 0:SE], c["bk"], mt).then_inc(s["k_hi_done"], 1)

            def v_copy(n, slot, kt, bank):
                act.wait_ge(s["v_ready"], 3 * n + kt + 1)
                act.activation(v[:, slot, kt], bank[0:KP, :], ACT.Copy).then_inc(s["v_done"], 1)

            def x_hi(i):
                for j in range(2):
                    act.wait_ge(s["xt_ready"], 2 * i + j + 1)
                    act.activation(xt[0][:, :, j * T:(j + 1) * T], gen[j][:, 0:QT].rearrange("p (c t) -> p c t", c=KC),
                                   ACT.Copy).then_inc(s["xt_hi_done"], 1)

            def q_hi(i, half, g):
                act.wait_ge(s["q_ready"], 2 * i + half + 1)
                for o in range(2):
                    mt = 2 * half + o
                    last = act.activation(q[0][:, mt], gen[g][:, o * PT:(o + 1) * PT], ACT.Identity, bias=c["bq"][:, mt:mt + 1])
                last.then_inc(s["q_hi_done"], 1)

            def place_q(n, j, i):
                act.wait_ge(s["q_hi_done"], 2 * i + 2)
                if not known(n, 0):
                    act.wait_ge(s["sc_done"], 12 * n)
                for h in range(HQ):
                    r = slice(DH * h, DH * (h + 1))
                    last = act.activation(qbd[0][r, :, h], f32(q[0][r, :, j * T:(j + 1) * T]), ACT.Copy)
                last.then_inc(s["qbd_hi_done"], 1)

            def exp(n, u):
                act.wait_ge(s["clip_done"], 12 * n + 3 * u + 3)
                act.activation(e[:, u % 2], e[:, u % 2], ACT.Exp, scale=SCALE).then_inc(s["exp_done"], 1)

            def out_hi(n):
                act.wait_ge(s["on_done"], n + 1)
                if not known(n, 0):
                    act.wait_ge(s["y_ready"], n)
                act.activation(ot[0][:].rearrange("p c t -> p (c t)"), on[:], ACT.Copy).then_inc(s["ot_hi_done"], 1)

            def tile_hi(p):
                for j in range(2):
                    act.wait_ge(f["xt_ready"], 2 * p + j + 1)
                    act.activation(f["tile"](2 * p + j, 0), tile_bank(p, j).rearrange("p (c t) -> p c t", c=KC), ACT.Copy)\
                       .then_inc(f["xt_hi_done"], 1)

            def ffn_weight_hi(n):
                act.wait_ge(f["w_in" + str(n)], 16)
                act.activation(f["wg0"][n][0], f["raw"][n], ACT.Copy).then_inc(f["w_hi_done"], 1)

            def step(i, j, more, more_pairs, more_context):
                n = 2 * i + j
                extra = j == 1 and more_pairs
                exp(n, 0)
                if not known(n, 0):
                    out_hi(n - 1)
                if more:
                    k_hi(n + 1, 1 - j, 0, 1)
                exp(n, 1)
                if more:
                    k_hi(n + 1, 1 - j, 1, 0)
                if extra:
                    x_hi(i + 1)
                exp(n, 2)
                if more:
                    k_hi(n + 1, 1 - j, 2, 0)
                if extra:
                    q_hi(i + 1, 0, 1)
                if more:
                    k_hi(n + 1, 1 - j, 3, 0 if extra else 1)
                if extra:
                    q_hi(i + 1, 1, 1)
                exp(n, 3)
                if more:
                    place_q(n + 1, 1 - j, i + j)
                    for kt in range(KT):
                        v_copy(n + 1, 1 - j, kt, gen[kt % 2])
                if more_context:
                    context_hi(n + 2)

            for mt in range(READY_KEYS, KC):
                k_hi(0, 0, mt, mt % 2)
            act.wait_ge(s["xo_in"], 16)
            act.activation(w["o"][0][:], raw[1][:], ACT.Copy).then_inc(s["xo_hi_done"], 1)
            v_copy(0, 0, 0, sc[:, 0])
            x_hi(0)
            v_copy(0, 0, 1, sc[:, 1])
            for half in range(2):
                q_hi(0, half, half)
            act.wait_ge(s["setup"], 3)
            place_q(0, 0, 0)
            context_hi(1)
            v_copy(0, 0, 2, gen[0])
            step(0, 0, True, True, True)
            step(0, 1, True, True, True)
            with act.Fori(1, PAIRS - 1) as i:
                step(i, 0, True, True, True)
                step(i, 1, True, True, True)
            step(PAIRS - 1, 0, True, False, False)
            exp(LASTB, 0)
            out_hi(LASTB - 1)
            exp(LASTB, 1)
            exp(LASTB, 2)
            tile_hi(0)
            exp(LASTB, 3)
            ffn_weight_hi(0)
            ffn_weight_hi(1)
            out_hi(LASTB)
            tile_hi(1)
            tile_hi(2)

        @block.vector
        def _(dve):
            def context_lo(n):
                for part, r in enumerate((slice(0, 2), slice(2, KC))):
                    dve.wait_ge(s["c_hi_done"], 2 * n + part + 1)
                    dve.tensor_tensor(ctx[1][:, r, 0:S], craw[:, r], f32(ctx[0][:, r, 0:S]), ALU.subtract).then_inc(s["c_lo_done"], 1)

            def layernorm_stats(i):
                dve.wait_ge(s["xa_in"], 16 * i + 16)
                for j in range(2):
                    dve.bn_stats(st[:, j], xa[0:T, j]).then_inc(s["stats_done"], 1)
                if not known(i, 0):
                    dve.wait_ge(s["xn_done"], 2 * i)
                dve.wait_ge(s["stats_done"], 2 * i + 2)
                carry_waits(dve, fence[:])
                for j in range(2):
                    dve.bn_aggr(mv[:, j], st[:, j]).then_inc(s["aggr_done"], 1)

            def layernorm_apply(i):
                for j in range(2):
                    dve.wait_ge(s["rstd_done"], 2 * i + j + 1)
                    if not known(i, 0):
                        dve.wait_ge(s["xt_ready"], 2 * i + j - 1)
                    dve.tensor_scalar(xn[0:T, j], xa[0:T, j], mv[:, j, 0:1], rstd[:, j], ALU.subtract, ALU.mult)\
                       .then_inc(s["xn_done"], 1)

            def x_lo(i):
                for j in range(2):
                    dve.wait_ge(s["xt_hi_done"], 2 * i + j + 1)
                    dve.tensor_tensor(xt[1][:, :, j * T:(j + 1) * T], gen[j][:, 0:QT].rearrange("p (c t) -> p c t", c=KC),
                                      f32(xt[0][:, :, j * T:(j + 1) * T]), ALU.subtract).then_inc(s["xt_lo_done"], 1)

            def k_lo(n, slot, mt, g):
                dve.wait_ge(s["k_hi_done"], 4 * n + mt + 1)
                key_lo(dve, k[slot], gen[g][:, 0:SE], c["bk"], mt).then_inc(s["k_lo_done"], 1)

            def q_lo(i, half, g):
                dve.wait_ge(s["q_hi_done"], 2 * i + half + 1)
                for o in range(2):
                    mt = 2 * half + o
                    last = dve.scalar_tensor_tensor(out=q[1][:, mt], in0=gen[g][:, o * PT:(o + 1) * PT], scalar=c["bq"][:, mt:mt + 1],
                                                    in1=f32(q[0][:, mt]), op0=ALU.add, op1=ALU.subtract)
                last.then_inc(s["q_lo_done"], 1)

            def place_q(n, j, i):
                dve.wait_ge(s["q_lo_done"], 2 * i + 2)
                if not known(n, 0):
                    dve.wait_ge(s["sc_done"], 12 * n)
                for h in range(HQ):
                    r = slice(DH * h, DH * (h + 1))
                    last = dve.tensor_copy(qbd[1][r, :, h], q[1][r, :, j * T:(j + 1) * T])
                last.then_inc(s["qbd_lo_done"], 1)

            def clip(n, u):
                if not (known(n, 0) and u < 2):
                    dve.wait_ge(s["av_done"], 4 * n + u - 1)
                    dve.wait_ge(s["esum_step"], 8 * n + 2 * u - 2)
                for kt in range(KT):
                    r = KT * u + kt
                    dve.wait_ge(s["sc_done"], 12 * n + r + 1)
                    dve.tensor_scalar(e[:, u % 2, kt], sc[0:KP, r % 4, 0:QT], c["bound"][:, bass.ds(n * KT + kt, 1)],
                                      -CLIP / SCALE, ALU.min, ALU.max).then_inc(s["clip_done"], 1)

            def tail_stats(n, g=1, y=y[:]):
                dve.wait_ge(s["y_ready"], n + 1)
                if not known(n, 0, LASTB):
                    dve.wait_ge(s["x2_step"], 3 * n)
                dve.tensor_tensor(y, gen[g][0:T, :], c["bo_full"][0:T], ALU.add).then_inc(s["y_done"], 1)
                dve.wait_ge(s["y_done"], n + 1)
                dve.bn_stats(yst[:], y).then_inc(s["yst_done"], 1)
                dve.wait_ge(s["yst_done"], n + 1)
                carry_waits(dve, fence[:])
                dve.bn_aggr(ymv[:], yst[:]).then_inc(s["ymv_done"], 1)

            def tail_apply(n, y=y[:]):
                dve.wait_ge(s["ysc_step"], 4 * n + 4)
                dve.tensor_scalar(y, y, ymv[:, 0:1], ysc[:, 3:4], ALU.subtract, ALU.mult).then_inc(s["d_done"], 1)

            def invert_sums(n, u):
                dve.wait_ge(s["z_done"], 4 * n + u + 1)
                if u == 0 and not known(n, 0):
                    dve.wait_ge(s["on_done"], n)
                cols = slice(u * T, (u + 1) * T)
                dve.reciprocal(rz[:, cols], z[:, cols]).then_inc(s["rz_done"], 1)

            def normalise(n):
                dve.wait_ge(s["rz_done"], 4 * n + 4)
                dve.wait_ge(s["av_done"], 4 * n + 4)
                if not known(n, 0):
                    dve.wait_ge(s["ot_lo_done"], n)
                dve.tensor_tensor(on[:], av[:, 0:QT], rz[:], ALU.mult).then_inc(s["on_done"], 1)

            def out_lo(n):
                dve.wait_ge(s["ot_hi_done"], n + 1)
                dve.tensor_tensor(ot[1][:].rearrange("p c t -> p (c t)"), on[:], f32(ot[0][:].rearrange("p c t -> p (c t)")),
                                  ALU.subtract).then_inc(s["ot_lo_done"], 1)

            def tile_stats(p):
                for j in range(2):
                    dve.wait_ge(f["x_in" + str(j)], 16 * p + 16)
                    dve.bn_stats(tst[:, j], xa[:, j]).then_inc(f["stats_done"], 1)
                if p:
                    dve.wait_ge(f["xn_done"], 2 * p)
                dve.wait_ge(f["stats_done"], 2 * p + 2)
                carry_waits(dve, fence[:])
                for j in range(2):
                    dve.bn_aggr(tmv[:, j], tst[:, j]).then_inc(f["aggr_done"], 1)

            def tile_apply(p):
                for j in range(2):
                    dve.wait_ge(f["rstd_done"], 2 * p + j + 1)
                    dve.wait_ge(f["xt_ready"], 2 * p + j - 1) if p else dve.wait_ge(s["xt_ready"], 2 * PAIRS)
                    dve.tensor_scalar(xn[:, j], xa[:, j], tmv[:, j, 0:1], trstd[:, j], ALU.subtract, ALU.mult)\
                       .then_inc(f["xn_done"], 1)

            def tile_lo(p):
                for j in range(2):
                    dve.wait_ge(f["xt_hi_done"], 2 * p + j + 1)
                    dve.tensor_tensor(f["tile"](2 * p + j, 1), tile_bank(p, j).rearrange("p (c t) -> p c t", c=KC),
                                      f32(f["tile"](2 * p + j, 0)), ALU.subtract).then_inc(f["xt_lo_done"], 1)

            def ffn_weight_lo(n):
                dve.wait_ge(f["w_hi_done"], n + 1)
                dve.tensor_tensor(f["wg0"][n][1], f["raw"][n], f32(f["wg0"][n][0]), ALU.subtract).then_inc(f["w_lo_done"], 1)

            def finish(part):
                if part == 0:
                    dve.wait_ge(s["d_done"], B)
                    dve.tensor_tensor(y_last, y_last, c["gamma"][0:T], ALU.mult).then_inc(s["last_step"], 1)
                elif part == 1:
                    dve.wait_ge(s["last_step"], 1)
                    dve.tensor_tensor(y_last, y_last, c["beta"][0:T], ALU.add).then_inc(s["last_step"], 1)
                else:
                    dve.wait_ge(s["last_step"], 2)
                    dve.wait_ge(xr_in[1], 16 * PAIRS)
                    dve.tensor_tensor(xr[:, 1], xr[:, 1], y_last, ALU.add).then_inc(s["last_step"], 1)

            def step(i, j, more, more_pairs, more_context):
                n = 2 * i + j
                extra = j == 1 and more_pairs
                if not known(n, 0):
                    invert_sums(n - 1, 3)
                clip(n, 0)
                if more and not known(n, 0):
                    context_lo(n + 1)
                if not known(n, 0):
                    normalise(n - 1)
                clip(n, 1)
                if not known(n, 0):
                    out_lo(n - 1)
                if more:
                    k_lo(n + 1, 1 - j, 0, 1)
                    k_lo(n + 1, 1 - j, 1, 0)
                if not known(n, 0):
                    tail_stats(n - 1)
                if extra:
                    x_lo(i + 1)
                if j == 0 and more_pairs:
                    layernorm_stats(i + 1)
                clip(n, 2)
                if more:
                    k_lo(n + 1, 1 - j, 2, 0)
                invert_sums(n, 0)
                if extra:
                    q_lo(i + 1, 0, 1)
                if not known(n, 0):
                    tail_apply(n - 1)
                if more:
                    k_lo(n + 1, 1 - j, 3, 0 if extra else 1)
                if extra:
                    q_lo(i + 1, 1, 1)
                if j == 0 and more_pairs:
                    layernorm_apply(i + 1)
                clip(n, 3)
                invert_sums(n, 1)
                if more:
                    place_q(n + 1, 1 - j, i + j)
                invert_sums(n, 2)

            layernorm_stats(0)
            dve.wait_ge(s["small_in"], 80)
            for mt in range(READY_KEYS, KC):
                k_lo(0, 0, mt, mt % 2)
            for j in range(2):
                dve.wait_ge(c["x1_out"][j], 16 * PAIRS)
            layernorm_apply(0)
            dve.tensor_copy(maskf[:], c["mask"][:]).then_inc(s["mask_step"], 1)
            dve.wait_ge(s["mask_step"], 1)
            dve.tensor_scalar(c["bound"][:], maskf[:], 0.5, 2 * CLIP / SCALE, ALU.is_gt, ALU.mult).then_inc(s["mask_step"], 1)
            dve.wait_ge(s["mask_step"], 2)
            dve.tensor_scalar(c["bound"][:], c["bound"][:], -CLIP / SCALE, None, ALU.add).then_inc(s["mask_step"], 1)
            dve.tensor_scalar(c["rs"][:], c["rs"][:], 0.0, 0.3, ALU.max, ALU.min).then_inc(s["rs_step"], 1)
            dve.wait_ge(s["rs_step"], 1)
            dve.tensor_tensor(c["rs2"][:], c["rs"][:], c["rs"][:], ALU.mult).then_inc(s["rs_step"], 1)
            x_lo(0)
            dve.wait_ge(s["xo_hi_done"], 1)
            dve.tensor_tensor(w["o"][1][:], raw[1][:], f32(w["o"][0][:]), ALU.subtract).then_inc(s["xo_lo_done"], 1)
            for half in range(2):
                q_lo(0, half, half)
            dve.wait_ge(s["setup"], 3)
            dve.wait_ge(s["mask_step"], 3)
            place_q(0, 0, 0)
            context_lo(1)
            dve.wait_ge(s["wide_in"], 48)
            dve.wait_ge(s["bias_ready"], 1)
            dve.tensor_tensor(c["bo_full"][:], av[:], bo[:], ALU.add).then_inc(s["bias_added"], 1)
            step(0, 0, True, True, True)
            step(0, 1, True, True, True)
            with dve.Fori(1, PAIRS - 1) as i:
                step(i, 0, True, True, True)
                step(i, 1, True, True, True)
            step(PAIRS - 1, 0, True, False, False)
            tile_stats(0)
            invert_sums(LASTB - 1, 3)
            clip(LASTB, 0)
            normalise(LASTB - 1)
            clip(LASTB, 1)
            tile_apply(0)
            out_lo(LASTB - 1)
            clip(LASTB, 2)
            invert_sums(LASTB, 0)
            clip(LASTB, 3)
            tile_lo(0)
            invert_sums(LASTB, 1)
            invert_sums(LASTB, 2)
            invert_sums(LASTB, 3)
            normalise(LASTB)
            tile_stats(1)
            ffn_weight_lo(0)
            ffn_weight_lo(1)
            out_lo(LASTB)
            tile_apply(1)
            tail_stats(LASTB - 1)
            tile_lo(1)
            tail_apply(LASTB - 1)
            tail_stats(LASTB, 0, y_last)
            tile_stats(2)
            tail_apply(LASTB, y_last)
            finish(0)
            finish(1)
            tile_apply(2)
            finish(2)
            tile_lo(2)


def build_ffn(nc, dram, consts, f, sems):
    with ExitStack() as scope:
        m = Memory(nc, scope)
        x = m.sb("x3", [P, FT * D])
        xt, tile_xt = f["xt"], f["tile"]
        fence = m.sb("fence_f3", [1, 1])
        st = m.sb("st3", [P, 2, 6])
        mv = m.sb("mv3", [P, 2, 2])
        veps = m.sb("veps3", [P, 2, 1])
        rstd = m.sb("rstd3", [P, 2, 1])
        xn = m.sb("xn3", [P, 2, D])
        raw, raw2 = f["raw"], f["raw2"]
        wg = [f["wg0"], [[m.sb(f"w{n}_{part}1", [P, KC, HC], F32R)[:] for part in ("hi", "lo")] for n in (1, 3)]]
        fly = [m.sb(f"fly_{n}", [P, HT, D], F32R) for n in ("hi", "lo")]
        w2 = [[m.sb(f"w2_{part}{slot}", [P, HT, D], F32R) for part in ("hi", "lo")] for slot in range(2)]
        had = m.sb("had", [P, P], F32R)
        had_raw = m.sb("had_raw", [P, P])
        gate, hf = f["spare"]
        hid = [m.sb(f"hid_{n}", [P, 2, HT, 512], F32R) for n in ("hi", "lo")]
        psg = m.ps("psg", [P, 2, 512])
        psu = m.ps("psu", [P, 2, 512])
        psy = m.ps("psy", [P, 2, 512])
        psh = m.ps("psh", [P, 2, 512])
        s = f
        x_in, w_in = (s["x_in0"], s["x_in1"]), (s["w_in0"], s["w_in1"], s["w_in2"])
        UNITS = HT * len(FGROUPS)
        HSCALE = float(F) ** -0.5
        fly_dram = f["fly_dram"]

        def known(i, *values):
            return isinstance(i, int) and i in values

        block = scope.enter_context(nc.Block())

        def xtile(t):
            return x[:, bass.ds(t * D, D)]

        def first_split(c):
            return 4 if known(c, 0) else 0

        @block.sync
        def _(sp):
            def tile(i, j):
                at, row = bass.ds(held(sp, (2 * i + j) * D), D), bass.ds(held(sp, (2 * i + j) * P), P)
                sp.wait_ge(x_in[j], 16 * i)
                sp.dma_start(x[:, at], dram["x2"][row, :]).then_inc(x_in[j], 16)

            def weights(c):
                at = bass.ds(held(sp, c * KC * HC), KC * HC)
                rows = [bass.ds(held(sp, c * HT + t), 1) for t in range(HT)]
                sp.wait_ge(s["w_lo_done"], 3 * c)
                for n, name in enumerate(("w1", "w3")):
                    sp.dma_start(raw[n], dram[name][:, at].rearrange("p (k n) -> p k n", k=KC)).then_inc(w_in[n], 16)
                for t in range(HT):
                    sp.dma_start(raw2[:, t].rearrange("p (c n) -> p c n", n=BCOL),
                                 fly_dram[:, rows[t]].rearrange("p t c n -> p (t c) n")).then_inc(w_in[2], 16)

            for j in range(2):
                sp.wait_ge(s["x2_out" + str(j)], 16 * (PAIRS - 1))
            for j in range(2):
                tile(LEAD, j)
            sp.dma_start(had_raw[:], dram["had"]).then_inc(s["had_in"], 16)
            for i in range(LEAD + 1, TP):
                if (2 * i + 2) * P > (B - 2) * T and 2 * i * P <= (B - 2) * T:
                    for j in range(2):
                        sp.wait_ge(s["x2_out" + str(j)], 16 * PAIRS)
                for j in range(2):
                    tile(i, j)
            for t in range(2 * LEAD):
                sp.dma_start(x[:, t * D:(t + 1) * D], dram["x2"][t * P:(t + 1) * P, :]).then_inc(s["rest_in"], 16)
            with sp.Fori(1, CHUNKS) as c:
                weights(c)
            for t in range(FT):
                sp.wait_ge(s["y_done"], (CHUNKS - 1) * FT + t + 1)
                sp.dma_start(dram["out"][t * P:(t + 1) * P, :], x[:, t * D:(t + 1) * D]).then_inc(s["out_done"], 16)
            sp.wait_ge(s["out_done"], 16 * FT)

        @block.gpsimd
        def _(pool):
            def layernorm(i):
                for j in range(2):
                    pool.wait_ge(s["aggr_done"], 2 * i + j + 1)
                    pool.tensor_tensor(veps[:, j], mv[:, j, 1:2], consts["eps"][:], ALU.add).then_inc(s["veps_done"], 1)
                    pool.wait_ge(s["veps_done"], 2 * i + j + 1)
                    pool.tensor_tensor(rstd[:, j], veps[:, j], consts["minus_half"][:], ALU.pow).then_inc(s["rstd_done"], 1)

            def hidden_lo(c, n):
                width = FGROUPS[n // HT][1]
                pool.wait_ge(s["hid_hi_done"], UNITS * c + n + 1)
                pool.tensor_tensor(hid[1][:, (n // HT) % 2, n % HT, 0:width], hf[:, n % 2, 0:width],
                                   f32(hid[0][:, (n // HT) % 2, n % HT, 0:width]), ALU.subtract).then_inc(s["hid_lo_done"], 1)

            layernorm(LEAD)
            for n in range(UNITS):
                if n + LEAD + 1 < TP:
                    layernorm(n + LEAD + 1)
                hidden_lo(0, n)
            with pool.Fori(1, CHUNKS) as c:
                for n in range(UNITS):
                    hidden_lo(c, n)

        @block.tensor
        def _(pe):
            def transpose_x(i):
                for j in range(2):
                    pe.wait_ge(s["xn_done"], 2 * i + j + 1)
                    pe.wait_ge(s["xt_lo_done"], 2 * i + j - 1)
                    if i == TP - 1:
                        pe.wait_ge(s["y_done"], 3 + j)
                    for kc in range(KC):
                        last = pe.transpose(psy[:, j, kc * P:(kc + 1) * P], xn[:, j, kc * P:(kc + 1) * P], consts["ident"][:])
                    last.then_inc(s["xt_ready"], 1)

            def hadamard(c):
                pe.wait_ge(s["w_lo_done"], 3 * c + 3)
                if not known(c, 0):
                    pe.wait_ge(s["w2_lo_done"], HT * c)
                for t in range(HT):
                    pe.matmul(psh[:, t], had[:], fly[0][:, t], start=True, stop=False)
                    pe.matmul(psh[:, t], had[:], fly[1][:, t], start=False, stop=True).then_inc(s["fly_ready"], 1)

            def up(c, slot, g):
                at, width = FGROUPS[g]
                for t in range(HT):
                    n = HT * g + t
                    if n == 0:
                        pe.wait_ge(s["w_lo_done"], 3 * c + 2)
                    if t == 0 and known(c, 0):
                        pe.wait_ge(s["xt_lo_done"], (at + width) // P)
                    for which, (ps, done) in enumerate(((psg, "gate_ready"), (psu, "up_ready"))):
                        if not (known(c, 0) and n < 2):
                            pe.wait_ge(s["silu_done" if which == 0 else "h_done"], UNITS * c + n - 1)
                        for kc in range(KC):
                            wh, wl = wg[slot][which]
                            last = three_pass(pe, ps[:, t, 0:width], wh[:, kc, t * P:(t + 1) * P], wl[:, kc, t * P:(t + 1) * P],
                                              xt[g][0][:, kc, 0:width], xt[g][1][:, kc, 0:width], kc == 0, kc == KC - 1)
                        last.then_inc(s[done], 1)
                        if which == 0 and known(c, 0) and LEAD <= n + LEAD - 1 < TP:
                            transpose_x(n + LEAD - 1)

            def down(c, slot, g):
                at, width = FGROUPS[g]
                pe.wait_ge(s["hid_lo_done"], UNITS * c + HT * g + HT)
                if g == 0:
                    pe.wait_ge(s["w2_lo_done"], HT * c + HT)
                for k in range(width // P):
                    tile = at // P + k
                    if not (known(c, 0) and tile < 2):
                        pe.wait_ge(s["y_done"], FT * c + tile - 1)
                    if known(c, 0) and tile < 6:
                        pe.wait_ge(s["xt_lo_done"], 2 * (TP - 2 + tile // 4) + tile % 2 + 1)
                    for t in range(HT):
                        last = three_pass(pe, psy[:, tile % 2], hid[0][:, g % 2, t, k * P:(k + 1) * P], hid[1][:, g % 2, t, k * P:(k + 1) * P],
                                          w2[slot][0][:, t], w2[slot][1][:, t], t == 0, t == HT - 1)
                    last.then_inc(s["y_ready"], 1)

            def chunk(c, slot, more):
                up(c, slot, 0)
                if known(c, 0):
                    hadamard(0)
                else:
                    down(c - 1, 1 - slot, 3)
                up(c, slot, 1)
                down(c, slot, 0)
                up(c, slot, 2)
                down(c, slot, 1)
                up(c, slot, 3)
                if more:
                    hadamard(c + 1)
                down(c, slot, 2)

            chunk(0, 0, True)
            chunk(1, 1, True)
            with pe.Fori(1, CHUNKS // 2 - 1) as i:
                chunk(2 * i, 0, True)
                chunk(2 * i + 1, 1, True)
            chunk(CHUNKS - 2, 0, True)
            chunk(CHUNKS - 1, 1, False)
            down(CHUNKS - 1, 1, 3)

        @block.scalar
        def _(act):
            def x_hi(i):
                for j in range(2):
                    act.wait_ge(s["xt_ready"], 2 * i + j + 1)
                    act.activation(tile_xt(2 * i + j, 0), psy[:, j].rearrange("p (c t) -> p c t", c=KC),
                                   ACT.Copy).then_inc(s["xt_hi_done"], 1)

            def split_hi(c, slot, parts):
                for n in parts:
                    dst, src = ((wg[slot][0][0], raw[0]), (wg[slot][1][0], raw[1]), (fly[0], raw2))[n]
                    act.wait_ge(w_in[n], 16 * c + 16 if n < 2 else 32 * c + 32)
                    if n == 2 and not known(c, 0):
                        act.wait_ge(s["fly_ready"], HT * c)
                    act.activation(dst[:], src[:], ACT.Copy).then_inc(s["w_hi_done"], 1)

            def w2_hi(c, slot):
                for t in range(HT):
                    act.wait_ge(s["fly_ready"], HT * c + t + 1)
                    act.activation(w2[slot][0][:, t], psh[:, t], ACT.Copy, scale=HSCALE).then_inc(s["w2_hi_done"], 1)

            def unit(c, n):
                g, t, width = n // HT, n % HT, FGROUPS[n // HT][1]
                act.wait_ge(s["gate_ready"], UNITS * c + n + 1)
                if not (known(c, 0) and n < 2):
                    act.wait_ge(s["h_done"], UNITS * c + n - 1)
                act.activation(gate[:, t, 0:width], psg[:, t, 0:width], ACT.Silu).then_inc(s["silu_done"], 1)
                act.wait_ge(s["h_done"], UNITS * c + n + 1)
                act.activation(hid[0][:, g % 2, t, 0:width], hf[:, t, 0:width], ACT.Copy).then_inc(s["hid_hi_done"], 1)

            def chunk(c, slot, more):
                for n in range(UNITS):
                    if n % HT == 0 and not (known(c, 0) and n < 2 * HT):
                        act.wait_ge(s["y_ready"], FT * c + (-2, 0, 4, 8)[n // HT])
                    if known(c, 0) and LEAD <= n + LEAD - 1 < TP:
                        x_hi(n + LEAD - 1)
                    unit(c, n)
                    if n == 1 and known(c, 0):
                        w2_hi(0, 0)
                    if more and 0 <= n - first_split(c) < 3:
                        split_hi(c + 1, 1 - slot, (n - first_split(c),))
                if more:
                    w2_hi(c + 1, 1 - slot)

            split_hi(0, 0, (2,))
            chunk(0, 0, True)
            chunk(1, 1, True)
            with act.Fori(1, CHUNKS // 2 - 1) as i:
                chunk(2 * i, 0, True)
                chunk(2 * i + 1, 1, True)
            chunk(CHUNKS - 2, 0, True)
            chunk(CHUNKS - 1, 1, False)

        @block.vector
        def _(dve):
            def stats(i):
                for j in range(2):
                    dve.wait_ge(x_in[j], 16 * i + 16)
                    dve.bn_stats(st[:, j], xtile(2 * i + j)).then_inc(s["stats_done"], 1)
                if not known(i, 0):
                    dve.wait_ge(s["xn_done"], 2 * i)
                dve.wait_ge(s["stats_done"], 2 * i + 2)
                carry_waits(dve, fence[:])
                for j in range(2):
                    dve.bn_aggr(mv[:, j], st[:, j]).then_inc(s["aggr_done"], 1)

            def apply(i):
                for j in range(2):
                    dve.wait_ge(s["rstd_done"], 2 * i + j + 1)
                    if not known(i, 0):
                        dve.wait_ge(s["xt_ready"], 2 * i + j - 1)
                    dve.tensor_scalar(xn[:, j], xtile(2 * i + j), mv[:, j, 0:1], rstd[:, j], ALU.subtract, ALU.mult)\
                       .then_inc(s["xn_done"], 1)

            def x_lo(i):
                for j in range(2):
                    dve.wait_ge(s["xt_hi_done"], 2 * i + j + 1)
                    dve.tensor_tensor(tile_xt(2 * i + j, 1), psy[:, j].rearrange("p (c t) -> p c t", c=KC), f32(tile_xt(2 * i + j, 0)),
                                      ALU.subtract).then_inc(s["xt_lo_done"], 1)

            def split_lo(c, slot, parts):
                for n in parts:
                    dst, src = ((wg[slot][0], raw[0]), (wg[slot][1], raw[1]), (fly, raw2))[n]
                    dve.wait_ge(s["w_hi_done"], 3 * c + n + 1)
                    dve.tensor_tensor(dst[1][:], src[:], f32(dst[0][:]), ALU.subtract).then_inc(s["w_lo_done"], 1)

            def w2_lo(c, slot):
                for t in range(HT):
                    dve.wait_ge(s["w2_hi_done"], HT * c + t + 1)
                    dve.scalar_tensor_tensor(out=w2[slot][1][:, t], in0=psh[:, t], scalar=HSCALE, in1=f32(w2[slot][0][:, t]),
                                             op0=ALU.mult, op1=ALU.subtract).then_inc(s["w2_lo_done"], 1)

            def unit(c, n):
                t, width = n % HT, FGROUPS[n // HT][1]
                dve.wait_ge(s["silu_done"], UNITS * c + n + 1)
                dve.wait_ge(s["up_ready"], UNITS * c + n + 1)
                if not (known(c, 0) and n < 2):
                    dve.wait_ge(s["hid_lo_done"], UNITS * c + n - 1)
                dve.tensor_tensor(hf[:, t, 0:width], gate[:, t, 0:width], psu[:, t, 0:width], ALU.mult).then_inc(s["h_done"], 1)

            def add(c, tiles):
                for tile in tiles:
                    dve.wait_ge(s["y_ready"], FT * c + tile + 1)
                    if known(c, 0) and tile == 0:
                        dve.wait_ge(s["rest_in"], 16 * 2 * LEAD)
                    part = x[:, tile * D:(tile + 1) * D]
                    dve.tensor_tensor(part, psy[:, tile % 2], part, ALU.add).then_inc(s["y_done"], 1)

            def chunk(c, slot, more):
                for n in range(4):
                    if known(c, 0) and n:
                        x_lo(n + LEAD - 1)
                        if n + LEAD < TP:
                            apply(n + LEAD)
                    unit(c, n)
                    if known(c, 0) and n + LEAD + 1 < TP:
                        stats(n + LEAD + 1)
                    if n == 1:
                        w2_lo(0, 0) if known(c, 0) else add(c - 1, (12, 13))
                    if more and n < 3 and not known(c, 0):
                        split_lo(c + 1, 1 - slot, (n,))
                add(c, range(0, 4))
                if known(c, 0):
                    x_lo(TP - 1)
                for n in range(4, UNITS):
                    unit(c, n)
                    if n == 5:
                        add(c, range(4, 8))
                    if more and known(c, 0) and n < 7:
                        split_lo(1, 1 - slot, (n - 4,))
                add(c, range(8, 12))
                if more:
                    w2_lo(c + 1, 1 - slot)

            stats(LEAD)
            apply(LEAD)
            dve.wait_ge(s["had_in"], 16)
            dve.tensor_copy(had[:], had_raw[:]).then_inc(s["had_done"], 1)
            split_lo(0, 0, (2,))
            chunk(0, 0, True)
            chunk(1, 1, True)
            with dve.Fori(1, CHUNKS // 2 - 1) as i:
                chunk(2 * i, 0, True)
                chunk(2 * i + 1, 1, True)
            chunk(CHUNKS - 2, 0, True)
            chunk(CHUNKS - 1, 1, False)
            add(CHUNKS - 1, (12, 13))


def ffn_parts(dram, w, raw, c, sems):
    f = {n: sems.sem("f_" + n) for n in
         ("x_in0 x_in1 rest_in stats_done aggr_done veps_done rstd_done xn_done xt_ready xt_hi_done xt_lo_done had_in had_done "
          "w_in0 w_in1 w_in2 w_hi_done w_lo_done fly_ready w2_hi_done w2_lo_done gate_ready up_ready silu_done h_done "
          "hid_hi_done hid_lo_done y_ready y_done out_done").split()}
    f.update({n: c[n] for n in ("x2_out0", "x2_out1")})
    f["xt"] = xt = [w[n] for n in "kvqo"]
    f["tile"] = lambda t, part: xt[t // TILES_G][part][:, :, (t % TILES_G) * P:(t % TILES_G + 1) * P]
    f["raw"] = [raw[1][:, :, n * HC:(n + 1) * HC] for n in range(2)]
    f["raw2"] = raw[0][:, 0:HT]
    f["wg0"] = [[part[:, :, 0:HC] for part in pair] for pair in (c["k_slot0"], c["ctx"])]
    f["spare"] = c["spare"]
    f["fly_dram"] = dram["w2_fly"].rearrange("p (c t) n -> p t c n", t=B)
    return f


def build(nc, dram):
    with ExitStack() as root:
        sems = Memory(nc, root)
        consts = {"ident": sems.sb("ident", [P, P]), "eps": sems.sb("eps", [P, 1]), "minus_half": sems.sb("minus_half", [P, 1])}
        with ExitStack() as scope:
            m = Memory(nc, scope)
            w = {n: [m.sb(f"w{n}_{part}", [P, KC, D], F32R) for part in ("hi", "lo")] for n in "qkvo"}
            raw = [m.sb(f"raw{n}", [P, KC, D]) for n in range(2)]
            c = dict(consts, x1_out=[sems.sem(f"x1_out{j}") for j in range(2)], **{n: sems.sem(n) for n in SHARED})
            for name, shape, dt in (("bq", [P, KC], F32), ("bk", [P, KC], F32), ("bv", [P, KC], F32), ("rs", [P, 1], F32),
                                    ("mask", [KP, B * KT], I32)):
                c[name] = m.sb(name, shape, dt)
            with ExitStack() as under:
                c["stream"] = Memory(nc, under).sb("stream", [T, B * D])
            c["ctx"] = [m.sb(f"ctx_{n}", [P, KC, SE], F32R) for n in ("hi", "lo")]
            c["k_slot0"] = [m.sb(f"k2_{n}0", [P, KC, SE], F32R) for n in ("hi", "lo")]
            c["spare"] = [m.sb(f"spare{n}", [P, 2, D]) for n in range(2)]
            m.sb("stream_end", [P, B * D - 4 * KC * SE - 4 * D])
            f = ffn_parts(dram, w, raw, c, sems)
            build_self(nc, dram, w, raw, consts, c, sems)
            build_cross(nc, dram, w, raw, c, f, sems)
            build_ffn(nc, dram, consts, f, sems)


def layouts(i):
    import numpy as np

    def stationary(w):
        return w.T.reshape(KC, P, D).transpose(1, 0, 2)

    def natural(w):
        return w.reshape(KC, P, D).transpose(1, 0, 2)

    def column(v):
        return v.reshape(KC, P).T

    def hidden(w):
        return w.T.reshape(KC, P, CHUNKS, HC).transpose(1, 2, 0, 3).reshape(P, CHUNKS * KC * HC)

    h = np.ones((1, 1), np.float32)
    while h.shape[0] < P:
        h = np.block([[h, h], [h, -h]])
    return {
        "x": i["x"].transpose(1, 0, 2).reshape(T, B * D),
        "ctx": i["ctx_2048"].transpose(2, 0, 1).reshape(KC, P, B, S).transpose(1, 2, 0, 3).reshape(P, B * KC * S),
        "mask": i["mask_BxS2_ik0"].reshape(B, KT, KP).transpose(2, 0, 1).reshape(KP, B * KT),
        "wq": natural(i["L0_attn_Wq"]), "wk": stationary(i["L0_attn_Wk"]), "wv": natural(i["L0_attn_Wv"]),
        "wo": stationary(i["L0_attn_Wo"]), "wdown_t": i["L0_attn_Wdown"].T, "wup": i["L0_attn_Wup"],
        "xq": stationary(i["L0_xattn_Wq"]), "xk": stationary(i["L0_xattn_Wk"]), "xv": stationary(i["L0_xattn_Wv"]),
        "xo": stationary(i["L0_xattn_Wo"]), "bq": column(i["L0_xattn_bq"]), "bk": column(i["L0_xattn_bk"]),
        "bv": column(i["L0_xattn_bv"]), "bo": i["L0_xattn_bo"].reshape(1, D), "gamma": i["L0_xattn_ln_gamma"].reshape(1, D),
        "beta": i["L0_xattn_ln_beta"].reshape(1, D), "rs": i["L0_xattn_residual_scale"].reshape(1, 1),
        "w1": hidden(i["L0_ffn_W1"]), "w3": hidden(i["L0_ffn_W3"]),
        "w2": i["L0_ffn_W2"].T.reshape(B, P, PAIRS, BCOL).transpose(1, 2, 0, 3).reshape(P, PAIRS * B, BCOL),
        "ident": np.eye(P, dtype=np.float32), "had": h,
    }


def kernel(**inputs):
    import numpy as np
    import concourse.bacc as bacc
    from concourse.bass_utils import run_bass_kernel_spmd

    nc = bacc.Bacc("TRN2", target_bir_lowering=False, num_devices=1)
    arrays = {"in_" + n: np.ascontiguousarray(a) for n, a in layouts({n: np.asarray(a) for n, a in inputs.items()}).items()}
    dram = {n[3:]: nc.dram_tensor(n, a.shape, mybir.dt.from_np(a.dtype), kind="ExternalInput").ap() for n, a in arrays.items()}
    dram["out"] = nc.dram_tensor("out", (TOK, D), F32, kind="ExternalOutput").ap()
    dram["x1"] = nc.dram_tensor("x1", (T, B * D), F32, kind="Internal").ap()
    dram["x2"] = nc.dram_tensor("x2", (TOK, D), F32, kind="Internal").ap()
    dram["w2_fly"] = nc.dram_tensor("w2_fly", (P, PAIRS * B, BCOL), F32, kind="Internal").ap()
    build(nc, dram)
    r = run_bass_kernel_spmd(nc, [arrays], core_ids=[0])
    return r.results[0]["out"].reshape(B, T, D)
```
